# Optimizing a Trainium2 kernel written in Bass

```python
import numpy as np
import jax
import jax.numpy as jnp

def _softmax(x, axis=-1):
    return jax.nn.softmax(x, axis=axis)

def _gelu(x):
    return jax.nn.gelu(x, approximate=True)

def _silu(x):
    return jax.nn.silu(x)

def _sigmoid(x):
    return jax.nn.sigmoid(x)

def _layernorm(x, axis=-1, eps=1e-05):
    m = jnp.mean(x, axis=axis, keepdims=True)
    v = jnp.var(x, axis=axis, keepdims=True)
    return (x - m) / jnp.sqrt(v + eps)

def _scatter_add(tgt, idx, src, axis=0):
    return tgt.at[idx].add(src)

def _segment_sum(src, seg, n):
    return jax.ops.segment_sum(src, seg, n)
kernel_name = 'mk_flamingo_gated_d4_seqx_r8_20a6da'

def setup_inputs(seed: int=0):
    np.random.seed(seed)
    _w = jnp.asarray

    def _rec_inputs():
        import jax
        import jax.numpy as jnp
        _rk = jax.random.key(seed)
        x = 7.22e-05 + 1 * jax.random.normal(jax.random.fold_in(_rk, 1), (4, 256, 256), jnp.float32)
        _lenS = 256 - jax.random.randint(jax.random.fold_in(_rk, 7), (4,), 0, max(1, 256 // 4) + 1, jnp.int32)
        _lenS2 = 256 - jax.random.randint(jax.random.fold_in(_rk, 8), (4,), 0, max(1, 256 // 4) + 1, jnp.int32)
        _ctx_1024P = jax.random.normal(jax.random.fold_in(_rk, 11), (4, 16, 128), jnp.float32)
        _ctx_1024c = jax.random.dirichlet(jax.random.fold_in(_rk, 511), 0.3 * jnp.ones((16,), jnp.float32), (4, 256))
        _ctx_1024t = jnp.einsum('bsk,bkd->bsd', _ctx_1024c, _ctx_1024P)
        _ctx_1024t = _ctx_1024t * jax.lax.rsqrt(jnp.mean(jnp.square(_ctx_1024t)) + 1e-12) * 0.953939
        ctx_1024 = 2.81802e-05 + 1.00001 * (_ctx_1024t + 0.3 * jax.random.normal(jax.random.fold_in(_rk, 611), (4, 256, 128), jnp.float32))
        fside_BxS2xS2_0 = -3.05549e-07 + 0.0199987 * jax.random.normal(jax.random.fold_in(_rk, 12), (4, 256, 256), jnp.float32)
        _g = jax.random.normal(jax.random.fold_in(_rk, 9001), (2, 4), jnp.float32)
        _g = jnp.sign(_g) * jnp.maximum(jnp.abs(_g), 1.0) + (_g == 0) * 1.0
        g_xattn = _g[0]
        g_ffn = _g[1]
        return (x, ctx_1024, fside_BxS2xS2_0, g_xattn, g_ffn)
    x, ctx_1024, fside_BxS2xS2_0, g_xattn, g_ffn = _rec_inputs()

    def _L0_xattn_setup():
        import jax, jax.numpy as jnp
        import numpy as np
        key = jax.random.key(seed)
        ks = jax.random.split(key, 6)
        B, L, N, C, D = (8, 64, 256, 128, 128)
        return {'teacher_logits': jax.random.normal(ks[0], (B, L, N), dtype=jnp.float32), 'teacher_features': jax.random.normal(ks[1], (B, N, C), dtype=jnp.float32), 'Wq': jax.random.normal(ks[2], (D, C), dtype=jnp.float32) * (1.0 / np.sqrt(C)), 'bq': jnp.zeros((D,), dtype=jnp.float32), 'Wk': jax.random.normal(ks[3], (D, C), dtype=jnp.float32) * (1.0 / np.sqrt(C)), 'bk': jnp.zeros((D,), dtype=jnp.float32)}
    _L0_xattn_all = _L0_xattn_setup()
    _L0_xattn_in = {k: v for k, v in _L0_xattn_all.items() if k in ('Wq', 'bq', 'Wk', 'bk')}
    del _L0_xattn_all

    def _L0_ffn_setup():
        import jax, jax.numpy as jnp
        import numpy as np
        BLOCK_SIZE = 32
        HIDDEN_SIZE = 256
        MLP_DIM = 2048
        NVFP4_LUT = jnp.array([0.0, 0.5, 1.0, 1.5, 2.0, 3.0, 4.0, 6.0, 0.0, -0.5, -1.0, -1.5, -2.0, -3.0, -4.0, -6.0], dtype=jnp.float32)

        def dequant_nvfp4(W_packed, scales, block=BLOCK_SIZE):
            N = W_packed.shape[0]
            low = W_packed & 15
            high = W_packed >> 4 & 15
            idx = jnp.stack([low, high], axis=-1).reshape(N, -1)
            vals = NVFP4_LUT[idx]
            K = vals.shape[1]
            vals = vals.reshape(N, K // block, block) * scales[:, :, None]
            return vals.reshape(N, K)
        key = jax.random.key(seed)
        ks = jax.random.split(key, 7)
        x = jax.random.normal(ks[0], (4, 32, HIDDEN_SIZE), dtype=jnp.float32)
        gate_W_packed = jax.random.randint(ks[1], (MLP_DIM, HIDDEN_SIZE // 2), 0, 32, dtype=jnp.int32)
        gate_scales = jax.random.uniform(ks[2], (MLP_DIM, HIDDEN_SIZE // BLOCK_SIZE), dtype=jnp.float32) * 0.1 + 0.001
        up_W_packed = jax.random.randint(ks[3], (MLP_DIM, HIDDEN_SIZE // 2), 0, 32, dtype=jnp.int32)
        up_scales = jax.random.uniform(ks[4], (MLP_DIM, HIDDEN_SIZE // BLOCK_SIZE), dtype=jnp.float32) * 0.1 + 0.001
        down_W_packed = jax.random.randint(ks[5], (HIDDEN_SIZE, MLP_DIM // 2), 0, 32, dtype=jnp.int32)
        down_scales = jax.random.uniform(ks[6], (HIDDEN_SIZE, MLP_DIM // BLOCK_SIZE), dtype=jnp.float32) * 0.1 + 0.001
        return {'x': x, 'gate_W_packed': gate_W_packed, 'gate_scales': gate_scales, 'up_W_packed': up_W_packed, 'up_scales': up_scales, 'down_W_packed': down_W_packed, 'down_scales': down_scales}
    _L0_ffn_all = _L0_ffn_setup()
    _L0_ffn_in = {k: v for k, v in _L0_ffn_all.items() if k in ('gate_W_packed', 'gate_scales', 'up_W_packed', 'up_scales', 'down_W_packed', 'down_scales')}
    del _L0_ffn_all

    def _L1_xattn_setup():
        import jax, jax.numpy as jnp
        import numpy as np
        EPS = 1e-06
        QMAX = 127.0

        def _smooth_quant_linear(x, w):
            amax_x = jnp.max(jnp.abs(x), axis=0)
            amax_w = jnp.max(jnp.abs(w), axis=0)
            s = jnp.sqrt(jnp.maximum(amax_x, EPS) / jnp.maximum(amax_w, EPS))
            s = jnp.maximum(s, EPS)
            xs = x / s
            ws = w * s
            x_scale = jnp.maximum(jnp.max(jnp.abs(xs), axis=-1, keepdims=True), EPS) / QMAX
            w_scale = jnp.maximum(jnp.max(jnp.abs(ws), axis=-1, keepdims=True), EPS) / QMAX
            x_q = jnp.clip(jnp.round(xs / x_scale), -QMAX, QMAX)
            w_q = jnp.clip(jnp.round(ws / w_scale), -QMAX, QMAX)
            return x_q @ w_q.T * x_scale * w_scale.T

        def _expert_forward(xe, guw, dw):
            h = _smooth_quant_linear(xe, guw)
            gate, up = jnp.split(h, 2, axis=-1)
            a = jax.nn.silu(gate) * up
            return _smooth_quant_linear(a, dw)
        key = jax.random.key(seed)
        k1, k2, k3 = jax.random.split(key, 3)
        E, T, D, I = (8, 256, 256, 128)
        x = jax.random.normal(k1, (E, T, D), dtype=jnp.float32)
        gate_up_weight = jax.random.normal(k2, (E, 2 * I, D), dtype=jnp.float32) * 0.02
        down_weight = jax.random.normal(k3, (E, D, I), dtype=jnp.float32) * 0.02
        return {'x': x, 'gate_up_weight': gate_up_weight, 'down_weight': down_weight}
    _L1_xattn_all = _L1_xattn_setup()
    _L1_xattn_in = {k: v for k, v in _L1_xattn_all.items() if k in ()}
    del _L1_xattn_all

    def _L1_ffn_setup():
        import jax, jax.numpy as jnp
        import numpy as np
        TOPK = 2
        NORM_TOPK = True
        SCALE = 1.0
        EPS = 1e-09
        key = jax.random.key(seed)
        ks = jax.random.split(key, 9)
        h, i, E = (256, 128, 16)
        std = 0.02
        return {'x': jax.random.normal(ks[0], (1, 256, h), jnp.float32), 'Wr': jax.random.normal(ks[1], (E, h), jnp.float32) * std, 'bias': jnp.zeros((E,), jnp.float32), 'Wg': jax.random.normal(ks[2], (E, h, i), jnp.float32) * std, 'Wu': jax.random.normal(ks[3], (E, h, i), jnp.float32) * std, 'Wd': jax.random.normal(ks[4], (E, i, h), jnp.float32) * std, 'sWg': jax.random.normal(ks[5], (h, i), jnp.float32) * std, 'sWu': jax.random.normal(ks[6], (h, i), jnp.float32) * std, 'sWd': jax.random.normal(ks[7], (i, h), jnp.float32) * std}
    _L1_ffn_all = _L1_ffn_setup()
    _L1_ffn_in = {k: v for k, v in _L1_ffn_all.items() if k in ('Wr', 'bias', 'Wg', 'Wu', 'Wd', 'sWg', 'sWu', 'sWd')}
    del _L1_ffn_all

    def _L2_xattn_setup():
        import jax, jax.numpy as jnp
        import numpy as np
        B, S1, S2, DCA = (2, 256, 128, 16)
        QDIM, KDIM, H = (256, 128, 16)
        HD = QDIM // H
        SCALE = HD ** (-0.5)
        EPS = 1e-06
        DCA_WEIGHT = 1.0

        def _ln(t, w, b):
            m = jnp.mean(t, axis=-1, keepdims=True)
            v = jnp.var(t, axis=-1, keepdims=True)
            return (t - m) * jax.lax.rsqrt(v + EPS) * w + b

        def _attn(q, k, v):
            s = jnp.einsum('bhqd,bhkd->bhqk', q, k) * SCALE
            p = jax.nn.softmax(s, axis=-1)
            return jnp.einsum('bhqk,bhkd->bhqd', p, v)
        key = jax.random.key(seed)
        ks = jax.random.split(key, 8)
        w = lambda k, shape: jax.random.normal(k, shape, jnp.float32) * 0.02
        return {'x': jax.random.normal(ks[0], (B, S1, QDIM), jnp.float32), 'y': jax.random.normal(ks[1], (B, S2 + DCA, KDIM), jnp.float32), 'Wq': w(ks[2], (QDIM, QDIM)), 'bq': jnp.zeros((QDIM,), jnp.float32), 'Wk': w(ks[3], (KDIM, QDIM)), 'bk': jnp.zeros((QDIM,), jnp.float32), 'Wv': w(ks[4], (KDIM, QDIM)), 'bv': jnp.zeros((QDIM,), jnp.float32), 'Wkv_dca': w(ks[5], (KDIM, 2 * QDIM)), 'bkv_dca': jnp.zeros((2 * QDIM,), jnp.float32), 'qn_w': jnp.ones((HD,), jnp.float32), 'qn_b': jnp.zeros((HD,), jnp.float32), 'kn_w': jnp.ones((HD,), jnp.float32), 'kn_b': jnp.zeros((HD,), jnp.float32), 'kn_dca_w': jnp.ones((HD,), jnp.float32), 'kn_dca_b': jnp.zeros((HD,), jnp.float32), 'Wo': w(ks[6], (QDIM, QDIM)), 'bo': jnp.zeros((QDIM,), jnp.float32)}
    _L2_xattn_all = _L2_xattn_setup()
    _L2_xattn_in = {k: v for k, v in _L2_xattn_all.items() if k in ('Wq', 'bq', 'Wk', 'bk', 'Wv', 'bv', 'Wkv_dca', 'bkv_dca', 'qn_w', 'qn_b', 'kn_w', 'kn_b', 'kn_dca_w', 'kn_dca_b', 'Wo', 'bo')}
    del _L2_xattn_all

    def _L2_ffn_setup():
        import jax, jax.numpy as jnp
        import numpy as np
        BLOCK = 32
        BITS = 8

        def bf16_round(x):
            return x.astype(jnp.bfloat16).astype(jnp.float32)

        def mx_quant(x):
            s = x.shape
            xb = x.reshape(s[:-1] + (s[-1] // BLOCK, BLOCK))
            amax = jnp.max(jnp.abs(xb), axis=-1, keepdims=True)
            shared_exp = jnp.floor(jnp.log2(jnp.where(amax > 0, amax, 1.0)))
            scale = jnp.exp2(shared_exp - (BITS - 2))
            q = jnp.clip(jnp.round(xb / scale), -2.0 ** (BITS - 1), 2.0 ** (BITS - 1) - 1) * scale
            q = jnp.where(amax > 0, q, 0.0).reshape(s)
            return x + jax.lax.stop_gradient(q - x)

        def mx_linear(x, W, b):
            y = jnp.einsum('btk,ok->bto', mx_quant(x), mx_quant(W))
            return bf16_round(y + b)

        def mx_layernorm(x, w, b, eps=1e-05):
            mu = jnp.mean(x, axis=-1, keepdims=True)
            var = jnp.mean(jnp.square(x - mu), axis=-1, keepdims=True)
            return bf16_round((x - mu) * jax.lax.rsqrt(var + eps) * w + b)

        def mx_gelu(x):
            c = jnp.float32(0.7978845608028654)
            return bf16_round(0.5 * x * (1.0 + jnp.tanh(c * (x + 0.044715 * x * x * x))))
        key = jax.random.key(seed)
        ks = jax.random.split(key, 5)
        B, S, H = (2, 256, 256)
        inputs = jax.random.normal(ks[0], (B, S, H), dtype=jnp.float32)
        ln_w = jnp.ones((H,), dtype=jnp.float32)
        ln_b = jnp.zeros((H,), dtype=jnp.float32)
        W1 = jax.random.normal(ks[1], (4 * H, H), dtype=jnp.float32) * (1.0 / np.sqrt(H))
        b1 = jnp.zeros((4 * H,), dtype=jnp.float32)
        W2 = jax.random.normal(ks[2], (H, 4 * H), dtype=jnp.float32) * (1.0 / np.sqrt(4 * H))
        b2 = jnp.zeros((H,), dtype=jnp.float32)
        return {'inputs': inputs, 'ln_w': ln_w, 'ln_b': ln_b, 'W1': W1, 'b1': b1, 'W2': W2, 'b2': b2}
    _L2_ffn_all = _L2_ffn_setup()
    _L2_ffn_in = {k: v for k, v in _L2_ffn_all.items() if k in ('ln_w', 'ln_b', 'W1', 'b1', 'W2', 'b2')}
    del _L2_ffn_all

    def _L3_xattn_setup():
        import jax, jax.numpy as jnp
        import numpy as np
        B_, L_, D_MODEL = (4, 256, 128)
        D_STATE, D_CONV, EXPAND = (16, 4, 2)
        D_INNER = EXPAND * D_MODEL
        DT_RANK = (D_MODEL + 15) // 16

        def silu(x):
            return x * jax.nn.sigmoid(x)
        key = jax.random.key(seed)
        ks = jax.random.split(key, 10)
        f32 = jnp.float32
        hidden_states = jax.random.normal(ks[0], (B_, L_, D_MODEL), dtype=f32)
        z = jax.random.normal(ks[1], (B_, D_INNER, L_), dtype=f32)
        in_proj_w = jax.random.normal(ks[2], (D_INNER, D_MODEL), dtype=f32) * 0.02
        conv_w = jax.random.normal(ks[3], (D_INNER, 1, D_CONV), dtype=f32) * 0.1
        conv_b = jax.random.normal(ks[4], (D_INNER,), dtype=f32) * 0.02
        x_proj_w = jax.random.normal(ks[5], (DT_RANK + 2 * D_STATE, D_INNER), dtype=f32) * 0.02
        dt_proj_w = jax.random.uniform(ks[6], (D_INNER, DT_RANK), dtype=f32, minval=-DT_RANK ** (-0.5), maxval=DT_RANK ** (-0.5))
        dt = jnp.exp(jax.random.uniform(ks[7], (D_INNER,), dtype=f32, minval=np.log(0.001), maxval=np.log(0.1)))
        dt_proj_b = jnp.log(jnp.expm1(dt))
        A_log = jnp.log(jnp.broadcast_to(jnp.arange(1, D_STATE + 1, dtype=f32), (D_INNER, D_STATE)))
        D = jnp.ones((D_INNER,), f32)
        return {'hidden_states': hidden_states, 'z': z, 'in_proj_w': in_proj_w, 'conv_w': conv_w, 'conv_b': conv_b, 'x_proj_w': x_proj_w, 'dt_proj_w': dt_proj_w, 'dt_proj_b': dt_proj_b, 'A_log': A_log, 'D': D}
    _L3_xattn_all = _L3_xattn_setup()
    _L3_xattn_in = {k: v for k, v in _L3_xattn_all.items() if k in ('in_proj_w', 'conv_w', 'conv_b', 'x_proj_w', 'dt_proj_w', 'dt_proj_b', 'A_log', 'D')}
    del _L3_xattn_all

    def _L3_ffn_setup():
        import jax, jax.numpy as jnp
        import numpy as np
        B, T, D = (1, 128, 256)
        F_DIM = 176
        E = 8
        TOPK = 2
        key = jax.random.key(seed)
        ks = jax.random.split(key, 5)
        x = jax.random.normal(ks[0], (B, T, D), dtype=jnp.float32)
        gate_w = jax.random.normal(ks[1], (E, D), dtype=jnp.float32) * 0.02
        gate_proj = jax.random.normal(ks[2], (E, F_DIM, D), dtype=jnp.float32) * 0.02
        up_proj = jax.random.normal(ks[3], (E, F_DIM, D), dtype=jnp.float32) * 0.02
        down_proj = jax.random.normal(ks[4], (E, D, F_DIM), dtype=jnp.float32) * 0.02
        return {'x': x, 'gate_w': gate_w, 'gate_proj': gate_proj, 'up_proj': up_proj, 'down_proj': down_proj}
    _L3_ffn_all = _L3_ffn_setup()
    _L3_ffn_in = {k: v for k, v in _L3_ffn_all.items() if k in ('gate_w', 'gate_proj', 'up_proj', 'down_proj')}
    del _L3_ffn_all
    return {'x': x, 'ctx_1024': ctx_1024, 'fside_BxS2xS2_0': fside_BxS2xS2_0, 'g_xattn': g_xattn, 'g_ffn': g_ffn, 'L0_xattn_Wq': _L0_xattn_in['Wq'], 'L0_xattn_bq': _L0_xattn_in['bq'], 'L0_xattn_Wk': _L0_xattn_in['Wk'], 'L0_xattn_bk': _L0_xattn_in['bk'], 'L0_ffn_gate_W_packed': _L0_ffn_in['gate_W_packed'], 'L0_ffn_gate_scales': _L0_ffn_in['gate_scales'], 'L0_ffn_up_W_packed': _L0_ffn_in['up_W_packed'], 'L0_ffn_up_scales': _L0_ffn_in['up_scales'], 'L0_ffn_down_W_packed': _L0_ffn_in['down_W_packed'], 'L0_ffn_down_scales': _L0_ffn_in['down_scales'], 'L1_ffn_Wr': _L1_ffn_in['Wr'], 'L1_ffn_bias': _L1_ffn_in['bias'], 'L1_ffn_Wg': _L1_ffn_in['Wg'], 'L1_ffn_Wu': _L1_ffn_in['Wu'], 'L1_ffn_Wd': _L1_ffn_in['Wd'], 'L1_ffn_sWg': _L1_ffn_in['sWg'], 'L1_ffn_sWu': _L1_ffn_in['sWu'], 'L1_ffn_sWd': _L1_ffn_in['sWd'], 'L2_xattn_Wq': _L2_xattn_in['Wq'], 'L2_xattn_bq': _L2_xattn_in['bq'], 'L2_xattn_Wk': _L2_xattn_in['Wk'], 'L2_xattn_bk': _L2_xattn_in['bk'], 'L2_xattn_Wv': _L2_xattn_in['Wv'], 'L2_xattn_bv': _L2_xattn_in['bv'], 'L2_xattn_Wkv_dca': _L2_xattn_in['Wkv_dca'], 'L2_xattn_bkv_dca': _L2_xattn_in['bkv_dca'], 'L2_xattn_qn_w': _L2_xattn_in['qn_w'], 'L2_xattn_qn_b': _L2_xattn_in['qn_b'], 'L2_xattn_kn_w': _L2_xattn_in['kn_w'], 'L2_xattn_kn_b': _L2_xattn_in['kn_b'], 'L2_xattn_kn_dca_w': _L2_xattn_in['kn_dca_w'], 'L2_xattn_kn_dca_b': _L2_xattn_in['kn_dca_b'], 'L2_xattn_Wo': _L2_xattn_in['Wo'], 'L2_xattn_bo': _L2_xattn_in['bo'], 'L2_ffn_ln_w': _L2_ffn_in['ln_w'], 'L2_ffn_ln_b': _L2_ffn_in['ln_b'], 'L2_ffn_W1': _L2_ffn_in['W1'], 'L2_ffn_b1': _L2_ffn_in['b1'], 'L2_ffn_W2': _L2_ffn_in['W2'], 'L2_ffn_b2': _L2_ffn_in['b2'], 'L3_xattn_in_proj_w': _L3_xattn_in['in_proj_w'], 'L3_xattn_conv_w': _L3_xattn_in['conv_w'], 'L3_xattn_conv_b': _L3_xattn_in['conv_b'], 'L3_xattn_x_proj_w': _L3_xattn_in['x_proj_w'], 'L3_xattn_dt_proj_w': _L3_xattn_in['dt_proj_w'], 'L3_xattn_dt_proj_b': _L3_xattn_in['dt_proj_b'], 'L3_xattn_A_log': _L3_xattn_in['A_log'], 'L3_xattn_D': _L3_xattn_in['D'], 'L3_ffn_gate_w': _L3_ffn_in['gate_w'], 'L3_ffn_gate_proj': _L3_ffn_in['gate_proj'], 'L3_ffn_up_proj': _L3_ffn_in['up_proj'], 'L3_ffn_down_proj': _L3_ffn_in['down_proj']}

def reference(x, ctx_1024, fside_BxS2xS2_0, g_xattn, g_ffn, L0_xattn_Wq, L0_xattn_bq, L0_xattn_Wk, L0_xattn_bk, L0_ffn_gate_W_packed, L0_ffn_gate_scales, L0_ffn_up_W_packed, L0_ffn_up_scales, L0_ffn_down_W_packed, L0_ffn_down_scales, L1_ffn_Wr, L1_ffn_bias, L1_ffn_Wg, L1_ffn_Wu, L1_ffn_Wd, L1_ffn_sWg, L1_ffn_sWu, L1_ffn_sWd, L2_xattn_Wq, L2_xattn_bq, L2_xattn_Wk, L2_xattn_bk, L2_xattn_Wv, L2_xattn_bv, L2_xattn_Wkv_dca, L2_xattn_bkv_dca, L2_xattn_qn_w, L2_xattn_qn_b, L2_xattn_kn_w, L2_xattn_kn_b, L2_xattn_kn_dca_w, L2_xattn_kn_dca_b, L2_xattn_Wo, L2_xattn_bo, L2_ffn_ln_w, L2_ffn_ln_b, L2_ffn_W1, L2_ffn_b1, L2_ffn_W2, L2_ffn_b2, L3_xattn_in_proj_w, L3_xattn_conv_w, L3_xattn_conv_b, L3_xattn_x_proj_w, L3_xattn_dt_proj_w, L3_xattn_dt_proj_b, L3_xattn_A_log, L3_xattn_D, L3_ffn_gate_w, L3_ffn_gate_proj, L3_ffn_up_proj, L3_ffn_down_proj):
    import jax
    import jax.numpy as jnp

    def _L0_xattn_ref(teacher_logits, teacher_features, Wq, bq, Wk, bk):
        import jax, jax.numpy as jnp
        import numpy as np
        query = jnp.einsum('bnc,dc->bnd', teacher_features, Wq) + bq
        key = jnp.einsum('bnc,dc->bnd', teacher_features, Wk) + bk
        energy = jnp.einsum('bnd,bmd->bnm', query, key)
        attention = jax.nn.softmax(energy, axis=-1)
        x_m = jnp.einsum('bln,bmn->blm', teacher_logits, attention)
        return x_m

    def _L0_ffn_ref(x, gate_W_packed, gate_scales, up_W_packed, up_scales, down_W_packed, down_scales):
        import jax, jax.numpy as jnp
        import numpy as np
        BLOCK_SIZE = 32
        HIDDEN_SIZE = 256
        MLP_DIM = 2048
        NVFP4_LUT = jnp.array([0.0, 0.5, 1.0, 1.5, 2.0, 3.0, 4.0, 6.0, 0.0, -0.5, -1.0, -1.5, -2.0, -3.0, -4.0, -6.0], dtype=jnp.float32)

        def dequant_nvfp4(W_packed, scales, block=BLOCK_SIZE):
            N = W_packed.shape[0]
            low = W_packed & 15
            high = W_packed >> 4 & 15
            idx = jnp.stack([low, high], axis=-1).reshape(N, -1)
            vals = NVFP4_LUT[idx]
            K = vals.shape[1]
            vals = vals.reshape(N, K // block, block) * scales[:, :, None]
            return vals.reshape(N, K)
        B, S, H = x.shape
        xt = x.reshape(B * S, H)
        Wg = dequant_nvfp4(gate_W_packed, gate_scales)
        Wu = dequant_nvfp4(up_W_packed, up_scales)
        Wd = dequant_nvfp4(down_W_packed, down_scales)
        gate = jnp.einsum('th,nh->tn', xt, Wg)
        up = jnp.einsum('th,nh->tn', xt, Wu)
        gelu = jnp.tanh(0.7978845608028654 * (gate + 0.044715 * gate ** 3)) * gate * 0.5 + gate * 0.5
        inter = gelu * up
        out = jnp.einsum('tn,hn->th', inter, Wd)
        return out.reshape(B, S, H)

    def _L1_xattn_ref(x, gate_up_weight, down_weight):
        import jax, jax.numpy as jnp
        import numpy as np
        EPS = 1e-06
        QMAX = 127.0

        def _smooth_quant_linear(x, w):
            amax_x = jnp.max(jnp.abs(x), axis=0)
            amax_w = jnp.max(jnp.abs(w), axis=0)
            s = jnp.sqrt(jnp.maximum(amax_x, EPS) / jnp.maximum(amax_w, EPS))
            s = jnp.maximum(s, EPS)
            xs = x / s
            ws = w * s
            x_scale = jnp.maximum(jnp.max(jnp.abs(xs), axis=-1, keepdims=True), EPS) / QMAX
            w_scale = jnp.maximum(jnp.max(jnp.abs(ws), axis=-1, keepdims=True), EPS) / QMAX
            x_q = jnp.clip(jnp.round(xs / x_scale), -QMAX, QMAX)
            w_q = jnp.clip(jnp.round(ws / w_scale), -QMAX, QMAX)
            return x_q @ w_q.T * x_scale * w_scale.T

        def _expert_forward(xe, guw, dw):
            h = _smooth_quant_linear(xe, guw)
            gate, up = jnp.split(h, 2, axis=-1)
            a = jax.nn.silu(gate) * up
            return _smooth_quant_linear(a, dw)
        return jax.vmap(_expert_forward)(x, gate_up_weight, down_weight)

    def _L1_ffn_ref(x, Wr, bias, Wg, Wu, Wd, sWg, sWu, sWd):
        import jax, jax.numpy as jnp
        import numpy as np
        TOPK = 2
        NORM_TOPK = True
        SCALE = 1.0
        EPS = 1e-09
        b, s, h = x.shape
        E = Wr.shape[0]
        xt = x.reshape(b * s, h)
        logits = xt @ Wr.T + bias
        probs = jax.nn.softmax(logits, axis=-1)
        topk_val, topk_idx = jax.lax.top_k(probs, TOPK)
        if NORM_TOPK:
            w = topk_val / (jnp.sum(topk_val, axis=-1, keepdims=True) + EPS)
        else:
            w = topk_val
        w = w * SCALE
        g = jnp.einsum('th,ehi->tei', xt, Wg)
        u = jnp.einsum('th,ehi->tei', xt, Wu)
        y = jnp.einsum('tei,eih->teh', jax.nn.silu(g) * u, Wd)
        oh = jax.nn.one_hot(topk_idx, E, dtype=x.dtype)
        routed = jnp.einsum('tke,tk,teh->th', oh, w, y)
        shared = jax.nn.silu(xt @ sWg) * (xt @ sWu) @ sWd
        return (routed + shared).reshape(b, s, h)

    def _L2_xattn_ref(x, y, Wq, bq, Wk, bk, Wv, bv, Wkv_dca, bkv_dca, qn_w, qn_b, kn_w, kn_b, kn_dca_w, kn_dca_b, Wo, bo):
        import jax, jax.numpy as jnp
        import numpy as np
        B, S1, S2, DCA = (2, 256, 128, 16)
        QDIM, KDIM, H = (256, 128, 16)
        HD = QDIM // H
        SCALE = HD ** (-0.5)
        EPS = 1e-06
        DCA_WEIGHT = 1.0

        def _ln(t, w, b):
            m = jnp.mean(t, axis=-1, keepdims=True)
            v = jnp.var(t, axis=-1, keepdims=True)
            return (t - m) * jax.lax.rsqrt(v + EPS) * w + b

        def _attn(q, k, v):
            s = jnp.einsum('bhqd,bhkd->bhqk', q, k) * SCALE
            p = jax.nn.softmax(s, axis=-1)
            return jnp.einsum('bhqk,bhkd->bhqd', p, v)
        b, s1, _ = x.shape
        y_dca = y[:, -DCA:, :]
        y_main = y[:, :-DCA, :]
        kv_dca = (y_dca @ Wkv_dca + bkv_dca).reshape(b, DCA, 2, H, HD)
        k_dca = _ln(kv_dca[:, :, 0], kn_dca_w, kn_dca_b)
        v_dca = kv_dca[:, :, 1]
        s2 = y_main.shape[1]
        q = _ln((x @ Wq + bq).reshape(b, s1, H, HD), qn_w, qn_b)
        kv = jnp.concatenate([y_main @ Wk + bk, y_main @ Wv + bv], axis=-1)
        kv = kv.reshape(b, s2, H, 2 * HD)
        k = _ln(kv[..., :HD], kn_w, kn_b)
        v = kv[..., HD:]
        qT = q.transpose(0, 2, 1, 3)
        ctx = _attn(qT, k.transpose(0, 2, 1, 3), v.transpose(0, 2, 1, 3))
        ctx = ctx.transpose(0, 2, 1, 3).reshape(b, s1, QDIM)
        ctx_dca = _attn(qT, k_dca.transpose(0, 2, 1, 3), v_dca.transpose(0, 2, 1, 3))
        ctx_dca = ctx_dca.transpose(0, 2, 1, 3).reshape(b, s1, QDIM)
        ctx = ctx + DCA_WEIGHT * ctx_dca
        return ctx @ Wo + bo

    def _L2_ffn_ref(inputs, ln_w, ln_b, W1, b1, W2, b2):
        import jax, jax.numpy as jnp
        import numpy as np
        BLOCK = 32
        BITS = 8

        def bf16_round(x):
            return x.astype(jnp.bfloat16).astype(jnp.float32)

        def mx_quant(x):
            s = x.shape
            xb = x.reshape(s[:-1] + (s[-1] // BLOCK, BLOCK))
            amax = jnp.max(jnp.abs(xb), axis=-1, keepdims=True)
            shared_exp = jnp.floor(jnp.log2(jnp.where(amax > 0, amax, 1.0)))
            scale = jnp.exp2(shared_exp - (BITS - 2))
            q = jnp.clip(jnp.round(xb / scale), -2.0 ** (BITS - 1), 2.0 ** (BITS - 1) - 1) * scale
            q = jnp.where(amax > 0, q, 0.0).reshape(s)
            return x + jax.lax.stop_gradient(q - x)

        def mx_linear(x, W, b):
            y = jnp.einsum('btk,ok->bto', mx_quant(x), mx_quant(W))
            return bf16_round(y + b)

        def mx_layernorm(x, w, b, eps=1e-05):
            mu = jnp.mean(x, axis=-1, keepdims=True)
            var = jnp.mean(jnp.square(x - mu), axis=-1, keepdims=True)
            return bf16_round((x - mu) * jax.lax.rsqrt(var + eps) * w + b)

        def mx_gelu(x):
            c = jnp.float32(0.7978845608028654)
            return bf16_round(0.5 * x * (1.0 + jnp.tanh(c * (x + 0.044715 * x * x * x))))
        x = bf16_round(inputs)
        residual = bf16_round(inputs)
        h = mx_layernorm(x, ln_w, ln_b)
        h = mx_linear(h, W1, b1)
        h = mx_gelu(h)
        h = mx_linear(h, W2, b2)
        return bf16_round(residual + h)

    def _L3_xattn_ref(hidden_states, z, in_proj_w, conv_w, conv_b, x_proj_w, dt_proj_w, dt_proj_b, A_log, D):
        import jax, jax.numpy as jnp
        import numpy as np
        B_, L_, D_MODEL = (4, 256, 128)
        D_STATE, D_CONV, EXPAND = (16, 4, 2)
        D_INNER = EXPAND * D_MODEL
        DT_RANK = (D_MODEL + 15) // 16

        def silu(x):
            return x * jax.nn.sigmoid(x)
        Bsz, L, _ = hidden_states.shape
        d_inner, _, d_conv = conv_w.shape
        dt_rank = dt_proj_w.shape[1]
        d_state = A_log.shape[1]
        x = jnp.einsum('bld,ed->bel', hidden_states, in_proj_w)
        xc = jax.lax.conv_general_dilated(x, conv_w, window_strides=(1,), padding=[(d_conv - 1, 0)], feature_group_count=d_inner, dimension_numbers=('NCH', 'OIH', 'NCH'))
        x = silu(xc + conv_b[None, :, None])
        x_dbl = jnp.einsum('bdl,ed->bel', x, x_proj_w)
        dt_low, Bm, Cm = jnp.split(x_dbl, [dt_rank, dt_rank + d_state], axis=1)
        dt = jnp.einsum('brl,dr->bdl', dt_low, dt_proj_w)
        dt = jax.nn.softplus(dt + dt_proj_b[None, :, None])
        A = -jnp.exp(A_log)
        dt_t = jnp.moveaxis(dt, -1, 0)
        B_t = jnp.moveaxis(Bm, -1, 0)
        C_t = jnp.moveaxis(Cm, -1, 0)
        u_t = jnp.moveaxis(x, -1, 0)

        def step(state, inp):
            d, b, c, u = inp
            dA = jnp.exp(d[..., None] * A)
            state = state * dA + (d * u)[..., None] * b[:, None, :]
            y = jnp.einsum('bdn,bn->bd', state, c)
            return (state, y)
        state0 = jnp.zeros((Bsz, d_inner, d_state), x.dtype)
        _, ys = jax.lax.scan(step, state0, (dt_t, B_t, C_t, u_t))
        y = jnp.moveaxis(ys, 0, 2)
        y = y + D[None, :, None] * x
        y = y * silu(z)
        return jnp.swapaxes(y, 1, 2)

    def _L3_ffn_ref(x, gate_w, gate_proj, up_proj, down_proj):
        import jax, jax.numpy as jnp
        import numpy as np
        B, T, D = (1, 128, 256)
        F_DIM = 176
        E = 8
        TOPK = 2
        b, t, d = x.shape
        x_flat = x.reshape(-1, d)
        n = x_flat.shape[0]
        router_logits = x_flat @ gate_w.T
        top_w, sel = jax.lax.top_k(router_logits, TOPK)
        top_w = jax.nn.softmax(top_w, axis=-1)
        tok_ids = jnp.arange(n)[:, None]
        tw = jnp.zeros((n, E), dtype=x.dtype).at[tok_ids, sel].add(top_w)
        g = jnp.einsum('nd,efd->enf', x_flat, gate_proj)
        u = jnp.einsum('nd,efd->enf', x_flat, up_proj)
        h = jax.nn.silu(g) * u
        eo = jnp.einsum('enf,edf->end', h, down_proj)
        out = jnp.einsum('end,ne->nd', eo, tw)
        return out.reshape(b, t, d)
    x = x + jnp.tanh(g_xattn[0]) * _L0_xattn_ref(_layernorm(x, axis=-1), ctx_1024, L0_xattn_Wq, L0_xattn_bq, L0_xattn_Wk, L0_xattn_bk)
    x = x + jnp.tanh(g_ffn[0]) * _L0_ffn_ref(_layernorm(x, axis=-1), L0_ffn_gate_W_packed, L0_ffn_gate_scales, L0_ffn_up_W_packed, L0_ffn_up_scales, L0_ffn_down_W_packed, L0_ffn_down_scales)
    x = x + jnp.tanh(g_xattn[1]) * _L1_xattn_ref(_layernorm(x, axis=-1), fside_BxS2xS2_0, ctx_1024)
    x = x + jnp.tanh(g_ffn[1]) * _L1_ffn_ref(_layernorm(x, axis=-1), L1_ffn_Wr, L1_ffn_bias, L1_ffn_Wg, L1_ffn_Wu, L1_ffn_Wd, L1_ffn_sWg, L1_ffn_sWu, L1_ffn_sWd)
    x = x + jnp.tanh(g_xattn[2]) * _L2_xattn_ref(_layernorm(x, axis=-1), ctx_1024, L2_xattn_Wq, L2_xattn_bq, L2_xattn_Wk, L2_xattn_bk, L2_xattn_Wv, L2_xattn_bv, L2_xattn_Wkv_dca, L2_xattn_bkv_dca, L2_xattn_qn_w, L2_xattn_qn_b, L2_xattn_kn_w, L2_xattn_kn_b, L2_xattn_kn_dca_w, L2_xattn_kn_dca_b, L2_xattn_Wo, L2_xattn_bo)
    x = x + jnp.tanh(g_ffn[2]) * _L2_ffn_ref(_layernorm(x, axis=-1), L2_ffn_ln_w, L2_ffn_ln_b, L2_ffn_W1, L2_ffn_b1, L2_ffn_W2, L2_ffn_b2)
    x = x + jnp.tanh(g_xattn[3]) * _L3_xattn_ref(ctx_1024, _layernorm(x, axis=-1), L3_xattn_in_proj_w, L3_xattn_conv_w, L3_xattn_conv_b, L3_xattn_x_proj_w, L3_xattn_dt_proj_w, L3_xattn_dt_proj_b, L3_xattn_A_log, L3_xattn_D)
    x = x + jnp.tanh(g_ffn[3]) * _L3_ffn_ref(_layernorm(x, axis=-1), L3_ffn_gate_w, L3_ffn_gate_proj, L3_ffn_up_proj, L3_ffn_down_proj)
    return x

_drawn_inputs = setup_inputs


def setup_inputs(seed=0):
    import zlib

    import numpy as np

    out = dict(_drawn_inputs(seed))
    spreads = {'L0_xattn_bq': (0.0, 0.1),
     'L0_xattn_bk': (0.0, 2.0),
     'L1_ffn_bias': (0.0, 0.8),
     'L2_xattn_bq': (0.0, 0.8),
     'L2_xattn_bk': (0.0, 0.8),
     'L2_xattn_bv': (0.0, 0.8),
     'L2_xattn_bkv_dca': (0.0, 0.8),
     'L2_xattn_qn_w': (1.0, 0.6),
     'L2_xattn_qn_b': (0.0, 0.8),
     'L2_xattn_kn_w': (1.0, 0.6),
     'L2_xattn_kn_b': (0.0, 2.0),
     'L2_xattn_kn_dca_w': (1.0, 0.6),
     'L2_xattn_kn_dca_b': (0.0, 2.0),
     'L2_xattn_bo': (0.0, 0.8),
     'L2_ffn_ln_w': (1.0, 0.6),
     'L2_ffn_ln_b': (0.0, 0.8),
     'L2_ffn_b1': (0.0, 0.8),
     'L2_ffn_b2': (0.0, 0.8),
     'L3_xattn_D': (1.0, 0.6)}
    factors = {'g_ffn': 8.0,
     'L1_ffn_Wr': 8.0,
     'L1_ffn_Wg': 8.0,
     'L1_ffn_Wu': 8.0,
     'L1_ffn_Wd': 8.0,
     'L1_ffn_sWg': 8.0,
     'L1_ffn_sWu': 8.0,
     'L1_ffn_sWd': 8.0,
     'L2_xattn_Wq': 8.0,
     'L2_xattn_Wk': 8.0,
     'L2_xattn_Wv': 8.0,
     'L2_xattn_Wkv_dca': 8.0,
     'L2_xattn_Wo': 8.0,
     'L3_xattn_in_proj_w': 8.0,
     'L3_xattn_conv_w': 8.0,
     'L3_xattn_conv_b': 8.0,
     'L3_xattn_x_proj_w': 8.0,
     'L3_xattn_dt_proj_w': 8.0,
     'L3_xattn_dt_proj_b': 8.0,
     'L3_xattn_A_log': 8.0,
     'L3_ffn_gate_w': 39.896,
     'L3_ffn_gate_proj': 41.504,
     'L3_ffn_up_proj': 35.924,
     'L3_ffn_down_proj': 36.087}
    for name, (base, spread) in spreads.items():
        noise = np.random.default_rng([zlib.crc32(name.encode()), seed]).standard_normal(out[name].shape)
        drawn = base * np.exp(spread * noise) if base else spread * noise
        out[name] = jnp.asarray(drawn.astype(out[name].dtype))
    for name, factor in factors.items():
        out[name] = (out[name] * factor).astype(out[name].dtype)
    return out
```

```python
from contextlib import ExitStack

import concourse.bass as bass
from concourse import mybir

P = 128
B, S, D, C = 4, 256, 256, 128
T = B * S
NT = T // P
KD = D // P
HALF = T // 2
TPH = HALF // P
LN_EPS = 1e-5
GELU_C = 0.7978845608028654
ROUND = 12582912.0

ALU = mybir.AluOpType
ACT = mybir.ActivationFunctionType
AX = mybir.AxisListType
F32 = mybir.dt.float32
BF16 = mybir.dt.bfloat16
F16 = mybir.dt.float16
U16 = mybir.dt.uint16
U32 = mybir.dt.uint32
I32 = mybir.dt.int32


class Steps:

    def __init__(self, eng, sem):
        self.eng, self.sem, self.n = eng, sem, 0

    def mark(self, ins):
        ins.then_inc(self.sem, 1)
        self.n += 1

    def settle(self):
        self.eng.wait_ge(self.sem, self.n)

    def link(self, ins):
        self.mark(ins)
        self.settle()


def build(nc, a, out, start=0, stop=99):
    with ExitStack() as ctx:
        def sb(name, shape, dt=F32):
            return ctx.enter_context(nc.sbuf_tensor(name, shape, dt))

        s_out = ctx.enter_context(nc.semaphore("out_stored"))
        held = []

        def sem(name):
            held.append(nc.alloc_semaphore(name=name))
            return held[-1]

        def give_back():
            with nc.Block(f"give_back_{len(held)}") as block:
                @block.gpsimd
                def _(pool):
                    nc.clear_and_free_semaphores(held)
            held.clear()

        ps = ctx.enter_context(nc.psum_tensor("ps", [P, 8, 512], F32))
        psb = ps[:, :, :].rearrange("p b n -> p (b n)").bitcast(BF16).rearrange("p (b n) -> p b n", b=8)

        x = sb("x", [P, NT, D])
        h = sb("h", [P, NT, D])
        hT = sb("hT", [P, KD, T])
        ctxT = sb("ctxT", [P, T])
        yssm = sb("yssm", [P, KD, T])
        ident = sb("ident", [P, P])
        identb = sb("identb", [P, P], BF16)
        iota = sb("iota", [P, 16])
        tg = sb("tg", [P, 8])
        lnst = sb("lnst", [P, NT, 6])
        lnmv = sb("lnmv", [P, NT, 2])
        lnsd = sb("lnsd", [P, 2, NT])
        W1q = sb("W1q", [P, KD, 4 * D], BF16)
        W2q = sb("W2q", [P, 4 * D // P, D], BF16)
        regA = sb("regA", [P, 12288])
        regB = sb("regB", [P, 13056])
        regC = sb("regC", [P, 13056])

        class Arena:

            def __init__(self, *regs):
                self.regs = [[r, 0, r.shape[1]] for r in regs]

            def take(self, shape, dt=F32):
                n = 1
                for s in shape:
                    n *= s
                words = n if dt in (F32, I32, U32) else (n + 1) // 2
                words = (words + 7) // 8 * 8
                for r in self.regs:
                    if r[1] + words <= r[2]:
                        v = r[0][:, r[1]:r[1] + (n if dt in (F32, I32, U32) else n // 2)]
                        r[1] += words
                        break
                else:
                    raise ValueError(f"arena full for {shape}: {[(q[1], q[2]) for q in self.regs]}")
                if dt != F32:
                    v = v.bitcast(dt)
                if len(shape) > 1:
                    names = "abcde"[:len(shape)]
                    v = v.rearrange(f"p ({' '.join(names)}) -> p {' '.join(names)}",
                                    **{k: s for k, s in zip(names[1:], shape[1:])})
                return v

        def norm_on_vector(dve, v, s_var, s_sd, s_h, interleave=False, src=x, dst=h):
            for t in range(NT):
                v.mark(nc.vector.bn_stats(lnst[:, t, :], src[:, t, :]))
            v.settle()
            for t in range(NT):
                v.mark(nc.vector.bn_aggr(lnmv[:, t, :], lnst[:, t, :]))
            v.settle()
            nc.vector.tensor_scalar(lnsd[:, 0, :], lnmv[:, :, 1], LN_EPS, None, ALU.add).then_inc(s_var, 1)
            dve.wait_ge(s_sd, 1)
            v.link(nc.vector.reciprocal(lnsd[:, 0, :], lnsd[:, 1, :]))
            for t in range(NT):
                o, i = dst[:, t, :], src[:, t, :]
                if interleave:
                    o = o.rearrange("p (a j) -> p j a", a=2)
                    i = i.rearrange("p (j a) -> p j a", a=2)
                nc.vector.tensor_scalar(o, i, lnmv[:, t, 0:1], lnsd[:, 0, t:t + 1],
                                        ALU.subtract, ALU.mult).then_inc(s_h, 1)

        def norm_on_scalar(act, s_var, s_sd):
            act.wait_ge(s_var, 1)
            nc.scalar.activation(lnsd[:, 1, :], lnsd[:, 0, :], ACT.Sqrt).then_inc(s_sd, 1)

        def turn_on_tensor(pe, src, bank0, s_src, src_at, s_turned, flat=False, dst_psum=None, idn=None):
            pt = ps if dst_psum is None else dst_psum
            for i in range(NT // 2):
                for t in (2 * i, 2 * i + 1):
                    if s_src is not None:
                        pe.wait_ge(s_src, src_at(t))
                    for k in range(KD):
                        o = pt[:, bank0 + i, k * 2 * P + (t % 2) * P:k * 2 * P + (t % 2) * P + P]
                        last = nc.tensor.transpose(o, src[:, t, k * P:(k + 1) * P], (idn or ident)[:, :])
                last.then_inc(s_turned, 1)

        def turned(bank, pt=None):
            return (ps if pt is None else pt)[:, bank, 0:KD * 2 * P].rearrange("p (k n) -> p k n", k=KD)

        def setup():
            g8 = sb("g8", [P, 8])
            s_in, s_step = sem("su_in"), sem("su_step")
            with nc.Block("setup") as block:
                @block.sync
                def _(sp):
                    sp.dma_start(g8[:, 0:4], a["g_xattn"].partition_broadcast(P)).then_inc(s_in, 16)
                    sp.dma_start(g8[:, 4:8], a["g_ffn"].partition_broadcast(P)).then_inc(s_in, 16)
                    sp.dma_start(ctxT[:, :], a["ctxT"]).then_inc(s_in, 16)
                    sp.dma_start(x[:, :, :], a["x"].rearrange("b (h p) d -> p (b h) d", p=P)).then_inc(s_in, 16)
                    sp.dma_start(ident[:, :], a["ident"]).then_inc(s_in, 16)
                    sp.dma_start(iota[:, :], a["iota"].partition_broadcast(P)).then_inc(s_in, 16)

                @block.scalar
                def _(act):
                    act.wait_ge(s_in, 96)
                    nc.scalar.activation(tg[:, :], g8[:, :], ACT.Tanh)

                @block.vector
                def _(dve):
                    dve.wait_ge(s_in, 96)
                    nc.vector.tensor_copy(identb[:, :], ident[:, :])

        NHC = 2048 // P
        WG, WU, WD = (regA[:, i * 4096:(i + 1) * 4096] for i in range(3))
        raw = [regB[:, i * 2048:(i + 1) * 2048].bitcast(I32) for i in range(3)]
        scl = [regB[:, (3 + i) * 2048:(4 + i) * 2048] for i in range(3)]
        WDv = WD.rearrange("p (c a n) -> p c a n", c=NHC // 2, a=2)

        def load_packed(sp, s_pk):
            for i, nm in enumerate(("gate", "up", "down")):
                sp.dma_start(raw[i], a[f"L0_{nm}_pk"]).then_inc(s_pk[i], 16)
                for g in range(8):
                    sp.dma_start(scl[i][16 * g:16 * g + 16, :],
                                 a[f"L0_{nm}_sc"][g, :].partition_broadcast(16)).then_inc(s_pk[i], 16)

        def dequant_on_vector(dve, v, dq, s_pk, s_nib, s_dq):
            val, mag, tmp = dq
            for i in range(3):
                dve.wait_ge(s_pk[i], 16 * 9)
                lo16 = raw[i].bitcast(U16).rearrange("p (n two) -> p n two", two=2)[:, :, 0]
                for par in range(2):
                    n = 2 * i + par
                    if n >= 2:
                        dve.wait_ge(s_dq, n - 1)
                    o = val[:, par, :]
                    v.mark(nc.vector.tensor_scalar(mag, lo16, 4 * par, 7, ALU.logical_shift_right, ALU.bitwise_and))
                    v.link(nc.vector.tensor_scalar(o, lo16, 8 << (4 * par), 12 - 4 * par,
                                                   ALU.bitwise_and, ALU.logical_shift_left))
                    v.link(nc.vector.tensor_scalar(tmp, mag, 64.0, float(0x3F00), ALU.mult, ALU.add))
                    v.link(nc.vector.scalar_tensor_tensor(tmp, mag, float(0x3F00), tmp, ALU.mult, ALU.min))
                    nc.vector.tensor_tensor(o, o, tmp, ALU.bitwise_or).then_inc(s_nib, 1)

        def dequant_on_gpsimd(pool, dq, s_nib, s_dq):
            for i, w in enumerate((WG, WU, WD)):
                for par in range(2):
                    pool.wait_ge(s_nib, 2 * i + par + 1)
                    code = dq[0][:, par, :].bitcast(BF16)
                    if i < 2:
                        o, q, sc = w[:, par * 2048:(par + 1) * 2048], code, scl[i]
                    else:
                        o = WDv[:, :, par, :]
                        q = code.rearrange("p (c n) -> p c n", n=D)
                        sc = scl[i].rearrange("p (c n) -> p c n", n=D)
                    nc.gpsimd.tensor_tensor(o, q, sc, ALU.mult).then_inc(s_dq, 1)

        def stage0():
            ar = Arena(regC)
            qT, kT = ar.take([T]), ar.take([T])
            att, attT = ar.take([NT, D]), ar.take([KD, T])
            w = ar.take([2, C])
            bqk = ar.take([2])
            nmx, den = ar.take([NT]), ar.take([NT])
            dq = [ar.take([2, 4 * HALF], U16), ar.take([4 * HALF], U16), ar.take([4 * HALF], U16)]
            s_w = sem("s0_w")
            s_var, s_sd, s_h = sem("s0_var"), sem("s0_sd"), sem("s0_h")
            s_proj, s_qk, s_en, s_mx = sem("s0_proj"), sem("s0_qk"), sem("s0_en"), sem("s0_mx")
            s_exp, s_att, s_hTp, s_hT = sem("s0_exp"), sem("s0_att"), sem("s0_hTp"), sem("s0_hT")
            s_pk, s_nib, s_dq = [sem(f"s0_pk{i}") for i in range(3)], sem("s0_nib"), sem("s0_dq")
            s_aTp, s_aT, s_mix, s_v = sem("s0_aTp"), sem("s0_aT"), sem("s0_mix"), sem("s0_v")
            with nc.Block("stage0") as block:
                @block.sync
                def _(sp):
                    sp.dma_start(w, a["L0_qkT"]).then_inc(s_w, 16)
                    sp.dma_start(bqk, a["L0_bqk"]).then_inc(s_w, 16)
                    load_packed(sp, s_pk)

                @block.scalar
                def _(act):
                    for i, dst in enumerate((qT, kT)):
                        for hf in range(2):
                            act.wait_ge(s_proj, 2 * i + hf + 1)
                            nc.scalar.activation(dst[:, hf * HALF:(hf + 1) * HALF], ps[:, 2 * i + hf, :],
                                                 ACT.Identity, bias=bqk[:, i:i + 1]).then_inc(s_qk, 1)
                    norm_on_scalar(act, s_var, s_sd)
                    for t in range(NT):
                        act.wait_ge(s_mx, t // 2 + 1)
                        nc.scalar.activation(att[:, t, :], ps[:, 4 + t // 2, (t % 2) * S:(t % 2 + 1) * S], ACT.Exp,
                                             bias=nmx[:, t:t + 1], accum_out=den[:, t:t + 1]).then_inc(s_exp, 1)
                    for i in range(NT // 2):
                        act.wait_ge(s_hTp, i + 1)
                        nc.scalar.copy(hT[:, :, i * 2 * P:(i + 1) * 2 * P], turned(i)).then_inc(s_hT, 1)

                @block.tensor
                def _(pe):
                    pe.wait_ge(s_w, 32)
                    for i in range(2):
                        for hf in range(2):
                            nc.tensor.matmul(ps[:, 2 * i + hf, :], w[:, i, :], ctxT[:, hf * HALF:(hf + 1) * HALF],
                                             start=True, stop=True).then_inc(s_proj, 1)
                    pe.wait_ge(s_qk, 4)
                    for t in range(NT):
                        b = t // 2
                        e = nc.tensor.matmul(ps[:, 4 + b, (t % 2) * S:(t % 2 + 1) * S], qT[:, t * P:(t + 1) * P],
                                             kT[:, b * S:(b + 1) * S], start=True, stop=True)
                        if t % 2:
                            e.then_inc(s_en, 1)
                    turn_on_tensor(pe, h, 0, s_h, lambda t: t + 1, s_hTp)
                    pe.wait_ge(s_exp, NT)
                    turn_on_tensor(pe, att, 4, s_att, lambda t: t + 1, s_aTp)
                    pe.wait_ge(s_hT, NT // 2)
                    for t in range(NT):
                        b = t // 2
                        pe.wait_ge(s_aT, b + 1)
                        for k in range(KD):
                            m = nc.tensor.matmul(ps[:, b, (t % 2) * S:(t % 2 + 1) * S], hT[:, k, t * P:(t + 1) * P],
                                                 attT[:, k, b * S:(b + 1) * S], start=k == 0, stop=k == KD - 1)
                        if t % 2:
                            m.then_inc(s_mix, 1)

                @block.vector
                def _(dve):
                    v = Steps(dve, s_v)
                    norm_on_vector(dve, v, s_var, s_sd, s_h)
                    for b in range(B):
                        dve.wait_ge(s_en, b + 1)
                        nc.vector.tensor_reduce(nmx[:, 2 * b:2 * b + 2], ps[:, 4 + b, :].rearrange("p (t m) -> p t m", t=2),
                                                AX.X, ALU.max, negate=True).then_inc(s_mx, 1)
                    for t in range(NT):
                        dve.wait_ge(s_exp, t + 1)
                        v.link(nc.vector.reciprocal(den[:, t:t + 1], den[:, t:t + 1]))
                        nc.vector.tensor_scalar(att[:, t, :], att[:, t, :], den[:, t:t + 1], None,
                                                ALU.mult).then_inc(s_att, 1)
                    for i in range(NT // 2):
                        dve.wait_ge(s_aTp, i + 1)
                        nc.vector.tensor_copy(attT[:, :, i * 2 * P:(i + 1) * 2 * P], turned(4 + i)).then_inc(s_aT, 1)
                    for b in range(B):
                        dve.wait_ge(s_mix, b + 1)
                        xb = x[:, 2 * b:2 * b + 2, :]
                        nc.vector.scalar_tensor_tensor(xb, ps[:, b, :].rearrange("p (t m) -> p t m", t=2),
                                                       tg[:, 0:1], xb, ALU.mult, ALU.add)
                    dequant_on_vector(dve, v, dq, s_pk, s_nib, s_dq)

                @block.gpsimd
                def _(pool):
                    dequant_on_gpsimd(pool, dq, s_nib, s_dq)

        def stage1():
            ar = Arena(regC)
            gel = ar.take([2, HALF])
            itm = ar.take([2, HALF])
            s_var, s_sd, s_h, s_hTp, s_hT = (sem("s1_" + n) for n in ("var", "sd", "h", "hTp", "hT"))
            s_gu, s_gel, s_itm, s_down, s_acc, s_v = (sem("s1_" + n) for n in ("gu", "gel", "itm", "down", "acc", "v"))
            s_x = sem("s1_x")
            NU = 2 * NHC
            with nc.Block("stage1") as block:
                @block.scalar
                def _(act):
                    norm_on_scalar(act, s_var, s_sd)
                    for i in range(NT // 2):
                        act.wait_ge(s_hTp, i + 1)
                        nc.scalar.copy(hT[:, :, i * 2 * P:(i + 1) * 2 * P], turned(4 + i)).then_inc(s_hT, 1)
                    for u in range(NU):
                        act.wait_ge(s_gu, u + 1)
                        if u >= 2:
                            act.wait_ge(s_itm, u - 1)
                        nc.scalar.activation(gel[:, u % 2, :], ps[:, 4 + 2 * (u % 2), :],
                                             ACT.Gelu_apprx_tanh).then_inc(s_gel, 1)

                @block.tensor
                def _(pe):
                    turn_on_tensor(pe, h, 4, s_h, lambda t: t + 1, s_hTp)

                    def gate_up(u):
                        hf, c = divmod(u, NHC)
                        if u < 2:
                            pe.wait_ge(s_hT, NT // 2)
                        else:
                            pe.wait_ge(s_itm, u - 1)
                        for j, w in enumerate((WG, WU)):
                            for k in range(2):
                                m = nc.tensor.matmul(ps[:, 4 + 2 * (u % 2) + j, :],
                                                     w[:, k * 2048 + c * P:k * 2048 + (c + 1) * P],
                                                     hT[:, k, hf * HALF:(hf + 1) * HALF], start=k == 0, stop=k == 1)
                        m.then_inc(s_gu, 1)

                    def down(u):
                        hf, c = divmod(u, NHC)
                        pe.wait_ge(s_itm, u + 1)
                        for t in range(TPH):
                            m = nc.tensor.matmul(ps[:, 2 * hf + t // 2, (t % 2) * D:(t % 2 + 1) * D],
                                                 itm[:, u % 2, t * P:(t + 1) * P], WDv[:, c // 2, c % 2, :],
                                                 start=(c == 0 and t % 2 == 0), stop=c == NHC - 1,
                                                 skip_group_check=True)
                        m.then_inc(s_down, 1)

                    gate_up(0)
                    for u in range(NU):
                        if u + 1 < NU:
                            gate_up(u + 1)
                        down(u)

                @block.vector
                def _(dve):
                    v = Steps(dve, s_v)
                    norm_on_vector(dve, v, s_var, s_sd, s_h, interleave=True)

                    def add_half(hf):
                        dve.wait_ge(s_down, NHC * (hf + 1))
                        for i in range(2):
                            xv = x[:, hf * TPH + 2 * i:hf * TPH + 2 * i + 2, :]
                            nc.vector.scalar_tensor_tensor(xv, ps[:, 2 * hf + i, :].rearrange("p (t n) -> p t n", t=2),
                                                           tg[:, 4:5], xv, ALU.mult, ALU.add)

                    for u in range(NU):
                        dve.wait_ge(s_gel, u + 1)
                        if u >= 2:
                            dve.wait_ge(s_down, u - 1)
                        nc.vector.tensor_tensor(itm[:, u % 2, :], gel[:, u % 2, :], ps[:, 5 + 2 * (u % 2), :],
                                                ALU.mult).then_inc(s_itm, 1)
                        if u == NHC + 1:
                            add_half(0)
                    add_half(1)

        QEPS, QMAX = 1e-6, 127.0

        def stage2():
            ar = Arena(regA, regC)
            fsT = ar.take([KD, T])
            xs, ws = ar.take([KD, T]), ar.take([KD, T])
            q1f, qbf = ar.take([2 * T * KD]), ar.take([2 * T * KD], BF16)
            four = lambda v, n: v.rearrange("p (j t n) -> p j t n", j=2, n=n)
            q1, qb = four(q1f, D), four(qbf, D)
            xqT, wqT = ar.take([KD, T], BF16), ar.take([KD, T], BF16)
            rows = ar.take([2, T])
            am = ar.take([4, NT])
            tok = ar.take([2, 3, NT])
            am2 = ar.take([4, B])
            tok2 = ar.take([2, 3, NT])
            gu = ar.take([B, 2, S])
            sil = ar.take([B, S])
            res = gu.rearrange("p b g s -> p (b g s)")
            aT = ar.take([T])
            as2, wd2 = ar.take([T]), ar.take([T])
            q2, q2b = four(q1f[:, 0:2 * T], P), four(qbf[:, 0:2 * T], P)
            aqT, dqT = ar.take([T], BF16), ar.take([T], BF16)
            (s_var, s_sd, s_h, s_hTp, s_hT, s_fs, s_v, s_am, s_s, s_xs, s_xsP, s_q, s_qP, s_qT, s_mm, s_rowP, s_row,
             s_gus, s_sil, s_am2, s_s2, s_as, s_asP, s_q2, s_q2P, s_q2T, s_mm2, s_row2P, s_row2, s_tokx, s_tokw) = (
                sem("s2_" + n) for n in ("var sd h hTp hT fs v am s xs xsP q qP qT mm rowP row gus sil am2 s2 as asP q2 "
                                         "q2P q2T mm2 row2P row2 tokx tokw").split())

            def tiles(v, n):
                return v.rearrange("p (t n) -> p t n", n=n)

            with nc.Block("stage2") as block:
                @block.sync
                def _(sp):
                    sp.dma_start(fsT, a["fsT"]).then_inc(s_fs, 16)
                    load_w3(sp)

                @block.scalar
                def _(act):
                    norm_on_scalar(act, s_var, s_sd)
                    act.wait_ge(s_am, 1)
                    nc.scalar.activation(am[:, 3, :], am[:, 2, :], ACT.Sqrt).then_inc(s_s, 1)
                    for j, dst in enumerate((xqT, wqT)):
                        for i in range(4):
                            act.wait_ge(s_qP, 4 * j + i + 1)
                            nc.scalar.copy(dst[:, :, i * 2 * P:(i + 1) * 2 * P], turned(4 * j + i, psb)).then_inc(s_qT, 1)
                    act.wait_ge(s_rowP, 1)
                    nc.scalar.copy(rows[:, 0, :], ps[:, 4:6, :].rearrange("p b n -> p (b n)")).then_inc(s_row, 1)
                    act.wait_ge(s_gus, 1)
                    nc.scalar.activation(sil, gu[:, :, 0, :], ACT.Silu).then_inc(s_sil, 1)
                    act.wait_ge(s_am2, 1)
                    nc.scalar.activation(am2[:, 3, :], am2[:, 2, :], ACT.Sqrt).then_inc(s_s2, 1)
                    for j, dst in enumerate((aqT, dqT)):
                        act.wait_ge(s_q2P, j + 1)
                        nc.scalar.copy(dst, psb[:, 4 + j, 0:T]).then_inc(s_q2T, 1)
                    act.wait_ge(s_row2P, 1)
                    nc.scalar.copy(rows[:, 1, :], ps[:, 6:8, :].rearrange("p b n -> p (b n)")).then_inc(s_row2, 1)

                @block.tensor
                def _(pe):
                    turn_on_tensor(pe, h, 0, s_h, lambda t: t + 1, s_hTp)

                    def turn_back(src, bank0, sem_src, at):
                        pe.wait_ge(sem_src, at)
                        for t in range(NT):
                            for k in range(KD):
                                m = nc.tensor.transpose(ps[:, bank0 + t // 2, (t % 2) * D + k * P:(t % 2) * D + (k + 1) * P],
                                                        src[:, k, t * P:(t + 1) * P], ident[:, :])
                        m.then_inc(s_xsP, 1)

                    pe.wait_ge(s_hT, 4)
                    turn_back(xs, 0, s_xs, 1)
                    turn_back(ws, 4, s_xs, 2)
                    for j in range(2):
                        pe.wait_ge(s_q, j + 1)
                        turn_on_tensor(pe, qb[:, j], 4 * j, None, None, s_qP, dst_psum=psb, idn=identb)
                    pe.wait_ge(s_tokx, 1)
                    pe.wait_ge(s_qT, 8)
                    for t in range(NT):
                        m = nc.tensor.matmul(ps[:, 4 + t // 4, (t % 4) * P:(t % 4 + 1) * P],
                                             tok[:, 0, 1, t:t + 1].broadcast_to([P, P]), ident[:, :],
                                             start=True, stop=True)
                    m.then_inc(s_rowP, 1)
                    for b in range(B):
                        for o in range(2):
                            for k in range(KD):
                                m = nc.tensor.matmul(ps[:, b, o * S:(o + 1) * S],
                                                     wqT[:, k, (2 * b + o) * P:(2 * b + o + 1) * P],
                                                     xqT[:, k, b * S:(b + 1) * S], start=k == 0, stop=k == KD - 1)
                        m.then_inc(s_mm, 1)
                    pe.wait_ge(s_gus, 1)
                    for j, src in enumerate((as2, wd2)):
                        pe.wait_ge(s_as, j + 1)
                        for t in range(NT):
                            m = nc.tensor.transpose(ps[:, 2 * j + t // 4, (t % 4) * P:(t % 4 + 1) * P],
                                                    src[:, t * P:(t + 1) * P], ident[:, :])
                        m.then_inc(s_asP, 1)
                    pe.wait_ge(s_row, 1)
                    for j in range(2):
                        pe.wait_ge(s_q2, j + 1)
                        for t in range(NT):
                            m = nc.tensor.transpose(psb[:, 4 + j, t * P:(t + 1) * P], q2b[:, j, t, :], identb[:, :])
                        m.then_inc(s_q2P, 1)
                    pe.wait_ge(s_tokw, 1)
                    for t in range(NT):
                        m = nc.tensor.matmul(ps[:, 6 + t // 4, (t % 4) * P:(t % 4 + 1) * P],
                                             tok2[:, 1, 1, t:t + 1].broadcast_to([P, P]), ident[:, :],
                                             start=True, stop=True)
                    m.then_inc(s_row2P, 1)
                    pe.wait_ge(s_q2T, 2)
                    for t in range(NT):
                        b = t // 2
                        m = nc.tensor.matmul(ps[:, b, (t % 2) * D:(t % 2 + 1) * D], aqT[:, t * P:(t + 1) * P],
                                             dqT[:, b * S:(b + 1) * S], start=True, stop=True)
                        if t % 2:
                            m.then_inc(s_mm2, 1)

                @block.vector
                def _(dve):
                    v = Steps(dve, s_v)
                    norm_on_vector(dve, v, s_var, s_sd, s_h)
                    for i in range(4):
                        dve.wait_ge(s_hTp, i + 1)
                        nc.vector.tensor_copy(hT[:, :, i * 2 * P:(i + 1) * 2 * P], turned(i)).then_inc(s_hT, 1)

                    def channel_scales(m, s_ready, s_root):
                        v.link(nc.vector.tensor_scalar(m[:, 0:2, :], m[:, 0:2, :], QEPS, None, ALU.max))
                        v.link(nc.vector.reciprocal(m[:, 1, :], m[:, 1, :]))
                        nc.vector.tensor_tensor(m[:, 2, :], m[:, 0, :], m[:, 1, :], ALU.mult).then_inc(s_ready, 1)
                        dve.wait_ge(s_root, 1)
                        v.link(nc.vector.tensor_scalar(m[:, 2, :], m[:, 3, :], QEPS, None, ALU.max))
                        v.link(nc.vector.reciprocal(m[:, 0, :], m[:, 2, :]))

                    def row_scales(tk, amax_src, s_ready=None):
                        v.link(nc.vector.tensor_reduce(tk[:, 0, :], amax_src, AX.X, ALU.max, apply_absolute_value=True))
                        v.link(nc.vector.tensor_scalar(tk[:, 1, :], tk[:, 0, :], QEPS, 1.0 / QMAX, ALU.max, ALU.mult))
                        ins = nc.vector.reciprocal(tk[:, 2, :], tk[:, 1, :])
                        v.link(ins)
                        if s_ready is not None:
                            nc.vector.tensor_copy(tk[:, 0, :], tk[:, 1, :]).then_inc(s_ready, 1)

                    def round_rows(src, n, tk, q, qb_, s_done):
                        for t in range(NT):
                            v.mark(nc.vector.tensor_scalar(q[:, t, :], src[:, t, :], tk[:, 2, t:t + 1], QMAX,
                                                           ALU.mult, ALU.min))
                        v.settle()
                        v.link(nc.vector.tensor_scalar(q, q, -QMAX, ROUND, ALU.max, ALU.add))
                        nc.vector.tensor_scalar(qb_, q, -ROUND, None, ALU.add).then_inc(s_done, 1)

                    segs = lambda w: w.rearrange("p k (b n) -> p (k b) n", b=B)
                    dve.wait_ge(s_fs, 16)
                    v.mark(nc.vector.tensor_reduce(am[:, 1, :], segs(fsT), AX.X, ALU.max, apply_absolute_value=True))
                    dve.wait_ge(s_hT, 4)
                    v.link(nc.vector.tensor_reduce(am[:, 0, :], segs(hT[:, :, :]), AX.X, ALU.max,
                                                   apply_absolute_value=True))
                    channel_scales(am, s_am, s_s)
                    nc.vector.tensor_tensor(segs(xs), segs(hT[:, :, :]), am[:, 0, :].unsqueeze(2).broadcast_to([P, NT, S]),
                                            ALU.mult).then_inc(s_xs, 1)
                    nc.vector.tensor_tensor(segs(ws), segs(fsT), am[:, 2, :].unsqueeze(2).broadcast_to([P, NT, S]),
                                            ALU.mult).then_inc(s_xs, 1)
                    for j in range(2):
                        dve.wait_ge(s_xsP, j + 1)
                        src = ps[:, 4 * j:4 * j + 4, :].rearrange("p b (t n) -> p (b t) n", t=2)
                        row_scales(tok[:, j], src, s_tokx if j == 0 else None)
                        round_rows(src, D, tok[:, j], q1[:, j], qb[:, j], s_q)
                    dve.wait_ge(s_row, 1)
                    for b in range(B):
                        dve.wait_ge(s_mm, b + 1)
                        for o in range(2):
                            v.mark(nc.vector.scalar_tensor_tensor(
                                gu[:, b, o, :], ps[:, b, o * S:(o + 1) * S], tok[:, 1, 1, 2 * b + o:2 * b + o + 1],
                                rows[:, 0, b * S:(b + 1) * S], ALU.mult, ALU.mult))
                    v.settle()
                    v.link(nc.vector.tensor_reduce(am2[:, 1, :], tiles(ctxT[:, :], S), AX.X, ALU.max,
                                                   apply_absolute_value=True))
                    v.settle()
                    dve.sem_inc(s_gus, 1)
                    dve.wait_ge(s_sil, 1)
                    v.link(nc.vector.tensor_tensor(tiles(aT, S), sil, gu[:, :, 1, :], ALU.mult))
                    v.link(nc.vector.tensor_reduce(am2[:, 0, :], tiles(aT, S), AX.X, ALU.max, apply_absolute_value=True))
                    channel_scales(am2, s_am2, s_s2)
                    nc.vector.tensor_tensor(tiles(as2, S), tiles(aT, S), am2[:, 0, :].unsqueeze(2).broadcast_to([P, B, S]),
                                            ALU.mult).then_inc(s_as, 1)
                    nc.vector.tensor_tensor(tiles(wd2, S), tiles(ctxT[:, :], S),
                                            am2[:, 2, :].unsqueeze(2).broadcast_to([P, B, S]), ALU.mult).then_inc(s_as, 1)
                    for j in range(2):
                        dve.wait_ge(s_asP, j + 1)
                        src = ps[:, 2 * j:2 * j + 2, :].rearrange("p b (t n) -> p (b t) n", t=4)
                        row_scales(tok2[:, j], src, s_tokw if j == 1 else None)
                        round_rows(src, P, tok2[:, j], q2[:, j], q2b[:, j], s_q2)
                    dve.wait_ge(s_row2, 1)
                    for b in range(B):
                        dve.wait_ge(s_mm2, b + 1)
                        for o in range(2):
                            t = 2 * b + o
                            v.mark(nc.vector.scalar_tensor_tensor(
                                res[:, t * D:(t + 1) * D], ps[:, b, o * D:(o + 1) * D], tok2[:, 0, 1, t:t + 1],
                                rows[:, 1, b * S:(b + 1) * S], ALU.mult, ALU.mult))
                        v.settle()
                        xb = x[:, 2 * b:2 * b + 2, :]
                        nc.vector.scalar_tensor_tensor(xb, tiles(res[:, 2 * b * D:2 * (b + 1) * D], D), tg[:, 1:2], xb,
                                                       ALU.mult, ALU.add)

        NST, DTR, TAPS = 16, 8, 4
        NBC = 2 * NST

        def ssm():
            ar = Arena(regC, regA, regB)
            LP = S + TAPS - 1
            xpad = ar.take([KD, B, LP])
            u, dt, du = ar.take([KD, T]), ar.take([KD, T]), ar.take([KD, T])
            sA, sB = ar.take([T]), ar.take([T])
            xpad2 = ar.take([KD, T])
            in_w = ar.take([KD * P])
            cw = ar.take([KD, TAPS + 3])
            alog = ar.take([KD, NST])
            xp_w = ar.take([KD, 3 * NBC + DTR])
            dt_w = ar.take([D])
            dtl = ar.take([T])
            bcf = ar.take([T])
            bc1, bc2 = ar.take([T], BF16), ar.take([T], BF16)
            bcs = ar.take([T], BF16)
            self_, selb = ar.take([NBC]), ar.take([NBC], BF16)
            dA = ar.take([2, B, S])
            dBu, hs, hc = ar.take([2, T]), ar.take([2, T]), ar.take([2, T])
            (s_w, s_xi, s_xc, s_u, s_xp, s_dt, s_e, s_v, s_bcs, s_bc, s_dA, s_A, s_hc, s_y, s_dbu, s_z, s_fr, s_hcp) = (
                sem("m_" + n) for n in ("w xi xc u xp dt e v bcs bc dA A hc y dbu z fr hcp").split())
            NU = NST * KD
            with nc.Block("ssm") as block:
                @block.sync
                def _(sp):
                    for dst, nm in ((in_w, "m_in"), (cw, "m_cw"), (alog, "m_alog"), (xp_w, "m_xp"),
                                    (dt_w[3 * NBC:3 * NBC + DTR, :], "m_dtw"), (self_[0:3 * NBC, :], "m_sel")):
                        sp.dma_start(dst, a[nm]).then_inc(s_w, 16)

                @block.scalar
                def _(act):
                    act.wait_ge(s_w, 96)
                    nc.scalar.activation(alog, alog, ACT.Exp).then_inc(s_A, 1)
                    for i in range(4):
                        k, hf = divmod(i, 2)
                        act.wait_ge(s_xi, i + 1)
                        nc.scalar.copy(xpad[:, k, 2 * hf:2 * hf + 2, TAPS - 1:LP],
                                       ps[:, i, :].rearrange("p (b l) -> p b l", b=2)).then_inc(s_xc, 1)
                    for k in range(KD):
                        act.wait_ge(s_u, k + 1)
                        nc.scalar.activation(u[:, k, :], u[:, k, :], ACT.Silu).then_inc(s_z, 1)
                    for k in range(KD):
                        if k == 0:
                            act.wait_ge(s_xp, 2)
                        nc.scalar.activation(sA if k == 0 else sB, ps[:, 2 * k:2 * k + 2, :].rearrange("p b n -> p (b n)"),
                                             ACT.Abs, bias=cw[:, k, TAPS + 1:TAPS + 2]).then_inc(s_e, 1)
                        act.wait_ge(s_e, k + 1)
                        nc.scalar.activation(dt[:, k, :], sA if k == 0 else sB, ACT.Exp, scale=-1.0).then_inc(s_dt, 1)
                    act.wait_ge(s_fr, 1)
                    for i in range(NU):
                        n, k = divmod(i, KD)
                        if i >= 2:
                            act.wait_ge(s_hc, i - 1)
                        nc.scalar.activation(dA[:, i % 2, :, 1:S], dt[:, k, :].rearrange("p (b l) -> p b l", b=B)[:, :, 1:S],
                                             ACT.Exp, scale=alog[:, k, n:n + 1]).then_inc(s_dA, 1)

                @block.tensor
                def _(pe):
                    pe.wait_ge(s_w, 96)
                    for i in range(4):
                        k, hf = divmod(i, 2)
                        nc.tensor.matmul(ps[:, i, :], in_w[:, k * P:(k + 1) * P], ctxT[:, hf * HALF:(hf + 1) * HALF],
                                         start=True, stop=True).then_inc(s_xi, 1)
                    pe.wait_ge(s_z, 2)
                    for hf in range(2):
                        for k in range(KD):
                            m = nc.tensor.matmul(ps[0:3 * NBC + DTR, 4 + hf, :], xp_w[:, k, :],
                                                 u[:, k, hf * HALF:(hf + 1) * HALF], start=k == 0, stop=k == KD - 1)
                    m.then_inc(s_xp, 1)
                    pe.wait_ge(s_bcs, 1)
                    dtr = slice(3 * NBC, 3 * NBC + DTR)
                    for k in range(KD):
                        for hf in range(2):
                            m = nc.tensor.matmul(ps[:, 2 * k + hf, :], dt_w[dtr, k * P:(k + 1) * P],
                                                 dtl[dtr, hf * HALF:(hf + 1) * HALF], start=True, stop=True)
                    m.then_inc(s_xp, 1)
                    pe.wait_ge(s_fr, 1)
                    for n in range(NST):
                        if n >= 2:
                            pe.wait_ge(s_hc, 2 * (n - 1))
                        for j in range(2):
                            for hf in range(2):
                                r = j * NST + n
                                m = nc.tensor.matmul(ps[:, 4 * (n % 2) + 2 * j + hf, :], selb[0:3 * NBC, r:r + 1].broadcast_to([3 * NBC, P]),
                                                     bcs[0:3 * NBC, hf * HALF:(hf + 1) * HALF], start=True, stop=True)
                        m.then_inc(s_bc, 1)

                @block.vector
                def _(dve):
                    v = Steps(dve, s_v)
                    v.mark(nc.vector.memset(xpad[:, :, :, 0:TAPS - 1], 0.0))
                    v.mark(nc.vector.memset(dA[:, :, :, 0:1], 0.0))
                    dve.wait_ge(s_w, 96)
                    dve.wait_ge(s_A, 1)
                    v.mark(nc.vector.tensor_copy(selb[0:3 * NBC, :], self_[0:3 * NBC, :]))
                    v.link(nc.vector.tensor_scalar(alog, alog, -1.0, None, ALU.mult))
                    for k in range(KD):
                        dve.wait_ge(s_xc, 2 * k + 2)
                        o = u[:, k, :].rearrange("p (b l) -> p b l", b=B)
                        v.link(nc.vector.tensor_scalar(o, xpad[:, k, :, TAPS - 1:LP], cw[:, k, TAPS - 1:TAPS],
                                                       cw[:, k, TAPS:TAPS + 1], ALU.mult, ALU.add))
                        for q in range(TAPS - 1):
                            ins = nc.vector.scalar_tensor_tensor(o, xpad[:, k, :, q:q + S], cw[:, k, q:q + 1], o,
                                                                 ALU.mult, ALU.add)
                            if q < TAPS - 2:
                                v.link(ins)
                        ins.then_inc(s_u, 1)
                    dve.wait_ge(s_xp, 1)
                    R = 3 * NBC
                    proj = ps[:, 4:6, :].rearrange("p b n -> p (b n)")
                    v.mark(nc.vector.tensor_copy(dtl[R:R + DTR, :], proj[R:R + DTR, :]))
                    v.link(nc.vector.tensor_copy(bc1[0:R, :], proj[0:R, :]))
                    v.link(nc.vector.tensor_tensor(bcf[0:R, :], proj[0:R, :], bc1[0:R, :], ALU.subtract))
                    v.link(nc.vector.tensor_copy(bc2[0:R, :], bcf[0:R, :]))
                    v.link(nc.vector.tensor_tensor(bcf[0:R, :], bcf[0:R, :], bc2[0:R, :], ALU.subtract))
                    v.mark(nc.vector.tensor_copy(bcs[0:NBC, :], bc1[0:NBC, :]))
                    v.mark(nc.vector.tensor_copy(bcs[NBC:2 * NBC, :], bc2[NBC:2 * NBC, :]))
                    v.mark(nc.vector.tensor_copy(bcs[2 * NBC:R, :], bcf[2 * NBC:R, :]))
                    v.settle()
                    dve.sem_inc(s_bcs, 1)
                    dve.wait_ge(s_xp, 2)
                    for k, w in ((0, sA), (1, sB)):
                        z = ps[:, 2 * k:2 * k + 2, :].rearrange("p b n -> p (b n)")
                        dve.wait_ge(s_e, k + 1)
                        bias = cw[:, k, TAPS + 1:TAPS + 2]
                        v.mark(nc.vector.tensor_scalar(xpad2[:, k, :], z, bias, 0.0, ALU.add, ALU.max))
                    for k, w in ((0, sA), (1, sB)):
                        dve.wait_ge(s_dt, k + 1)
                        e, q = dt[:, k, :], du[:, k, :]
                        v.link(nc.vector.tensor_scalar(w, e, 2.0, None, ALU.add))
                        v.link(nc.vector.reciprocal(q, w))
                        v.link(nc.vector.tensor_tensor(e, e, q, ALU.mult))
                        v.link(nc.vector.tensor_tensor(q, e, e, ALU.mult))
                        v.link(nc.vector.tensor_scalar(w, q, 2.0 / 17, 2.0 / 15, ALU.mult, ALU.add))
                        v.link(nc.vector.tensor_tensor(w, w, q, ALU.mult))
                        for c in (13, 11, 9, 7, 5, 3):
                            v.link(nc.vector.scalar_tensor_tensor(w, w, 2.0 / c, q, ALU.add, ALU.mult))
                        v.link(nc.vector.scalar_tensor_tensor(w, w, 2.0, e, ALU.add, ALU.mult))
                        v.link(nc.vector.tensor_tensor(e, w, xpad2[:, k, :], ALU.add))
                        v.link(nc.vector.tensor_tensor(q, e, u[:, k, :], ALU.mult))
                    dve.sem_inc(s_fr, 1)
                    for i in range(NU):
                        n, k = divmod(i, KD)
                        bank = 4 * (n % 2)
                        dve.wait_ge(s_bc, n + 1)
                        v.link(nc.vector.tensor_tensor(dBu[:, i % 2, :], du[:, k, :],
                                                       ps[:, bank:bank + 2, :].rearrange("p b n -> p (b n)"), ALU.mult))
                        dve.wait_ge(s_dA, i + 1)
                        v.link(nc.vector.tensor_tensor_scan(hs[:, i % 2, :], dA[:, i % 2].rearrange("p b l -> p (b l)"),
                                                            dBu[:, i % 2, :], 0.0, ALU.mult, ALU.add))
                        if i >= 2:
                            dve.wait_ge(s_y, i - 1)
                        nc.vector.tensor_tensor(hc[:, i % 2, :], hs[:, i % 2, :],
                                                ps[:, bank + 2:bank + 4, :].rearrange("p b n -> p (b n)"),
                                                ALU.mult).then_inc(s_hc, 1)
                    dve.wait_ge(s_y, NU)
                    for k in range(KD):
                        v.mark(nc.vector.scalar_tensor_tensor(yssm[:, k, :], u[:, k, :], cw[:, k, TAPS + 2:TAPS + 3],
                                                              yssm[:, k, :], ALU.mult, ALU.add))

                @block.gpsimd
                def _(pool):
                    for i in range(NU):
                        k = i % KD
                        pool.wait_ge(s_hc, i + 1)
                        if i < KD:
                            ins = nc.gpsimd.tensor_copy(yssm[:, k, :], hc[:, i % 2, :])
                        else:
                            if i >= 2:
                                pool.wait_ge(s_y, i - 1)
                            ins = nc.gpsimd.tensor_tensor(yssm[:, k, :], yssm[:, k, :], hc[:, i % 2, :], ALU.add)
                        ins.then_inc(s_y, 1)

        def stage6():
            ar = Arena(regC)
            sil, gated = ar.take([NT, D]), ar.take([NT, D])
            s_var, s_sd, s_h, s_sil, s_gt, s_gP, s_v = (sem("s6_" + n) for n in ("var sd h sil gt gP v").split())
            with nc.Block("stage6") as block:
                @block.scalar
                def _(act):
                    norm_on_scalar(act, s_var, s_sd)
                    for t in range(NT):
                        act.wait_ge(s_h, t + 1)
                        nc.scalar.activation(sil[:, t, :], h[:, t, :], ACT.Silu).then_inc(s_sil, 1)

                @block.tensor
                def _(pe):
                    for b in range(B):
                        pe.wait_ge(s_gt, 2 * b + 2)
                        for l in range(2):
                            for k in range(KD):
                                m = nc.tensor.transpose(ps[:, b, l * D + k * P:l * D + (k + 1) * P],
                                                        gated[:, 2 * b + k, l * P:(l + 1) * P], ident[:, :])
                        m.then_inc(s_gP, 1)

                @block.vector
                def _(dve):
                    v = Steps(dve, s_v)
                    norm_on_vector(dve, v, s_var, s_sd, s_h)
                    for b in range(B):
                        for k in range(KD):
                            t = 2 * b + k
                            dve.wait_ge(s_sil, t + 1)
                            nc.vector.tensor_tensor(gated[:, t, :], sil[:, t, :], yssm[:, k, b * S:(b + 1) * S],
                                                    ALU.mult).then_inc(s_gt, 1)
                    for b in range(B):
                        dve.wait_ge(s_gP, b + 1)
                        xb = x[:, 2 * b:2 * b + 2, :]
                        nc.vector.scalar_tensor_tensor(xb, ps[:, b, :].rearrange("p (t m) -> p t m", t=2),
                                                       tg[:, 3:4], xb, ALU.mult, ALU.add)

        def moe_views(reg, units):
            n = units * P
            gate, up = (reg[:, j * 2 * n:(j + 1) * 2 * n].rearrange("p (k c i) -> p k c i", k=KD, i=P) for j in range(2))
            return gate, up, reg[:, 4 * n:6 * n].rearrange("p (c n) -> p c n", n=D)

        s_w3, s_w7 = (ctx.enter_context(nc.semaphore(n)) for n in ("w3_loaded", "w7_loaded"))
        NE3, NE7, F7 = 16, 8, 176
        NC3, NC7 = NE3 + 1, NE7 * F7 // P
        W3, W7 = moe_views(regB, NC3), moe_views(regA, NC7)
        rt3, rt7 = sb("rt3", [P, KD, NE3]), sb("rt7", [P, KD, NE7])
        bias3 = sb("bias3", [P, NE3])
        sel7 = sb("sel7", [NE7, NC7 * P])

        def load_w3(sp):
            for dst, nm in zip((regB[:, 0:2 * NC3 * P], regB[:, 2 * NC3 * P:4 * NC3 * P], regB[:, 4 * NC3 * P:6 * NC3 * P]),
                               ("gate", "up", "down")):
                sp.dma_start(dst, a[f"L1_{nm}"]).then_inc(s_w3, 16)
            sp.dma_start(rt3[:, :, :], a["L1_router"]).then_inc(s_w3, 16)
            sp.dma_start(bias3[:, :], a["L1_bias"].partition_broadcast(P)).then_inc(s_w3, 16)

        def load_w7(sp):
            for dst, nm in zip((regA[:, 0:2 * NC7 * P], regA[:, 2 * NC7 * P:4 * NC7 * P], regA[:, 4 * NC7 * P:6 * NC7 * P]),
                               ("gate", "up", "down")):
                sp.dma_start(dst, a[f"L3_{nm}"]).then_inc(s_w7, 16)
            sp.dma_start(rt7[:, :, :], a["L3_router"]).then_inc(s_w7, 16)
            sp.dma_start(sel7[:, :], a["sel7"]).then_inc(s_w7, 16)

        def moe_stage(tag, E, NC, W, router, select, gate_col, s_weights, loads, load=None, shared=False,
                      bias=None, prefetch=None):
            ar = Arena(regC)
            gel, itm = ar.take([2, HALF]), ar.take([2, HALF])
            lg, ex, comb, hit = (ar.take([NT, E]) for _ in range(4))
            top, idx, idf, wk = ar.take([NT, 8]), ar.take([NT, 8], U32), ar.take([NT, 2]), ar.take([NT, 2])
            col = ar.take([3, NT])
            combT = ar.take([T])[0:E, :]
            wg, wu, wd = W
            (s_var, s_sd, s_h, s_hTp, s_hT, s_v, s_lg, s_ein, s_exp, s_comb, s_cTp, s_cT, s_gu, s_gel, s_itm, s_down,
             s_add) = (sem(f"{tag}_" + n) for n in ("var sd h hTp hT v lg ein exp comb cTp cT gu gel itm down add").split())
            NU = 2 * NC
            routed = lambda u: not (shared and u % NC == NC - 1)
            over = lambda v: v.unsqueeze(2).broadcast_to([P, NT, E])
            with nc.Block(tag) as block:
                @block.sync
                def _(sp):
                    if load is not None:
                        load(sp)
                    if prefetch is not None:
                        prefetch(sp)

                @block.scalar
                def _(act):
                    norm_on_scalar(act, s_var, s_sd)
                    for i in range(NT // 2):
                        act.wait_ge(s_hTp, i + 1)
                        nc.scalar.copy(hT[:, :, i * 2 * P:(i + 1) * 2 * P], turned(2 + i)).then_inc(s_hT, 1)
                    act.wait_ge(s_ein, 1)
                    if shared:
                        nc.scalar.activation(ex, lg, ACT.Exp).then_inc(s_exp, 1)
                    else:
                        nc.scalar.activation(col[:, 1, :], col[:, 0, :], ACT.Exp).then_inc(s_exp, 1)
                    act.wait_ge(s_cTp, 1)
                    nc.scalar.copy(combT, ps[0:E, 6:8, :].rearrange("p b n -> p (b n)")).then_inc(s_cT, 1)
                    for u in range(NU):
                        act.wait_ge(s_gu, u + 1)
                        if u >= 2:
                            act.wait_ge(s_itm, u - 1)
                        nc.scalar.activation(gel[:, u % 2, :], ps[:, 2 + 2 * (u % 2), :], ACT.Silu).then_inc(s_gel, 1)

                @block.tensor
                def _(pe):
                    turn_on_tensor(pe, h, 2, s_h, lambda t: t + 1, s_hTp)
                    pe.wait_ge(s_hT, NT // 2)
                    pe.wait_ge(s_weights, 16 * loads)
                    for t in range(NT):
                        for k in range(KD):
                            m = nc.tensor.matmul(ps[:, 6, t * E:(t + 1) * E], hT[:, k, t * P:(t + 1) * P],
                                                 router[:, k, :], start=k == 0, stop=k == KD - 1)
                    m.then_inc(s_lg, 1)
                    pe.wait_ge(s_comb, 1)
                    for t in range(NT):
                        m = nc.tensor.transpose(ps[0:E, 6 + t // 4, (t % 4) * P:(t % 4 + 1) * P], comb[:, t, :], ident[:, :])
                    m.then_inc(s_cTp, 1)
                    pe.wait_ge(s_cT, 1)

                    def gate_up(u):
                        hf, c = divmod(u, NC)
                        if u >= 2:
                            pe.wait_ge(s_itm, u - 1)
                        if routed(u):
                            m = nc.tensor.matmul(ps[:, 6 + u % 2, :], select(c), combT[:, hf * HALF:(hf + 1) * HALF],
                                                 start=True, stop=True)
                        for j, w in enumerate((wg, wu)):
                            for k in range(KD):
                                m = nc.tensor.matmul(ps[:, 2 + 2 * (u % 2) + j, :], w[:, k, c, :],
                                                     hT[:, k, hf * HALF:(hf + 1) * HALF], start=k == 0, stop=k == KD - 1)
                        m.then_inc(s_gu, 1)

                    def down(u):
                        hf, c = divmod(u, NC)
                        pe.wait_ge(s_itm, u + 1)
                        if u == NC:
                            pe.wait_ge(s_add, 1)
                        for t in range(TPH):
                            m = nc.tensor.matmul(ps[:, t // 2, (t % 2) * D:(t % 2 + 1) * D],
                                                 itm[:, u % 2, t * P:(t + 1) * P], wd[:, c, :],
                                                 start=(c == 0 and t % 2 == 0), stop=c == NC - 1, skip_group_check=True)
                        m.then_inc(s_down, 1)

                    gate_up(0)
                    for u in range(NU):
                        if u + 1 < NU:
                            gate_up(u + 1)
                        down(u)

                @block.vector
                def _(dve):
                    v = Steps(dve, s_v)
                    norm_on_vector(dve, v, s_var, s_sd, s_h)
                    dve.wait_ge(s_lg, 1)
                    psl = ps[:, 6, 0:NT * E].rearrange("p (t e) -> p t e", e=E)
                    if shared:
                        v.link(nc.vector.tensor_tensor(lg, psl, bias[:, :].unsqueeze(1).broadcast_to([P, NT, E]), ALU.add))
                        v.link(nc.vector.tensor_reduce(col[:, 0, :], lg, AX.X, ALU.max))
                        nc.vector.tensor_tensor(lg, lg, over(col[:, 0, :]), ALU.subtract).then_inc(s_ein, 1)
                        dve.wait_ge(s_exp, 1)
                        v.link(nc.vector.tensor_reduce(col[:, 1, :], ex, AX.X, ALU.add))
                        v.link(nc.vector.reciprocal(col[:, 2, :], col[:, 1, :]))
                        v.link(nc.vector.tensor_tensor(lg, ex, over(col[:, 2, :]), ALU.mult))
                    else:
                        v.link(nc.vector.tensor_copy(lg, psl))
                    for t in range(NT):
                        v.mark(nc.vector.max(top[:, t, :], lg[:, t, :]))
                    v.settle()
                    for t in range(NT):
                        v.mark(nc.vector.max_index(idx[:, t, :], top[:, t, :], lg[:, t, :]))
                    v.settle()
                    v.link(nc.vector.tensor_copy(idf, idx[:, :, 0:2]))
                    if shared:
                        v.link(nc.vector.tensor_reduce(col[:, 0, :], top[:, :, 0:2], AX.X, ALU.add))
                        v.link(nc.vector.tensor_scalar(col[:, 0, :], col[:, 0, :], 1e-9, None, ALU.add))
                        v.link(nc.vector.reciprocal(col[:, 1, :], col[:, 0, :]))
                        v.link(nc.vector.tensor_tensor(wk, top[:, :, 0:2], col[:, 1, :].unsqueeze(2).broadcast_to([P, NT, 2]),
                                                       ALU.mult))
                    else:
                        nc.vector.tensor_tensor(col[:, 0, :], top[:, :, 1], top[:, :, 0], ALU.subtract).then_inc(s_ein, 1)
                        dve.wait_ge(s_exp, 1)
                        v.link(nc.vector.tensor_scalar(col[:, 2, :], col[:, 1, :], 1.0, None, ALU.add))
                        v.link(nc.vector.reciprocal(wk[:, :, 0], col[:, 2, :]))
                        v.link(nc.vector.tensor_tensor(wk[:, :, 1], wk[:, :, 0], col[:, 1, :], ALU.mult))
                    it = iota[:, 0:E].unsqueeze(1).broadcast_to([P, NT, E])
                    for k, dst in ((0, comb), (1, hit)):
                        v.link(nc.vector.tensor_tensor(dst, it, over(idf[:, :, k]), ALU.is_equal))
                        v.link(nc.vector.tensor_tensor(dst, dst, over(wk[:, :, k]), ALU.mult))
                    nc.vector.tensor_tensor(comb, comb, hit, ALU.add).then_inc(s_comb, 1)

                    def add_half(hf):
                        dve.wait_ge(s_down, NC * (hf + 1))
                        for i in range(2):
                            xv = x[:, hf * TPH + 2 * i:hf * TPH + 2 * i + 2, :]
                            ins = nc.vector.scalar_tensor_tensor(xv, ps[:, i, :].rearrange("p (t n) -> p t n", t=2),
                                                                 tg[:, gate_col:gate_col + 1], xv, ALU.mult, ALU.add)
                        ins.then_inc(s_add, 1)

                    for u in range(NU):
                        dve.wait_ge(s_gel, u + 1)
                        if u >= 2:
                            dve.wait_ge(s_down, u - 1)
                        o = itm[:, u % 2, :]
                        first = nc.vector.tensor_tensor(o, gel[:, u % 2, :], ps[:, 3 + 2 * (u % 2), :], ALU.mult)
                        if routed(u):
                            v.link(first)
                            first = nc.vector.tensor_tensor(o, o, ps[:, 6 + u % 2, :], ALU.mult)
                        first.then_inc(s_itm, 1)
                        if u == NC - 1:
                            add_half(0)
                    add_half(1)

        def stage3():
            moe_stage("stage3", NE3, NC3, W3, rt3, lambda c: ident[0:NE3, c:c + 1].broadcast_to([NE3, P]), 5,
                      s_w3, 5, shared=True, bias=bias3, load=load_w3 if start == 3 else None)

        NH, HD, NDCA = 16, 16, 16
        HPAD = 2 * HD
        SCALE4, EPS4 = HD ** -0.5, 1e-6
        NMAIN = S - NDCA
        HPB = P // HPAD
        NBLK = NH // HPB
        VW = 2 * (HD + 1)

        def stage4():
            ar = Arena(regA, regB, regC)
            qpad, kpad = ar.take([NT, NH, HPAD]), ar.take([NT, NH, HPAD])
            q4T, k4T = ar.take([NBLK, T]), ar.take([NBLK, T])
            kv = ar.take([NT, 2 * D])
            q, t1 = ar.take([NT, D]), h
            vaug = ar.take([NT, NH, VW])
            prob = ar.take([4, 2 * S])
            wq, wkv, wdca, wo = ar.take([KD, D]), ar.take([2 * D]), ar.take([2 * D]), ar.take([KD, D])
            ctxm, ctxd = ar.take([B, P]), ar.take([B, P])
            bkv = ar.take([2, 2 * D])
            bq, bo = ar.take([D]), ar.take([D])
            qn, kn = ar.take([2, HD]), ar.take([2, 2, HD])
            mask = ar.take([2, 2])
            st = ar.take([4, NT * NH])
            rz = ar.take([2, 4, 2, 2])
            o = h
            part = ar.take([2, 4, 2, HD])
            (s_var, s_sd, s_h, s_hTp, s_hT, s_w, s_v, s_q, s_qe, s_kv, s_kve, s_qv, s_qs, s_sqi, s_sq, s_pad, s_padP, s_padT,
             s_s1, s_m1, s_s2, s_p, s_pv, s_o, s_oP, s_oT, s_fin, s_x, s_ctx, s_va) = (
                sem("s4_" + n) for n in ("var sd h hTp hT w v q qe kv kve qv qs sqi sq pad padP padT s1 m1 s2 p pv o oP oT out "
                                         "x ctx va").split())
            groups = lambda w: w.rearrange("p t (g d) -> p (t g) d", d=HD)
            kview = kv.rearrange("p t (g d) -> p (t g) d", d=HPAD)[:, :, 0:HD]
            wide = lambda c: st[:, c, :].unsqueeze(2).broadcast_to([P, NT * NH, HD])
            flat4 = lambda w: w.rearrange("p t g d -> p (t g) d")
            NG = NT * 2
            NHB = B * NH

            with nc.Block("stage4") as block:
                @block.sync
                def _(sp):
                    for dst, nm in ((wq, "q4_wq"), (wkv, "q4_wkv"), (wdca, "q4_wdca"), (wo, "q4_wo")):
                        sp.dma_start(dst, a[nm]).then_inc(s_w, 16)
                    row = lambda nm: a[nm].partition_broadcast(P)
                    sp.dma_start(bkv[:, 0, :], row("q4_bkv")).then_inc(s_w, 16)
                    sp.dma_start(bkv[0:NMAIN - P, 1, :], a["q4_bkv"].partition_broadcast(NMAIN - P)).then_inc(s_w, 16)
                    sp.dma_start(bkv[NMAIN - P:P, 1, :], a["q4_bdca"].partition_broadcast(NDCA)).then_inc(s_w, 16)
                    sp.dma_start(bq, row("q4_bq")).then_inc(s_w, 16)
                    sp.dma_start(bo, row("q4_bo")).then_inc(s_w, 16)
                    sp.dma_start(qn, row("q4_qn")).then_inc(s_w, 16)
                    sp.dma_start(kn[:, 0], row("q4_kn")).then_inc(s_w, 16)
                    sp.dma_start(kn[0:NMAIN - P, 1], a["q4_kn"].partition_broadcast(NMAIN - P)).then_inc(s_w, 16)
                    sp.dma_start(kn[NMAIN - P:P, 1], a["q4_kd"].partition_broadcast(NDCA)).then_inc(s_w, 16)
                    sp.dma_start(mask, a["q4_mask"]).then_inc(s_w, 16)

                @block.gpsimd
                def _(pool):
                    pool.wait_ge(s_w, 16 * 14)
                    c = ctxT[:, :].rearrange("p (b two n) -> p b two n", two=2, n=P)[:, :, 1, :]
                    nc.gpsimd.tensor_copy(ctxm[:, :, 0:NMAIN - P], c[:, :, 0:NMAIN - P]).then_inc(s_ctx, 1)
                    nc.gpsimd.memset(ctxm[:, :, NMAIN - P:P], 0.0).then_inc(s_ctx, 1)
                    nc.gpsimd.memset(ctxd[:, :, 0:NMAIN - P], 0.0).then_inc(s_ctx, 1)
                    nc.gpsimd.tensor_copy(ctxd[:, :, NMAIN - P:P], c[:, :, NMAIN - P:P]).then_inc(s_ctx, 1)
                    nc.gpsimd.memset(qpad[:, :, :, HD:HPAD], 0.0).then_inc(s_va, 1)
                    nc.gpsimd.memset(kpad[:, :, :, HD:HPAD], 0.0).then_inc(s_va, 1)
                    pool.wait_ge(s_va, 2)
                    for par in range(2):
                        for j in range(2):
                            nc.gpsimd.tensor_scalar(kpad[:, par::2, :, HD + j], kpad[:, par::2, :, HD + j],
                                                    mask[:, par, j:j + 1], None, ALU.add).then_inc(s_va, 1)
                    pool.wait_ge(s_kve, NT)
                    for t in range(NT):
                        for j in range(2):
                            mk = mask[:, t % 2, j:j + 1]
                            src = kv[:, t, :].rearrange("p (g d) -> p g d", d=HPAD)[:, :, HD:HPAD]
                            c0 = j * (HD + 1)
                            nc.gpsimd.tensor_scalar(vaug[:, t, :, c0:c0 + HD], src, mk, None, ALU.mult).then_inc(s_va, 1)
                    pool.wait_ge(s_va, 6 + 2 * NT)
                    for par in range(2):
                        for j in range(2):
                            c0 = j * (HD + 1) + HD
                            nc.gpsimd.tensor_copy(vaug[:, par::2, :, c0], kpad[:, par::2, :, HD + j]).then_inc(s_va, 1)

                @block.scalar
                def _(act):
                    norm_on_scalar(act, s_var, s_sd)
                    for i in range(NT // 2):
                        act.wait_ge(s_hTp, i + 1)
                        nc.scalar.copy(hT[:, :, i * 2 * P:(i + 1) * 2 * P], turned(4 + i)).then_inc(s_hT, 1)
                    for i in range(2):
                        act.wait_ge(s_sqi, i + 1)
                        nc.scalar.activation(groups(t1[:, :, :]), (kview, groups(q))[i], ACT.Square).then_inc(s_sq, 1)
                        act.wait_ge(s_qv, i + 1)
                        nc.scalar.activation(st[:, 1, :], st[:, 0, :], ACT.Sqrt).then_inc(s_qs, 1)
                    for i in range(3 * 8):
                        dst = (k4T, q4T, q4T)[i // 8]
                        if i % 2:
                            continue
                        act.wait_ge(s_padP, i + 2)
                        blk, _ = divmod(i % 8, 2)
                        nc.scalar.copy(dst[:, blk, :], ps[:, (i % 8):(i % 8) + 2, :].rearrange("p b n -> p (b n)")).then_inc(s_padT, 1)
                    for n in range(NHB):
                        act.wait_ge(s_s2, n + 1)
                        if n >= 4:
                            act.wait_ge(s_pv, n // 4)
                        nc.scalar.activation(prob[:, n % 4, :], ps[:, n % 6, :], ACT.Exp, scale=SCALE4).then_inc(s_p, 1)
                    for i in range(4):
                        act.wait_ge(s_oP, i + 1)
                        nc.scalar.copy(hT[:, :, i * 2 * P:(i + 1) * 2 * P], turned(i)).then_inc(s_oT, 1)

                @block.tensor
                def _(pe):
                    turn_on_tensor(pe, h, 4, s_h, lambda t: t + 1, s_hTp)
                    pe.wait_ge(s_w, 16 * 14)
                    pe.wait_ge(s_ctx, 4)
                    for t in range(NT):
                        if t >= 4:
                            pe.wait_ge(s_kve, t - 3)
                        b = t // 2
                        if t % 2 == 0:
                            m = nc.tensor.matmul(ps[:, t % 4, :], ctxT[:, t * P:(t + 1) * P], wkv, start=True, stop=True)
                        else:
                            nc.tensor.matmul(ps[:, t % 4, :], ctxm[:, b, :], wkv, start=True, stop=False)
                            m = nc.tensor.matmul(ps[:, t % 4, :], ctxd[:, b, :], wdca, start=False, stop=True)
                        m.then_inc(s_kv, 1)
                    pe.wait_ge(s_hT, 4)
                    for t in range(NT):
                        for k in range(KD):
                            m = nc.tensor.matmul(ps[:, 4 + t // 2, (t % 2) * D:(t % 2 + 1) * D], hT[:, k, t * P:(t + 1) * P],
                                                 wq[:, k, :], start=k == 0, stop=k == KD - 1)
                        if t % 2:
                            m.then_inc(s_q, 1)

                    def turn_heads(src, n):
                        for blk in range(NBLK):
                            for i in range(2):
                                if n == 1:
                                    pe.wait_ge(s_padT, blk + 1)
                                if n == 0 and blk >= 2:
                                    pe.wait_ge(s_qe, 4)
                                for t in range(4 * i, 4 * i + 4):
                                    m = nc.tensor.transpose(ps[:, 2 * blk + i, (t % 4) * P:(t % 4 + 1) * P],
                                                            src[:, t].rearrange("p g d -> p (g d)")[:, blk * P:(blk + 1) * P],
                                                            ident[:, :])
                                m.then_inc(s_padP, 1)

                    pe.wait_ge(s_va, 6)
                    pe.wait_ge(s_kve, NT)
                    pe.wait_ge(s_pad, 1)
                    turn_heads(kpad, 0)
                    pe.wait_ge(s_pad, 2)
                    turn_heads(qpad, 1)
                    for g in range(NG):
                        t, half = divmod(g, 2)
                        b = t // 2
                        pe.wait_ge(s_padT, 8)
                        if g >= 2:
                            pe.wait_ge(s_m1, 2 * (g - 1))
                        for jb in range(2):
                            blk = 2 * half + jb
                            for j in range(HPB):
                                r = slice(j * HPAD, j * HPAD + HD)
                                m = nc.tensor.matmul(ps[:, 4 * (g % 2) + j, jb * S:(jb + 1) * S],
                                                     q4T[r, blk, t * P:(t + 1) * P], k4T[r, blk, b * S:(b + 1) * S],
                                                     start=True, stop=True)
                        m.then_inc(s_s1, 1)
                    pe.wait_ge(s_m1, 2 * NG)
                    turn_heads(qpad, 2)
                    pe.wait_ge(s_padT, 12)

                    def scores(n):
                        b, hd = divmod(n, NH)
                        blk, j = divmod(hd, HPB)
                        if n >= 6:
                            pe.wait_ge(s_p, n - 5)
                        r = slice(j * HPAD, j * HPAD + HD + 2)
                        for kt in range(2):
                            m = nc.tensor.matmul(ps[:, n % 6, kt * S:(kt + 1) * S],
                                                 k4T[r, blk, b * S + kt * P:b * S + (kt + 1) * P],
                                                 q4T[r, blk, b * S:(b + 1) * S], start=True, stop=True)
                        m.then_inc(s_s2, 1)

                    pe.wait_ge(s_va, 6 + 2 * NT + 4)
                    for n in range(5):
                        scores(n)
                    for n in range(NHB):
                        if n + 5 < NHB:
                            scores(n + 5)
                        b, hd = divmod(n, NH)
                        g = n // 4
                        pe.wait_ge(s_p, n + 1)
                        if n % 4 == 0 and g >= 2:
                            pe.wait_ge(s_o, g - 1)
                        for qt in range(2):
                            c0 = (2 * (n % 4) + qt) * VW
                            for kt in range(2):
                                m = nc.tensor.matmul(ps[:, 6 + g % 2, c0:c0 + VW],
                                                     prob[:, n % 4, kt * S + qt * P:kt * S + (qt + 1) * P],
                                                     vaug[:, 2 * b + kt, hd, :], start=kt == 0, stop=kt == 1)
                        if n % 4 == 3:
                            m.then_inc(s_pv, 1)
                    pe.wait_ge(s_o, NHB // 4)
                    turn_on_tensor(pe, o, 0, None, None, s_oP)
                    pe.wait_ge(s_oT, 4)
                    for t in range(NT):
                        for k in range(KD):
                            m = nc.tensor.matmul(ps[:, 4 + t // 2, (t % 2) * D:(t % 2 + 1) * D], hT[:, k, t * P:(t + 1) * P],
                                                 wo[:, k, :], start=k == 0, stop=k == KD - 1)
                        if t % 2:
                            m.then_inc(s_fin, 1)

                @block.vector
                def _(dve):
                    v = Steps(dve, s_v)
                    norm_on_vector(dve, v, s_var, s_sd, s_h)
                    dve.wait_ge(s_w, 16 * 14)
                    for t in range(NT):
                        dve.wait_ge(s_kv, t + 1)
                        nc.vector.tensor_tensor(kv[:, t, :], ps[:, t % 4, :], bkv[:, t % 2, :], ALU.add).then_inc(s_kve, 1)
                    for i in range(4):
                        dve.wait_ge(s_q, i + 1)
                        nc.vector.tensor_tensor(q[:, 2 * i:2 * i + 2, :], ps[:, 4 + i, :].rearrange("p (t n) -> p t n", t=2),
                                                bq.unsqueeze(1).broadcast_to([P, 2, D]), ALU.add).then_inc(s_qe, 1)
                    dve.wait_ge(s_kve, NT)
                    dve.wait_ge(s_qe, 4)
                    dve.wait_ge(s_va, 2)

                    def head_norm(i, src, dst, w, bias):
                        v.link(nc.vector.tensor_reduce(st[:, 2, :], src, AX.X, ALU.add))
                        v.link(nc.vector.tensor_scalar(st[:, 3, :], st[:, 2, :], 1.0 / HD, None, ALU.mult))
                        nc.vector.tensor_tensor(src, src, wide(3), ALU.subtract).then_inc(s_sqi, 1)
                        dve.wait_ge(s_sq, i + 1)
                        v.link(nc.vector.tensor_reduce(st[:, 2, :], groups(t1[:, :, :]), AX.X, ALU.add))
                        nc.vector.tensor_scalar(st[:, 0, :], st[:, 2, :], 1.0 / HD, EPS4, ALU.mult, ALU.add).then_inc(s_qv, 1)
                        dve.wait_ge(s_qs, i + 1)
                        v.link(nc.vector.reciprocal(st[:, 2, :], st[:, 1, :]))
                        v.link(nc.vector.tensor_tensor(src, src, wide(2), ALU.mult))
                        for par in range(2):
                            sv = src.rearrange("p (t g) d -> p t g d", g=NH)[:, par::2]
                            for tt in range(NT // 2):
                                v.mark(nc.vector.tensor_tensor(sv[:, tt], sv[:, tt],
                                                               w(par).unsqueeze(1).broadcast_to([P, NH, HD]), ALU.mult))
                        v.settle()
                        for par in range(2):
                            sv = src.rearrange("p (t g) d -> p t g d", g=NH)[:, par::2]
                            for tt in range(NT // 2):
                                v.mark(nc.vector.tensor_tensor(dst[:, 2 * tt + par, :, 0:HD], sv[:, tt],
                                                               bias(par).unsqueeze(1).broadcast_to([P, NH, HD]), ALU.add))
                        v.settle()
                        dve.sem_inc(s_pad, 1)

                    head_norm(0, kview, kpad, lambda p_: kn[:, p_, 0, :], lambda p_: kn[:, p_, 1, :])
                    head_norm(1, groups(q), qpad, lambda p_: qn[:, 0, :], lambda p_: qn[:, 1, :])
                    for g in range(NG):
                        t, half = divmod(g, 2)
                        dve.wait_ge(s_s1, g + 1)
                        if g == 0:
                            dve.wait_ge(s_padP, 16)
                        sc = ps[:, 4 * (g % 2):4 * (g % 2) + 4, :].rearrange("p j (c n) -> p j c n", c=2)
                        dst = qpad[:, t].rearrange("p (c j) d -> p j c d", j=HPB)[:, :, 2 * half:2 * half + 2, :]
                        for j, (lo, hi) in enumerate(((0, NMAIN), (NMAIN, S))):
                            nc.vector.tensor_reduce(dst[:, :, :, HD + j], sc[:, :, :, lo:hi], AX.X, ALU.max,
                                                    negate=True).then_inc(s_m1, 1)
                    for g in range(NHB // 4):
                        b, blk = divmod(g, NBLK)
                        dve.wait_ge(s_pv, g + 1)
                        pv = ps[:, 6 + g % 2, 0:8 * VW].rearrange("p (j t c d) -> p j t c d", j=4, t=2, c=2)
                        for c in range(2):
                            v.mark(nc.vector.reciprocal(rz[:, g % 2, :, :, c], pv[:, :, :, c, HD]))
                        v.settle()
                        for c in range(2):
                            v.mark(nc.vector.tensor_tensor(part[:, c], pv[:, :, :, c, 0:HD],
                                                           rz[:, g % 2, :, :, c].unsqueeze(3).broadcast_to([P, 4, 2, HD]),
                                                           ALU.mult))
                        v.settle()
                        dst = o[:, 2 * b:2 * b + 2, :].rearrange("p t (g d) -> p g t d", d=HD)[:, HPB * blk:HPB * (blk + 1)]
                        nc.vector.tensor_tensor(dst, part[:, 0], part[:, 1], ALU.add).then_inc(s_o, 1)
                    for i in range(4):
                        dve.wait_ge(s_fin, i + 1)
                        xb = x[:, 2 * i:2 * i + 2, :]
                        v.link(nc.vector.tensor_tensor(t1[:, 2 * i:2 * i + 2, :], ps[:, 4 + i, :].rearrange("p (t n) -> p t n", t=2),
                                                       bo.unsqueeze(1).broadcast_to([P, 2, D]), ALU.add))
                        nc.vector.scalar_tensor_tensor(xb, t1[:, 2 * i:2 * i + 2, :], tg[:, 2:3], xb, ALU.mult, ALU.add)

        BLK, FF = 32, 4 * D
        s_w5 = ctx.enter_context(nc.semaphore("w5_loaded"))
        W5raw = regC[:, 8960:13056].rearrange("p (j n) -> p j n", j=2)

        def load_w5(sp):
            sp.dma_start(W5raw[:, 0, :], a["L2_W1"]).then_inc(s_w5, 16)
            sp.dma_start(W5raw[:, 1, :], a["L2_W2"]).then_inc(s_w5, 16)

        def mx_quantize(v, src, dst, tmp, am, s_done=None):
            n = src.shape[1]
            wide = lambda c: am[:, c, 0:n].unsqueeze(2).broadcast_to([P, n, BLK])
            v.link(nc.vector.tensor_reduce(am[:, 0, 0:n], src, AX.X, ALU.max, apply_absolute_value=True))
            e = am[:, 0, 0:n].bitcast(I32)
            v.link(nc.vector.tensor_scalar(e, e, 0x7F800000, None, ALU.bitwise_and))
            v.mark(nc.vector.tensor_scalar(am[:, 1, 0:n], am[:, 0, 0:n], 2.0 ** -100, ROUND / 64, ALU.max, ALU.mult))
            v.link(nc.vector.tensor_scalar(am[:, 2, 0:n], am[:, 0, 0:n], 2.0 ** -100, 127 / 64, ALU.max, ALU.mult))
            v.link(nc.vector.tensor_tensor(tmp, src, wide(1), ALU.add))
            v.link(nc.vector.tensor_tensor(tmp, tmp, wide(1), ALU.subtract))
            ins = nc.vector.tensor_tensor(dst, tmp, wide(2), ALU.min)
            if s_done is None:
                v.link(ins)
            else:
                ins.then_inc(s_done, 1)

        def stage5():
            ar = Arena(regB, regC[:, 0:8960])
            blocks = lambda w: w.rearrange("p (n k) -> p n k", k=BLK)
            wq = ar.take([2, 2048], BF16)
            tmp = ar.take([2048])
            am = ar.take([3, 64])
            rb = ar.take([NT, D], BF16)
            y1, g1 = ar.take([2, FF], BF16), ar.take([2, FF], BF16)
            q1, q2 = ar.take([NT * D], BF16), ar.take([2, FF], BF16)
            q1T, q2T = ar.take([KD, T], BF16), ar.take([2, FF // P, P], BF16)
            tmp2 = ar.take([2, FF])
            am2 = ar.take([3, 64])
            lnw, lnb, b2 = ar.take([D]), ar.take([D]), ar.take([D])
            b1 = ar.take([FF])
            hb = ar.take([NT * D], BF16)
            y2, z = ar.take([D], BF16), ar.take([D], BF16)
            (s_var, s_sd, s_h, s_var2, s_sd2, s_h2, s_b, s_v, s_wq, s_wqT, s_wqe, s_q1, s_q1P, s_q1T, s_y1, s_y1b,
             s_g1, s_q2, s_q2P, s_q2T, s_y2, s_x) = (
                sem("s5_" + n) for n in ("var sd h var2 sd2 h2 b v wq wqT wqe q1 q1P q1T y1 y1b g1 q2 q2P q2T y2 x").split())
            with nc.Block("stage5") as block:
                @block.sync
                def _(sp):
                    load_w5(sp)
                    load_w7(sp)
                    for dst, nm in ((lnw, "L2_lnw"), (lnb, "L2_lnb"), (b1, "L2_b1"), (b2, "L2_b2")):
                        sp.dma_start(dst, a[nm].partition_broadcast(P)).then_inc(s_b, 16)

                @block.scalar
                def _(act):
                    norm_on_scalar(act, s_var, s_sd)
                    act.wait_ge(s_var2, 1)
                    nc.scalar.activation(lnsd[:, 1, :], lnsd[:, 0, :], ACT.Sqrt).then_inc(s_sd2, 1)
                    act.wait_ge(s_wqT, 1)
                    nc.scalar.copy(W1q[:, :, :], psb[:, 0:2, 0:FF]).then_inc(s_wqe, 1)
                    act.wait_ge(s_wqT, 2)
                    nc.scalar.copy(W2q[:, :, :].rearrange("p (b k) n -> p b (k n)", b=2), psb[:, 2:4, 0:FF]).then_inc(s_wqe, 1)
                    for i in range(4):
                        act.wait_ge(s_q1P, i + 1)
                        nc.scalar.copy(q1T[:, :, i * 2 * P:(i + 1) * 2 * P], turned(4 + i, psb)).then_inc(s_q1T, 1)
                    for t in range(NT + 1):
                        if t < NT:
                            act.wait_ge(s_y1b, t + 1)
                            if t >= 2:
                                act.wait_ge(s_q2, t - 1)
                            nc.scalar.activation(g1[:, t % 2, :], y1[:, t % 2, :], ACT.Gelu_apprx_tanh).then_inc(s_g1, 1)
                        if t >= 1:
                            act.wait_ge(s_q2P, t)
                            if t >= 3:
                                act.wait_ge(s_y2, t - 2)
                            nc.scalar.copy(q2T[:, (t - 1) % 2].rearrange("p k n -> p (k n)"),
                                           psb[:, 4 + (t - 1) % 2, 0:FF]).then_inc(s_q2T, 1)

                @block.tensor
                def _(pe):
                    pe.wait_ge(s_wq, 1)
                    for o in range(FF // P):
                        for k in range(KD):
                            m = nc.tensor.transpose(psb[:, k, o * P:(o + 1) * P], wq[:, 0, o * D + k * P:o * D + (k + 1) * P],
                                                    identb[:, :])
                    m.then_inc(s_wqT, 1)
                    pe.wait_ge(s_wq, 2)
                    for k in range(FF // P):
                        for o in range(KD):
                            m = nc.tensor.transpose(psb[:, 2 + k // 4, (k % 4) * D + o * P:(k % 4) * D + (o + 1) * P],
                                                    wq[:, 1, o * FF + k * P:o * FF + (k + 1) * P], identb[:, :])
                    m.then_inc(s_wqT, 1)
                    turn_on_tensor(pe, q1.rearrange("p (t n) -> p t n", n=D), 4, s_q1, lambda t: 1, s_q1P,
                                   dst_psum=psb, idn=identb)
                    pe.wait_ge(s_wqe, 2)
                    pe.wait_ge(s_q1T, 4)

                    def up(t):
                        if t >= 2:
                            pe.wait_ge(s_y1b, t - 1)
                        for n in range(2):
                            for k in range(KD):
                                m = nc.tensor.matmul(ps[:, 2 * (t % 2) + n, :], q1T[:, k, t * P:(t + 1) * P],
                                                     W1q[:, k, n * HALF:(n + 1) * HALF], start=k == 0, stop=k == KD - 1)
                        m.then_inc(s_y1, 1)

                    up(0)
                    for t in range(NT):
                        if t + 1 < NT:
                            up(t + 1)
                        pe.wait_ge(s_q2, t + 1)
                        if t >= 2:
                            pe.wait_ge(s_q2T, t - 1)
                        for k in range(FF // P):
                            m = nc.tensor.transpose(psb[:, 4 + t % 2, k * P:(k + 1) * P], q2[:, t % 2, k * P:(k + 1) * P],
                                                    identb[:, :])
                        m.then_inc(s_q2P, 1)
                        pe.wait_ge(s_q2T, t + 1)
                        if t >= 2:
                            pe.wait_ge(s_x, t - 1)
                        for k in range(FF // P):
                            m = nc.tensor.matmul(ps[:, 6 + t % 2, 0:D], q2T[:, t % 2, k, :], W2q[:, k, :],
                                                 start=k == 0, stop=k == FF // P - 1)
                        m.then_inc(s_y2, 1)

                @block.vector
                def _(dve):
                    v = Steps(dve, s_v)
                    dve.wait_ge(s_w5, 32)
                    for j in range(2):
                        mx_quantize(v, blocks(W5raw[:, j, :]), blocks(wq[:, j, :]), blocks(tmp), am, s_wq)
                    norm_on_vector(dve, v, s_var, s_sd, s_h, dst=rb)
                    dve.wait_ge(s_h, NT)
                    norm_on_vector(dve, v, s_var2, s_sd2, s_h2, src=rb, dst=h)
                    dve.wait_ge(s_h2, NT)
                    dve.wait_ge(s_b, 64)
                    rows = lambda w: w.unsqueeze(1).broadcast_to([P, NT, D])
                    v.link(nc.vector.tensor_tensor(h[:, :, :], h[:, :, :], rows(lnw), ALU.mult))
                    v.link(nc.vector.tensor_tensor(hb.rearrange("p (t n) -> p t n", n=D), h[:, :, :], rows(lnb), ALU.add))
                    mx_quantize(v, blocks(hb), blocks(q1), blocks(tmp), am, s_q1)

                    def hidden(t):
                        dve.wait_ge(s_y1, t + 1)
                        if t >= 2:
                            dve.wait_ge(s_g1, t - 1)
                        nc.vector.tensor_tensor(y1[:, t % 2, :], ps[:, 2 * (t % 2):2 * (t % 2) + 2, :].rearrange("p b n -> p (b n)"),
                                                b1, ALU.add).then_inc(s_y1b, 1)

                    def result(t):
                        dve.wait_ge(s_y2, t + 1)
                        v.link(nc.vector.tensor_tensor(y2, ps[:, 6 + t % 2, 0:D], b2, ALU.add))
                        v.link(nc.vector.tensor_tensor(z, y2, rb[:, t, :], ALU.add))
                        nc.vector.scalar_tensor_tensor(x[:, t, :], z, tg[:, 6:7], x[:, t, :], ALU.mult,
                                                       ALU.add).then_inc(s_x, 1)

                    hidden(0)
                    for t in range(NT):
                        if t + 1 < NT:
                            hidden(t + 1)
                        dve.wait_ge(s_g1, t + 1)
                        if t >= 2:
                            dve.wait_ge(s_q2P, t - 1)
                        mx_quantize(v, blocks(g1[:, t % 2, :]), blocks(q2[:, t % 2, :]), blocks(tmp2[:, t % 2, :]), am2, s_q2)
                        if t >= 1:
                            result(t - 1)
                    result(NT - 1)

        def stage7():
            moe_stage("stage7", NE7, NC7, W7, rt7, lambda c: sel7[:, c * P:(c + 1) * P], 7,
                      s_w7, 5, load=load_w7 if start == 7 else None)

        stages = [stage0, stage1, stage2, stage3, stage4, stage5, stage6, stage7]
        setup()
        if start in (0, 6):
            ssm()
        for i, f in enumerate(stages):
            if start <= i <= stop:
                f()
                if i == 3:
                    give_back()

        with nc.Block("store") as block:
            @block.sync
            def _(sp):
                sp.dma_start(out.rearrange("b (h p) d -> p (b h) d", p=P), x[:, :, :]).then_inc(s_out, 16)
                sp.wait_ge(s_out, 16)


def kernel(**inputs):
    import numpy as np
    import concourse.bacc as _bacc
    from concourse import mybir as _mybir
    from concourse.bass_utils import run_bass_kernel_spmd as _run

    f = {k: np.asarray(v) for k, v in inputs.items()}
    C2 = np.ascontiguousarray
    f["xx"] = f["x"]

    def pair_order(w):
        return C2(w.reshape(w.shape[0], -1, P, 2).transpose(0, 1, 3, 2)).reshape(w.shape[0], -1)

    def moe_in(w):
        return C2(w.reshape(KD, P, -1).transpose(1, 0, 2)).reshape(P, -1)

    def packed_rows(w):
        return pair_order(C2(w.T))

    arrays = {
        "x": f["xx"],
        "g_xattn": f["g_xattn"], "g_ffn": f["g_ffn"],
        "ctxT": C2(f["ctx_1024"].reshape(T, C).T),
        "L0_qkT": C2(np.stack([f["L0_xattn_Wq"].T, f["L0_xattn_Wk"].T], 1)),
        "L0_bqk": C2(np.stack([f["L0_xattn_bq"], f["L0_xattn_bk"]], 1)),
        "fsT": C2(f["fside_BxS2xS2_0"].transpose(2, 0, 1).reshape(KD, P, T).transpose(1, 0, 2)),
        **{f"L0_{n}_pk": packed_rows(f[f"L0_ffn_{n}_W_packed"]) for n in ("gate", "up")},
        **{f"L0_{n}_sc": pair_order(C2(f[f"L0_ffn_{n}_scales"].T)) for n in ("gate", "up")},
        "L0_down_pk": C2(f["L0_ffn_down_W_packed"].T.reshape(8, P, D).transpose(1, 0, 2)).reshape(P, -1),
        "L0_down_sc": C2(f["L0_ffn_down_scales"].T.reshape(8, 8, D).transpose(1, 0, 2)).reshape(8, -1),
        "L1_gate": moe_in(np.concatenate([f["L1_ffn_Wg"], f["L1_ffn_sWg"][None]], 0).transpose(1, 0, 2)),
        "L1_up": moe_in(np.concatenate([f["L1_ffn_Wu"], f["L1_ffn_sWu"][None]], 0).transpose(1, 0, 2)),
        "L1_down": C2(np.concatenate([f["L1_ffn_Wd"], f["L1_ffn_sWd"][None]], 0).transpose(1, 0, 2)).reshape(P, -1),
        "L1_router": C2(f["L1_ffn_Wr"].T.reshape(KD, P, 16).transpose(1, 0, 2)),
        "L2_W1": C2(f["L2_ffn_W1"].reshape(8, P, D).transpose(1, 0, 2)).reshape(P, -1),
        "L2_W2": C2(f["L2_ffn_W2"].reshape(2, P, 4 * D).transpose(1, 0, 2)).reshape(P, -1),
        "L2_lnw": f["L2_ffn_ln_w"], "L2_lnb": f["L2_ffn_ln_b"], "L2_b1": f["L2_ffn_b1"], "L2_b2": f["L2_ffn_b2"],
        "m_in": C2(f["L3_xattn_in_proj_w"].T),
        "m_cw": C2(np.concatenate([f["L3_xattn_conv_w"].reshape(D, 4), f["L3_xattn_conv_b"][:, None],
                                   f["L3_xattn_dt_proj_b"][:, None], f["L3_xattn_D"][:, None]], 1)
                   .reshape(KD, P, 7).transpose(1, 0, 2)),
        "m_alog": C2(f["L3_xattn_A_log"].reshape(KD, P, 16).transpose(1, 0, 2)),
        "m_xp": C2(np.concatenate([f["L3_xattn_x_proj_w"][8:]] * 3 + [f["L3_xattn_x_proj_w"][:8]], 0).T
                   .reshape(KD, P, 104).transpose(1, 0, 2)),
        "m_dtw": C2(f["L3_xattn_dt_proj_w"].T),
        "m_sel": np.tile(np.eye(32, dtype=np.float32), (3, 1)),
        "q4_wq": C2(f["L2_xattn_Wq"].reshape(KD, P, D).transpose(1, 0, 2)),
        "q4_wo": C2(f["L2_xattn_Wo"].reshape(KD, P, D).transpose(1, 0, 2)),
        "q4_wkv": C2(np.concatenate([f["L2_xattn_Wk"], f["L2_xattn_Wv"]], 1)),
        "q4_wdca": C2(f["L2_xattn_Wkv_dca"].reshape(P, 2, 16, 16).transpose(0, 2, 1, 3)).reshape(P, -1),
        "q4_bkv": np.concatenate([f["L2_xattn_bk"], f["L2_xattn_bv"]]),
        "q4_bdca": C2(f["L2_xattn_bkv_dca"].reshape(2, 16, 16).transpose(1, 0, 2)).reshape(-1),
        "q4_bq": f["L2_xattn_bq"], "q4_bo": f["L2_xattn_bo"],
        "q4_qn": np.stack([f["L2_xattn_qn_w"], f["L2_xattn_qn_b"]]),
        "q4_kn": np.stack([f["L2_xattn_kn_w"], f["L2_xattn_kn_b"]]),
        "q4_kd": np.stack([f["L2_xattn_kn_dca_w"], f["L2_xattn_kn_dca_b"]]),
        "q4_mask": np.stack([np.stack([np.ones(P), np.arange(P) < P - 16], 1),
                             np.stack([np.zeros(P), np.arange(P) >= P - 16], 1)], 2).astype(np.float32),
        "L1_bias": f["L1_ffn_bias"],
        "L3_gate": moe_in(f["L3_ffn_gate_proj"].transpose(2, 0, 1)),
        "L3_up": moe_in(f["L3_ffn_up_proj"].transpose(2, 0, 1)),
        "L3_down": C2(f["L3_ffn_down_proj"].transpose(0, 2, 1).reshape(11, P, D).transpose(1, 0, 2)).reshape(P, -1),
        "L3_router": C2(f["L3_ffn_gate_w"].T.reshape(KD, P, 8).transpose(1, 0, 2)),
        "iota": np.arange(16, dtype=np.float32),
        "sel7": np.repeat(np.eye(8, dtype=np.float32), 176, 1),
        "ident": np.eye(P, dtype=np.float32),
    }
    nc = _bacc.Bacc("TRN2", target_bir_lowering=False, num_devices=1)
    args = {k: nc.dram_tensor("in_" + k, v.shape, _mybir.dt.from_np(v.dtype), kind="ExternalInput").ap()
            for k, v in arrays.items()}
    out = nc.dram_tensor("out_x", (B, S, D), F32, kind="ExternalOutput").ap()
    build(nc, args, out)
    r = _run(nc, [{"in_" + k: v for k, v in arrays.items()}], core_ids=[0])
    return r.results[0]["out_x"]
```

```python
from contextlib import ExitStack

import concourse.bass as bass
from concourse import mybir

P = 128
B, S, D, C = 4, 256, 256, 128
T = B * S
NT = T // P
KD = D // P
HALF = T // 2
TPH = HALF // P
LN_EPS = 1e-5
GELU_C = 0.7978845608028654
ROUND = 12582912.0

ALU = mybir.AluOpType
ACT = mybir.ActivationFunctionType
AX = mybir.AxisListType
F32 = mybir.dt.float32
BF16 = mybir.dt.bfloat16
F16 = mybir.dt.float16
U16 = mybir.dt.uint16
U32 = mybir.dt.uint32
I32 = mybir.dt.int32
F32R = mybir.dt.float32r


class Steps:

    def __init__(self, eng, sem):
        self.eng, self.sem, self.n = eng, sem, 0

    def mark(self, ins):
        ins.then_inc(self.sem, 1)
        self.n += 1

    def settle(self):
        self.eng.wait_ge(self.sem, self.n)

    def link(self, ins):
        self.mark(ins)
        self.settle()


def build(nc, a, out, start=0, stop=99):
    with ExitStack() as ctx:
        def sb(name, shape, dt=F32):
            return ctx.enter_context(nc.sbuf_tensor(name, shape, dt))

        s_out = ctx.enter_context(nc.semaphore("out_stored"))
        held = []

        def sem(name):
            held.append(nc.alloc_semaphore(name=name))
            return held[-1]

        def give_back():
            with nc.Block(f"give_back_{len(held)}") as block:
                @block.gpsimd
                def _(pool):
                    nc.clear_and_free_semaphores(held)
            held.clear()

        ps = ctx.enter_context(nc.psum_tensor("ps", [P, 8, 512], F32))
        psb = ps[:, :, :].rearrange("p b n -> p (b n)").bitcast(BF16).rearrange("p (b n) -> p b n", b=8)

        x = sb("x", [P, NT, D])
        h = sb("h", [P, NT, D])
        hT = sb("hT", [P, KD, T])
        ctxT = sb("ctxT", [P, T])
        yssm = sb("yssm", [P, KD, T])
        ident = sb("ident", [P, P])
        identb = sb("identb", [P, P], BF16)
        iota = sb("iota", [P, 16])
        tg = sb("tg", [P, 8])
        lnst = sb("lnst", [P, NT, 6])
        lnmv = sb("lnmv", [P, NT, 2])
        lnsd = sb("lnsd", [P, 2, NT])
        W1q = sb("W1q", [P, KD, 4 * D], BF16)
        W2q = sb("W2q", [P, 4 * D // P, D], BF16)
        regA = sb("regA", [P, 12288])
        g8 = sb("g8", [P, 8])
        rt3, rt7 = sb("rt3", [P, KD, 16]), sb("rt7", [P, KD, 8])
        bias3 = sb("bias3", [P, 16])
        WORDS_B = WORDS_C = 13056
        low = ExitStack()
        regB = low.enter_context(nc.sbuf_tensor("regB", [P, WORDS_B], F32))
        high = ExitStack()
        regC = high.enter_context(nc.sbuf_tensor("regC", [P, WORDS_C], F32, side="right"))

        class Arena:

            def __init__(self, *regs):
                self.regs = [[r, 0, r.shape[1]] for r in regs]

            def take(self, shape, dt=F32):
                n = 1
                for s in shape:
                    n *= s
                words = n if dt in (F32, I32, U32) else (n + 1) // 2
                words = (words + 7) // 8 * 8
                for r in self.regs:
                    if r[1] + words <= r[2]:
                        v = r[0][:, r[1]:r[1] + (n if dt in (F32, I32, U32) else n // 2)]
                        r[1] += words
                        break
                else:
                    raise ValueError(f"arena full for {shape}: {[(q[1], q[2]) for q in self.regs]}")
                if dt != F32:
                    v = v.bitcast(dt)
                if len(shape) > 1:
                    names = "abcde"[:len(shape)]
                    v = v.rearrange(f"p ({' '.join(names)}) -> p {' '.join(names)}",
                                    **{k: s for k, s in zip(names[1:], shape[1:])})
                return v

        def norm_on_vector(dve, v, s_var, s_sd, s_h, interleave=False, src=x, dst=h):
            for t in range(NT):
                v.mark(nc.vector.bn_stats(lnst[:, t, :], src[:, t, :]))
            v.settle()
            for t in range(NT):
                v.mark(nc.vector.bn_aggr(lnmv[:, t, :], lnst[:, t, :]))
            v.settle()
            nc.vector.tensor_scalar(lnsd[:, 0, :], lnmv[:, :, 1], LN_EPS, None, ALU.add).then_inc(s_var, 1)
            dve.wait_ge(s_sd, 1)
            v.link(nc.vector.reciprocal(lnsd[:, 0, :], lnsd[:, 1, :]))
            for t in range(NT):
                o, i = dst[:, t, :], src[:, t, :]
                if interleave:
                    o = o.rearrange("p (a j) -> p j a", a=2)
                    i = i.rearrange("p (j a) -> p j a", a=2)
                nc.vector.tensor_scalar(o, i, lnmv[:, t, 0:1], lnsd[:, 0, t:t + 1],
                                        ALU.subtract, ALU.mult).then_inc(s_h, 1)

        def norm_on_scalar(act, s_var, s_sd):
            act.wait_ge(s_var, 1)
            nc.scalar.activation(lnsd[:, 1, :], lnsd[:, 0, :], ACT.Sqrt).then_inc(s_sd, 1)

        def turn_on_tensor(pe, src, bank0, s_src, src_at, s_turned, flat=False, dst_psum=None, idn=None):
            pt = ps if dst_psum is None else dst_psum
            for i in range(NT // 2):
                for t in (2 * i, 2 * i + 1):
                    if s_src is not None:
                        pe.wait_ge(s_src, src_at(t))
                    for k in range(KD):
                        o = pt[:, bank0 + i, k * 2 * P + (t % 2) * P:k * 2 * P + (t % 2) * P + P]
                        last = nc.tensor.transpose(o, src[:, t, k * P:(k + 1) * P], (idn or ident)[:, :])
                last.then_inc(s_turned, 1)

        def turned(bank, pt=None):
            return (ps if pt is None else pt)[:, bank, 0:KD * 2 * P].rearrange("p (k n) -> p k n", k=KD)

        def setup():
            s_in, s_step = sem("su_in"), sem("su_step")
            with nc.Block("setup") as block:
                @block.sync
                def _(sp):
                    sp.dma_start(g8[:, 0:4], a["g_xattn"].partition_broadcast(P)).then_inc(s_in, 16)
                    sp.dma_start(g8[:, 4:8], a["g_ffn"].partition_broadcast(P)).then_inc(s_in, 16)
                    sp.dma_start(ctxT[:, :], a["ctxT"]).then_inc(s_in, 16)
                    sp.dma_start(x[:, :, :], a["x"].rearrange("b (h p) d -> p (b h) d", p=P)).then_inc(s_in, 16)
                    sp.dma_start(ident[:, :], a["ident"]).then_inc(s_in, 16)
                    sp.dma_start(iota[:, :], a["iota"].partition_broadcast(P)).then_inc(s_in, 16)

                @block.scalar
                def _(act):
                    act.wait_ge(s_in, 96)
                    nc.scalar.activation(tg[:, :], g8[:, :], ACT.Tanh)

                @block.vector
                def _(dve):
                    dve.wait_ge(s_in, 96)
                    nc.vector.tensor_copy(identb[:, :], ident[:, :])

        NHC = 2048 // P
        WG, WU, WD = (regA[:, i * 4096:(i + 1) * 4096] for i in range(3))
        raw = [regB[:, i * 2048:(i + 1) * 2048].bitcast(I32) for i in range(3)]
        scl = [regB[:, (3 + i) * 2048:(4 + i) * 2048] for i in range(3)]
        WDv = WD.rearrange("p (c a n) -> p c a n", c=NHC // 2, a=2)

        def load_packed(sp, s_pk):
            for i, nm in enumerate(("gate", "up", "down")):
                sp.dma_start(raw[i], a[f"L0_{nm}_pk"]).then_inc(s_pk[i], 16)
                for g in range(8):
                    sp.dma_start(scl[i][16 * g:16 * g + 16, :],
                                 a[f"L0_{nm}_sc"][g, :].partition_broadcast(16)).then_inc(s_pk[i], 16)

        def dequant_on_vector(dve, v, dq, s_pk, s_nib, s_dq):
            val, mag, tmp = dq
            for i in range(3):
                dve.wait_ge(s_pk[i], 16 * 9)
                lo16 = raw[i].bitcast(U16).rearrange("p (n two) -> p n two", two=2)[:, :, 0]
                for par in range(2):
                    n = 2 * i + par
                    if n >= 2:
                        dve.wait_ge(s_dq, n - 1)
                    o = val[:, par, :]
                    v.mark(nc.vector.tensor_scalar(mag, lo16, 4 * par, 7, ALU.logical_shift_right, ALU.bitwise_and))
                    v.link(nc.vector.tensor_scalar(o, lo16, 8 << (4 * par), 12 - 4 * par,
                                                   ALU.bitwise_and, ALU.logical_shift_left))
                    v.link(nc.vector.tensor_scalar(tmp, mag, 64.0, float(0x3F00), ALU.mult, ALU.add))
                    v.link(nc.vector.scalar_tensor_tensor(tmp, mag, float(0x3F00), tmp, ALU.mult, ALU.min))
                    nc.vector.tensor_tensor(o, o, tmp, ALU.bitwise_or).then_inc(s_nib, 1)

        def dequant_on_gpsimd(pool, dq, s_nib, s_dq):
            for i, w in enumerate((WG, WU, WD)):
                for par in range(2):
                    pool.wait_ge(s_nib, 2 * i + par + 1)
                    code = dq[0][:, par, :].bitcast(BF16)
                    if i < 2:
                        o, q, sc = w[:, par * 2048:(par + 1) * 2048], code, scl[i]
                    else:
                        o = WDv[:, :, par, :]
                        q = code.rearrange("p (c n) -> p c n", n=D)
                        sc = scl[i].rearrange("p (c n) -> p c n", n=D)
                    nc.gpsimd.tensor_tensor(o, q, sc, ALU.mult).then_inc(s_dq, 1)

        def stage0():
            ar = Arena(regC)
            qT, kT = ar.take([T]), ar.take([T])
            att, attT = ar.take([NT, D]), ar.take([KD, T])
            w = ar.take([2, C])
            bqk = ar.take([2])
            nmx, den = ar.take([NT]), ar.take([NT])
            dq = [ar.take([2, 4 * HALF], U16), ar.take([4 * HALF], U16), ar.take([4 * HALF], U16)]
            s_w = sem("s0_w")
            s_var, s_sd, s_h = sem("s0_var"), sem("s0_sd"), sem("s0_h")
            s_proj, s_qk, s_en, s_mx = sem("s0_proj"), sem("s0_qk"), sem("s0_en"), sem("s0_mx")
            s_exp, s_att, s_hTp, s_hT = sem("s0_exp"), sem("s0_att"), sem("s0_hTp"), sem("s0_hT")
            s_pk, s_nib, s_dq = [sem(f"s0_pk{i}") for i in range(3)], sem("s0_nib"), sem("s0_dq")
            s_aTp, s_aT, s_mix, s_v = sem("s0_aTp"), sem("s0_aT"), sem("s0_mix"), sem("s0_v")
            with nc.Block("stage0") as block:
                @block.sync
                def _(sp):
                    sp.dma_start(w, a["L0_qkT"]).then_inc(s_w, 16)
                    sp.dma_start(bqk, a["L0_bqk"]).then_inc(s_w, 16)
                    load_packed(sp, s_pk)

                @block.scalar
                def _(act):
                    for i, dst in enumerate((qT, kT)):
                        for hf in range(2):
                            act.wait_ge(s_proj, 2 * i + hf + 1)
                            nc.scalar.activation(dst[:, hf * HALF:(hf + 1) * HALF], ps[:, 2 * i + hf, :],
                                                 ACT.Identity, bias=bqk[:, i:i + 1]).then_inc(s_qk, 1)
                    norm_on_scalar(act, s_var, s_sd)
                    for t in range(NT):
                        act.wait_ge(s_mx, t // 2 + 1)
                        nc.scalar.activation(att[:, t, :], ps[:, 4 + t // 2, (t % 2) * S:(t % 2 + 1) * S], ACT.Exp,
                                             bias=nmx[:, t:t + 1], accum_out=den[:, t:t + 1]).then_inc(s_exp, 1)
                    for i in range(NT // 2):
                        act.wait_ge(s_hTp, i + 1)
                        nc.scalar.copy(hT[:, :, i * 2 * P:(i + 1) * 2 * P], turned(i)).then_inc(s_hT, 1)

                @block.tensor
                def _(pe):
                    pe.wait_ge(s_w, 32)
                    for i in range(2):
                        for hf in range(2):
                            nc.tensor.matmul(ps[:, 2 * i + hf, :], w[:, i, :], ctxT[:, hf * HALF:(hf + 1) * HALF],
                                             start=True, stop=True).then_inc(s_proj, 1)
                    pe.wait_ge(s_qk, 4)
                    for t in range(NT):
                        b = t // 2
                        e = nc.tensor.matmul(ps[:, 4 + b, (t % 2) * S:(t % 2 + 1) * S], qT[:, t * P:(t + 1) * P],
                                             kT[:, b * S:(b + 1) * S], start=True, stop=True)
                        if t % 2:
                            e.then_inc(s_en, 1)
                    turn_on_tensor(pe, h, 0, s_h, lambda t: t + 1, s_hTp)
                    pe.wait_ge(s_exp, NT)
                    turn_on_tensor(pe, att, 4, s_att, lambda t: t + 1, s_aTp)
                    pe.wait_ge(s_hT, NT // 2)
                    for t in range(NT):
                        b = t // 2
                        pe.wait_ge(s_aT, b + 1)
                        for k in range(KD):
                            m = nc.tensor.matmul(ps[:, b, (t % 2) * S:(t % 2 + 1) * S], hT[:, k, t * P:(t + 1) * P],
                                                 attT[:, k, b * S:(b + 1) * S], start=k == 0, stop=k == KD - 1)
                        if t % 2:
                            m.then_inc(s_mix, 1)

                @block.vector
                def _(dve):
                    v = Steps(dve, s_v)
                    norm_on_vector(dve, v, s_var, s_sd, s_h)
                    for b in range(B):
                        dve.wait_ge(s_en, b + 1)
                        nc.vector.tensor_reduce(nmx[:, 2 * b:2 * b + 2], ps[:, 4 + b, :].rearrange("p (t m) -> p t m", t=2),
                                                AX.X, ALU.max, negate=True).then_inc(s_mx, 1)
                    for t in range(NT):
                        dve.wait_ge(s_exp, t + 1)
                        v.link(nc.vector.reciprocal(den[:, t:t + 1], den[:, t:t + 1]))
                        nc.vector.tensor_scalar(att[:, t, :], att[:, t, :], den[:, t:t + 1], None,
                                                ALU.mult).then_inc(s_att, 1)
                    for i in range(NT // 2):
                        dve.wait_ge(s_aTp, i + 1)
                        nc.vector.tensor_copy(attT[:, :, i * 2 * P:(i + 1) * 2 * P], turned(4 + i)).then_inc(s_aT, 1)
                    for b in range(B):
                        dve.wait_ge(s_mix, b + 1)
                        xb = x[:, 2 * b:2 * b + 2, :]
                        nc.vector.scalar_tensor_tensor(xb, ps[:, b, :].rearrange("p (t m) -> p t m", t=2),
                                                       tg[:, 0:1], xb, ALU.mult, ALU.add)
                    dequant_on_vector(dve, v, dq, s_pk, s_nib, s_dq)

                @block.gpsimd
                def _(pool):
                    dequant_on_gpsimd(pool, dq, s_nib, s_dq)

        NST, DTR, TAPS = 16, 8, 4
        NBC = 2 * NST

        arS = Arena(regC)
        u, dt, du = arS.take([KD, T]), arS.take([KD, T]), arS.take([KD, T])
        cw = arS.take([KD, TAPS + 3])
        alog = arS.take([KD, NST])
        bcs = arS.take([T], BF16)
        selb = arS.take([NBC], BF16)

        u_ssm = u

        def ssm_prepare():
            ar = Arena(regB)
            LP = S + TAPS - 1
            xpad = ar.take([KD, B, LP])
            sA, sB = ar.take([T]), ar.take([T])
            xpad2 = ar.take([KD, T])
            in_w = ar.take([KD * P])
            xp_w = ar.take([KD, 3 * NBC + DTR])
            dt_w = ar.take([D])
            dtl = ar.take([T])
            bcf = ar.take([T])
            bc1, bc2 = ar.take([T], BF16), ar.take([T], BF16)
            self_ = ar.take([NBC])
            s_w, s_xi, s_xc, s_u, s_xp, s_dt, s_e, s_v, s_bcs, s_A, s_z = (
                sem("m_" + n) for n in "w xi xc u xp dt e v bcs A z".split())
            with nc.Block("ssm_prepare") as block:
                @block.sync
                def _(sp):
                    for dst, nm in ((in_w, "m_in"), (cw, "m_cw"), (alog, "m_alog"), (xp_w, "m_xp"),
                                    (dt_w[3 * NBC:3 * NBC + DTR, :], "m_dtw"), (self_[0:3 * NBC, :], "m_sel")):
                        sp.dma_start(dst, a[nm]).then_inc(s_w, 16)

                @block.scalar
                def _(act):
                    act.wait_ge(s_w, 96)
                    nc.scalar.activation(alog, alog, ACT.Exp).then_inc(s_A, 1)
                    for i in range(4):
                        k, hf = divmod(i, 2)
                        act.wait_ge(s_xi, i + 1)
                        nc.scalar.copy(xpad[:, k, 2 * hf:2 * hf + 2, TAPS - 1:LP],
                                       ps[:, i, :].rearrange("p (b l) -> p b l", b=2)).then_inc(s_xc, 1)
                    for k in range(KD):
                        act.wait_ge(s_u, k + 1)
                        nc.scalar.activation(u[:, k, :], u[:, k, :], ACT.Silu).then_inc(s_z, 1)
                    for k in range(KD):
                        if k == 0:
                            act.wait_ge(s_xp, 2)
                        nc.scalar.activation(sA if k == 0 else sB, ps[:, 2 * k:2 * k + 2, :].rearrange("p b n -> p (b n)"),
                                             ACT.Abs, bias=cw[:, k, TAPS + 1:TAPS + 2]).then_inc(s_e, 1)
                        act.wait_ge(s_e, k + 1)
                        nc.scalar.activation(dt[:, k, :], sA if k == 0 else sB, ACT.Exp, scale=-1.0).then_inc(s_dt, 1)

                @block.tensor
                def _(pe):
                    pe.wait_ge(s_w, 96)
                    for i in range(4):
                        k, hf = divmod(i, 2)
                        nc.tensor.matmul(ps[:, i, :], in_w[:, k * P:(k + 1) * P], ctxT[:, hf * HALF:(hf + 1) * HALF],
                                         start=True, stop=True).then_inc(s_xi, 1)
                    pe.wait_ge(s_z, 2)
                    for hf in range(2):
                        for k in range(KD):
                            m = nc.tensor.matmul(ps[0:3 * NBC + DTR, 4 + hf, :], xp_w[:, k, :],
                                                 u[:, k, hf * HALF:(hf + 1) * HALF], start=k == 0, stop=k == KD - 1)
                    m.then_inc(s_xp, 1)
                    pe.wait_ge(s_bcs, 1)
                    dtr = slice(3 * NBC, 3 * NBC + DTR)
                    for k in range(KD):
                        for hf in range(2):
                            m = nc.tensor.matmul(ps[:, 2 * k + hf, :], dt_w[dtr, k * P:(k + 1) * P],
                                                 dtl[dtr, hf * HALF:(hf + 1) * HALF], start=True, stop=True)
                    m.then_inc(s_xp, 1)

                @block.vector
                def _(dve):
                    v = Steps(dve, s_v)
                    v.mark(nc.vector.memset(xpad[:, :, :, 0:TAPS - 1], 0.0))
                    dve.wait_ge(s_w, 96)
                    dve.wait_ge(s_A, 1)
                    v.mark(nc.vector.tensor_copy(selb[0:3 * NBC, :], self_[0:3 * NBC, :]))
                    v.link(nc.vector.tensor_scalar(alog, alog, -1.0, None, ALU.mult))
                    for k in range(KD):
                        dve.wait_ge(s_xc, 2 * k + 2)
                        o = u[:, k, :].rearrange("p (b l) -> p b l", b=B)
                        v.link(nc.vector.tensor_scalar(o, xpad[:, k, :, TAPS - 1:LP], cw[:, k, TAPS - 1:TAPS],
                                                       cw[:, k, TAPS:TAPS + 1], ALU.mult, ALU.add))
                        for q in range(TAPS - 1):
                            ins = nc.vector.scalar_tensor_tensor(o, xpad[:, k, :, q:q + S], cw[:, k, q:q + 1], o,
                                                                 ALU.mult, ALU.add)
                            if q < TAPS - 2:
                                v.link(ins)
                        ins.then_inc(s_u, 1)
                    dve.wait_ge(s_xp, 1)
                    R = 3 * NBC
                    proj = ps[:, 4:6, :].rearrange("p b n -> p (b n)")
                    v.mark(nc.vector.tensor_copy(dtl[R:R + DTR, :], proj[R:R + DTR, :]))
                    v.link(nc.vector.tensor_copy(bc1[0:R, :], proj[0:R, :]))
                    v.link(nc.vector.tensor_tensor(bcf[0:R, :], proj[0:R, :], bc1[0:R, :], ALU.subtract))
                    v.link(nc.vector.tensor_copy(bc2[0:R, :], bcf[0:R, :]))
                    v.link(nc.vector.tensor_tensor(bcf[0:R, :], bcf[0:R, :], bc2[0:R, :], ALU.subtract))
                    v.mark(nc.vector.tensor_copy(bcs[0:NBC, :], bc1[0:NBC, :]))
                    v.mark(nc.vector.tensor_copy(bcs[NBC:2 * NBC, :], bc2[NBC:2 * NBC, :]))
                    v.mark(nc.vector.tensor_copy(bcs[2 * NBC:R, :], bcf[2 * NBC:R, :]))
                    v.settle()
                    dve.sem_inc(s_bcs, 1)
                    dve.wait_ge(s_xp, 2)
                    for k, w in ((0, sA), (1, sB)):
                        z = ps[:, 2 * k:2 * k + 2, :].rearrange("p b n -> p (b n)")
                        dve.wait_ge(s_e, k + 1)
                        bias = cw[:, k, TAPS + 1:TAPS + 2]
                        v.mark(nc.vector.tensor_scalar(xpad2[:, k, :], z, bias, 0.0, ALU.add, ALU.max))
                    for k, w in ((0, sA), (1, sB)):
                        dve.wait_ge(s_dt, k + 1)
                        e, q = dt[:, k, :], du[:, k, :]
                        v.link(nc.vector.tensor_scalar(w, e, 2.0, None, ALU.add))
                        v.link(nc.vector.reciprocal(q, w))
                        v.link(nc.vector.tensor_tensor(e, e, q, ALU.mult))
                        v.link(nc.vector.tensor_tensor(q, e, e, ALU.mult))
                        v.link(nc.vector.tensor_scalar(w, q, 2.0 / 17, 2.0 / 15, ALU.mult, ALU.add))
                        v.link(nc.vector.tensor_tensor(w, w, q, ALU.mult))
                        for c in (13, 11, 9, 7, 5, 3):
                            v.link(nc.vector.scalar_tensor_tensor(w, w, 2.0 / c, q, ALU.add, ALU.mult))
                        v.link(nc.vector.scalar_tensor_tensor(w, w, 2.0, e, ALU.add, ALU.mult))
                        v.link(nc.vector.tensor_tensor(e, w, xpad2[:, k, :], ALU.add))
                        v.link(nc.vector.tensor_tensor(q, e, u[:, k, :], ALU.mult))

        def stage1():
            ar, arB = Arena(regC[:, arS.regs[0][1]:]), Arena(regB)
            gel = ar.take([2, HALF])
            itm = ar.take([2, HALF])
            HB = B // 2
            dA = arB.take([4, KD, HB, S])
            dBu, hs = arB.take([KD, HALF]), arB.take([KD, HALF])
            hc = arB.take([2, KD, HALF])
            s_var, s_sd, s_h, s_hTp, s_hT = (sem("s1_" + n) for n in ("var", "sd", "h", "hTp", "hT"))
            s_gu, s_gel, s_itm, s_down, s_add, s_v = (sem("s1_" + n) for n in ("gu", "gel", "itm", "down", "add", "v"))
            s_b, s_c, s_bu, s_dA, s_zero, s_scan, s_hc, s_y = (
                sem("s1_" + n) for n in ("brow", "crow", "bu", "dA", "zero", "scan", "hc", "y"))
            NU = 2 * NHC
            NGR = 2 * NST
            LEAD = 2

            def half(v, k, hf):
                return v[:, k, hf * HALF:(hf + 1) * HALF]

            with nc.Block("stage1") as block:
                @block.scalar
                def _(act):
                    def decays(g):
                        hf, n = divmod(g, NST)
                        if g >= 4:
                            act.wait_ge(s_scan, g - 3)
                        for k in range(KD):
                            src = half(dt, k, hf).rearrange("p (b l) -> p b l", b=HB)[:, :, 1:S]
                            nc.scalar.activation(dA[:, g % 4, k, :, 1:S], src, ACT.Exp,
                                                 scale=alog[:, k, n:n + 1]).then_inc(s_dA, 1)

                    norm_on_scalar(act, s_var, s_sd)
                    for i in range(NT // 2):
                        act.wait_ge(s_hTp, i + 1)
                        nc.scalar.copy(hT[:, :, i * 2 * P:(i + 1) * 2 * P], turned(2 + i)).then_inc(s_hT, 1)
                    for g in range(LEAD):
                        decays(g)
                    for u in range(0, NU, 2):
                        for w in (u, u + 1):
                            act.wait_ge(s_gu, w + 1)
                            if w >= 2:
                                act.wait_ge(s_itm, w - 1)
                            nc.scalar.activation(gel[:, w % 2, :], ps[:, 2 + 2 * (w % 2), :],
                                                 ACT.Gelu_apprx_tanh).then_inc(s_gel, 1)
                        for g in (u + LEAD, u + LEAD + 1):
                            if g < NGR:
                                decays(g)

                @block.tensor
                def _(pe):
                    turn_on_tensor(pe, h, 2, s_h, lambda t: t + 1, s_hTp)

                    def row(g, j):
                        hf, n = divmod(g, NST)
                        if g >= 1:
                            pe.wait_ge((s_bu, s_hc)[j], g)
                        r = j * NST + n
                        nc.tensor.matmul(ps[:, 6 + j, :], selb[0:3 * NBC, r:r + 1].broadcast_to([3 * NBC, P]),
                                         bcs[0:3 * NBC, hf * HALF:(hf + 1) * HALF],
                                         start=True, stop=True).then_inc((s_b, s_c)[j], 1)

                    def gate_up(u):
                        hf, c = divmod(u, NHC)
                        if u < 2:
                            pe.wait_ge(s_hT, NT // 2)
                        else:
                            pe.wait_ge(s_itm, u - 1)
                        for j, w in enumerate((WG, WU)):
                            for k in range(2):
                                m = nc.tensor.matmul(ps[:, 2 + 2 * (u % 2) + j, :],
                                                     w[:, k * 2048 + c * P:k * 2048 + (c + 1) * P],
                                                     hT[:, k, hf * HALF:(hf + 1) * HALF], start=k == 0, stop=k == 1)
                        m.then_inc(s_gu, 1)

                    def down(u):
                        hf, c = divmod(u, NHC)
                        pe.wait_ge(s_itm, u + 1)
                        if u == NHC:
                            pe.wait_ge(s_add, 1)
                        for t in range(TPH):
                            m = nc.tensor.matmul(ps[:, t // 2, (t % 2) * D:(t % 2 + 1) * D],
                                                 itm[:, u % 2, t * P:(t + 1) * P], WDv[:, c // 2, c % 2, :],
                                                 start=(c == 0 and t % 2 == 0), stop=c == NHC - 1,
                                                 skip_group_check=True)
                        m.then_inc(s_down, 1)

                    row(0, 0)
                    row(0, 1)
                    gate_up(0)
                    for u in range(NU):
                        if u + 1 < NU:
                            gate_up(u + 1)
                        if u >= 1:
                            row(u, 1)
                        down(u)
                        if u + 1 < NGR:
                            row(u + 1, 0)

                @block.vector
                def _(dve):
                    v = Steps(dve, s_v)
                    nc.vector.memset(dA[:, :, :, :, 0:1].rearrange("p a b c d -> p (a b c) d"), 0.0).then_inc(s_zero, 1)
                    norm_on_vector(dve, v, s_var, s_sd, s_h, interleave=True)
                    dve.wait_ge(s_zero, 1)

                    def add_half(hf):
                        dve.wait_ge(s_down, NHC * (hf + 1))
                        for i in range(2):
                            xv = x[:, hf * TPH + 2 * i:hf * TPH + 2 * i + 2, :]
                            ins = nc.vector.scalar_tensor_tensor(xv, ps[:, i, :].rearrange("p (t n) -> p t n", t=2),
                                                                 tg[:, 4:5], xv, ALU.mult, ALU.add)
                        ins.then_inc(s_add, 1)

                    def scan_group(g):
                        hf, n = divmod(g, NST)
                        dve.wait_ge(s_b, g + 1)
                        for k in range(KD):
                            v.mark(nc.vector.tensor_tensor(dBu[:, k, :], half(du, k, hf), ps[:, 6, :], ALU.mult))
                        v.settle()
                        dve.sem_inc(s_bu, 1)
                        dve.wait_ge(s_dA, KD * (g + 1))
                        for k in range(KD):
                            v.mark(nc.vector.tensor_tensor_scan(hs[:, k, :], dA[:, g % 4, k].rearrange("p b l -> p (b l)"),
                                                                dBu[:, k, :], 0.0, ALU.mult, ALU.add))
                        v.settle()
                        dve.sem_inc(s_scan, 1)
                        dve.wait_ge(s_c, g + 1)
                        if g >= 2:
                            dve.wait_ge(s_y, g - 1)
                        for k in range(KD):
                            ins = nc.vector.tensor_tensor(hc[:, g % 2, k, :], hs[:, k, :], ps[:, 7, :], ALU.mult)
                        ins.then_inc(s_hc, 1)

                    for u in range(NU):
                        dve.wait_ge(s_gel, u + 1)
                        if u >= 2:
                            dve.wait_ge(s_down, u - 1)
                        nc.vector.tensor_tensor(itm[:, u % 2, :], gel[:, u % 2, :], ps[:, 3 + 2 * (u % 2), :],
                                                ALU.mult).then_inc(s_itm, 1)
                        scan_group(u)
                        if u == NHC:
                            add_half(0)
                    add_half(1)
                    dve.wait_ge(s_y, NGR)
                    for k in range(KD):
                        v.mark(nc.vector.scalar_tensor_tensor(yssm[:, k, :], u_ssm[:, k, :], cw[:, k, TAPS + 2:TAPS + 3],
                                                              yssm[:, k, :], ALU.mult, ALU.add))

                @block.gpsimd
                def _(pool):
                    for g in range(NGR):
                        hf, n = divmod(g, NST)
                        pool.wait_ge(s_hc, g + 1)
                        y = yssm[:, :, hf * HALF:(hf + 1) * HALF]
                        if n == 0:
                            ins = nc.gpsimd.tensor_copy(y, hc[:, g % 2])
                        else:
                            pool.wait_ge(s_y, g)
                            ins = nc.gpsimd.tensor_tensor(y, y, hc[:, g % 2], ALU.add)
                        ins.then_inc(s_y, 1)

        QEPS, QMAX = 1e-6, 127.0

        def stage2():
            ar = Arena(regA, regC)
            fsT = ar.take([KD, T])
            xs, ws = ar.take([KD, T]), ar.take([KD, T])
            q1f, qbf = ar.take([2 * T * KD]), ar.take([2 * T * KD], BF16)
            four = lambda v, n: v.rearrange("p (j t n) -> p j t n", j=2, n=n)
            q1, qb = four(q1f, D), four(qbf, D)
            xqT, wqT = ar.take([KD, T], BF16), ar.take([KD, T], BF16)
            rows = ar.take([2, T])
            am = ar.take([4, NT])
            tok = ar.take([2, 3, NT])
            am2 = ar.take([4, B])
            tok2 = ar.take([2, 3, NT])
            gu = ar.take([B, 2, S])
            sil = ar.take([B, S])
            res = gu.rearrange("p b g s -> p (b g s)")
            aT = ar.take([T])
            as2, wd2 = ar.take([T]), ar.take([T])
            q2, q2b = four(q1f[:, 0:2 * T], P), four(qbf[:, 0:2 * T], P)
            aqT, dqT = ar.take([T], BF16), ar.take([T], BF16)
            (s_var, s_sd, s_h, s_hTp, s_hT, s_fs, s_v, s_am, s_s, s_xs, s_xsP, s_q, s_qP, s_qT, s_mm, s_rowP, s_row,
             s_gus, s_sil, s_am2, s_s2, s_as, s_asP, s_q2, s_q2P, s_q2T, s_mm2, s_row2P, s_row2, s_tokx, s_tokw) = (
                sem("s2_" + n) for n in ("var sd h hTp hT fs v am s xs xsP q qP qT mm rowP row gus sil am2 s2 as asP q2 "
                                         "q2P q2T mm2 row2P row2 tokx tokw").split())

            def tiles(v, n):
                return v.rearrange("p (t n) -> p t n", n=n)

            with nc.Block("stage2") as block:
                @block.sync
                def _(sp):
                    sp.dma_start(fsT, a["fsT"]).then_inc(s_fs, 16)
                    load_w3(sp)

                @block.scalar
                def _(act):
                    norm_on_scalar(act, s_var, s_sd)
                    act.wait_ge(s_am, 1)
                    nc.scalar.activation(am[:, 3, :], am[:, 2, :], ACT.Sqrt).then_inc(s_s, 1)
                    for j, dst in enumerate((xqT, wqT)):
                        for i in range(4):
                            act.wait_ge(s_qP, 4 * j + i + 1)
                            nc.scalar.copy(dst[:, :, i * 2 * P:(i + 1) * 2 * P], turned(4 * j + i, psb)).then_inc(s_qT, 1)
                    act.wait_ge(s_rowP, 1)
                    nc.scalar.copy(rows[:, 0, :], ps[:, 4:6, :].rearrange("p b n -> p (b n)")).then_inc(s_row, 1)
                    act.wait_ge(s_gus, 1)
                    nc.scalar.activation(sil, gu[:, :, 0, :], ACT.Silu).then_inc(s_sil, 1)
                    act.wait_ge(s_am2, 1)
                    nc.scalar.activation(am2[:, 3, :], am2[:, 2, :], ACT.Sqrt).then_inc(s_s2, 1)
                    for j, dst in enumerate((aqT, dqT)):
                        act.wait_ge(s_q2P, j + 1)
                        nc.scalar.copy(dst, psb[:, 4 + j, 0:T]).then_inc(s_q2T, 1)
                    act.wait_ge(s_row2P, 1)
                    nc.scalar.copy(rows[:, 1, :], ps[:, 6:8, :].rearrange("p b n -> p (b n)")).then_inc(s_row2, 1)

                @block.tensor
                def _(pe):
                    turn_on_tensor(pe, h, 0, s_h, lambda t: t + 1, s_hTp)

                    def turn_back(src, bank0, sem_src, at):
                        pe.wait_ge(sem_src, at)
                        for t in range(NT):
                            for k in range(KD):
                                m = nc.tensor.transpose(ps[:, bank0 + t // 2, (t % 2) * D + k * P:(t % 2) * D + (k + 1) * P],
                                                        src[:, k, t * P:(t + 1) * P], ident[:, :])
                        m.then_inc(s_xsP, 1)

                    pe.wait_ge(s_hT, 4)
                    turn_back(xs, 0, s_xs, 1)
                    turn_back(ws, 4, s_xs, 2)
                    for j in range(2):
                        pe.wait_ge(s_q, j + 1)
                        turn_on_tensor(pe, qb[:, j], 4 * j, None, None, s_qP, dst_psum=psb, idn=identb)
                    pe.wait_ge(s_tokx, 1)
                    pe.wait_ge(s_qT, 8)
                    for t in range(NT):
                        m = nc.tensor.matmul(ps[:, 4 + t // 4, (t % 4) * P:(t % 4 + 1) * P],
                                             tok[:, 0, 1, t:t + 1].broadcast_to([P, P]), ident[:, :],
                                             start=True, stop=True)
                    m.then_inc(s_rowP, 1)
                    for b in range(B):
                        for o in range(2):
                            for k in range(KD):
                                m = nc.tensor.matmul(ps[:, b, o * S:(o + 1) * S],
                                                     wqT[:, k, (2 * b + o) * P:(2 * b + o + 1) * P],
                                                     xqT[:, k, b * S:(b + 1) * S], start=k == 0, stop=k == KD - 1)
                        m.then_inc(s_mm, 1)
                    pe.wait_ge(s_gus, 1)
                    for j, src in enumerate((as2, wd2)):
                        pe.wait_ge(s_as, j + 1)
                        for t in range(NT):
                            m = nc.tensor.transpose(ps[:, 2 * j + t // 4, (t % 4) * P:(t % 4 + 1) * P],
                                                    src[:, t * P:(t + 1) * P], ident[:, :])
                        m.then_inc(s_asP, 1)
                    pe.wait_ge(s_row, 1)
                    for j in range(2):
                        pe.wait_ge(s_q2, j + 1)
                        for t in range(NT):
                            m = nc.tensor.transpose(psb[:, 4 + j, t * P:(t + 1) * P], q2b[:, j, t, :], identb[:, :])
                        m.then_inc(s_q2P, 1)
                    pe.wait_ge(s_tokw, 1)
                    for t in range(NT):
                        m = nc.tensor.matmul(ps[:, 6 + t // 4, (t % 4) * P:(t % 4 + 1) * P],
                                             tok2[:, 1, 1, t:t + 1].broadcast_to([P, P]), ident[:, :],
                                             start=True, stop=True)
                    m.then_inc(s_row2P, 1)
                    pe.wait_ge(s_q2T, 2)
                    for t in range(NT):
                        b = t // 2
                        m = nc.tensor.matmul(ps[:, b, (t % 2) * D:(t % 2 + 1) * D], aqT[:, t * P:(t + 1) * P],
                                             dqT[:, b * S:(b + 1) * S], start=True, stop=True)
                        if t % 2:
                            m.then_inc(s_mm2, 1)

                @block.vector
                def _(dve):
                    v = Steps(dve, s_v)
                    norm_on_vector(dve, v, s_var, s_sd, s_h)
                    for i in range(4):
                        dve.wait_ge(s_hTp, i + 1)
                        nc.vector.tensor_copy(hT[:, :, i * 2 * P:(i + 1) * 2 * P], turned(i)).then_inc(s_hT, 1)

                    def channel_scales(m, s_ready, s_root):
                        v.link(nc.vector.tensor_scalar(m[:, 0:2, :], m[:, 0:2, :], QEPS, None, ALU.max))
                        v.link(nc.vector.reciprocal(m[:, 1, :], m[:, 1, :]))
                        nc.vector.tensor_tensor(m[:, 2, :], m[:, 0, :], m[:, 1, :], ALU.mult).then_inc(s_ready, 1)
                        dve.wait_ge(s_root, 1)
                        v.link(nc.vector.tensor_scalar(m[:, 2, :], m[:, 3, :], QEPS, None, ALU.max))
                        v.link(nc.vector.reciprocal(m[:, 0, :], m[:, 2, :]))

                    def row_scales(tk, amax_src, s_ready=None):
                        v.link(nc.vector.tensor_reduce(tk[:, 0, :], amax_src, AX.X, ALU.max, apply_absolute_value=True))
                        v.link(nc.vector.tensor_scalar(tk[:, 1, :], tk[:, 0, :], QEPS, 1.0 / QMAX, ALU.max, ALU.mult))
                        ins = nc.vector.reciprocal(tk[:, 2, :], tk[:, 1, :])
                        v.link(ins)
                        if s_ready is not None:
                            nc.vector.tensor_copy(tk[:, 0, :], tk[:, 1, :]).then_inc(s_ready, 1)

                    def round_rows(src, n, tk, q, qb_, s_done):
                        for t in range(NT):
                            v.mark(nc.vector.tensor_scalar(q[:, t, :], src[:, t, :], tk[:, 2, t:t + 1], QMAX,
                                                           ALU.mult, ALU.min))
                        v.settle()
                        v.link(nc.vector.tensor_scalar(q, q, -QMAX, ROUND, ALU.max, ALU.add))
                        nc.vector.tensor_scalar(qb_, q, -ROUND, None, ALU.add).then_inc(s_done, 1)

                    segs = lambda w: w.rearrange("p k (b n) -> p (k b) n", b=B)
                    dve.wait_ge(s_fs, 16)
                    v.mark(nc.vector.tensor_reduce(am[:, 1, :], segs(fsT), AX.X, ALU.max, apply_absolute_value=True))
                    dve.wait_ge(s_hT, 4)
                    v.link(nc.vector.tensor_reduce(am[:, 0, :], segs(hT[:, :, :]), AX.X, ALU.max,
                                                   apply_absolute_value=True))
                    channel_scales(am, s_am, s_s)
                    nc.vector.tensor_tensor(segs(xs), segs(hT[:, :, :]), am[:, 0, :].unsqueeze(2).broadcast_to([P, NT, S]),
                                            ALU.mult).then_inc(s_xs, 1)
                    nc.vector.tensor_tensor(segs(ws), segs(fsT), am[:, 2, :].unsqueeze(2).broadcast_to([P, NT, S]),
                                            ALU.mult).then_inc(s_xs, 1)
                    for j in range(2):
                        dve.wait_ge(s_xsP, j + 1)
                        src = ps[:, 4 * j:4 * j + 4, :].rearrange("p b (t n) -> p (b t) n", t=2)
                        row_scales(tok[:, j], src, s_tokx if j == 0 else None)
                        round_rows(src, D, tok[:, j], q1[:, j], qb[:, j], s_q)
                    dve.wait_ge(s_row, 1)
                    for b in range(B):
                        dve.wait_ge(s_mm, b + 1)
                        for o in range(2):
                            v.mark(nc.vector.scalar_tensor_tensor(
                                gu[:, b, o, :], ps[:, b, o * S:(o + 1) * S], tok[:, 1, 1, 2 * b + o:2 * b + o + 1],
                                rows[:, 0, b * S:(b + 1) * S], ALU.mult, ALU.mult))
                    v.settle()
                    v.link(nc.vector.tensor_reduce(am2[:, 1, :], tiles(ctxT[:, :], S), AX.X, ALU.max,
                                                   apply_absolute_value=True))
                    v.settle()
                    dve.sem_inc(s_gus, 1)
                    dve.wait_ge(s_sil, 1)
                    v.link(nc.vector.tensor_tensor(tiles(aT, S), sil, gu[:, :, 1, :], ALU.mult))
                    v.link(nc.vector.tensor_reduce(am2[:, 0, :], tiles(aT, S), AX.X, ALU.max, apply_absolute_value=True))
                    channel_scales(am2, s_am2, s_s2)
                    nc.vector.tensor_tensor(tiles(as2, S), tiles(aT, S), am2[:, 0, :].unsqueeze(2).broadcast_to([P, B, S]),
                                            ALU.mult).then_inc(s_as, 1)
                    nc.vector.tensor_tensor(tiles(wd2, S), tiles(ctxT[:, :], S),
                                            am2[:, 2, :].unsqueeze(2).broadcast_to([P, B, S]), ALU.mult).then_inc(s_as, 1)
                    for j in range(2):
                        dve.wait_ge(s_asP, j + 1)
                        src = ps[:, 2 * j:2 * j + 2, :].rearrange("p b (t n) -> p (b t) n", t=4)
                        row_scales(tok2[:, j], src, s_tokw if j == 1 else None)
                        round_rows(src, P, tok2[:, j], q2[:, j], q2b[:, j], s_q2)
                    dve.wait_ge(s_row2, 1)
                    for b in range(B):
                        dve.wait_ge(s_mm2, b + 1)
                        for o in range(2):
                            t = 2 * b + o
                            v.mark(nc.vector.scalar_tensor_tensor(
                                res[:, t * D:(t + 1) * D], ps[:, b, o * D:(o + 1) * D], tok2[:, 0, 1, t:t + 1],
                                rows[:, 1, b * S:(b + 1) * S], ALU.mult, ALU.mult))
                        v.settle()
                        xb = x[:, 2 * b:2 * b + 2, :]
                        nc.vector.scalar_tensor_tensor(xb, tiles(res[:, 2 * b * D:2 * (b + 1) * D], D), tg[:, 1:2], xb,
                                                       ALU.mult, ALU.add)

        def stage6():
            ar = Arena(regC)
            sil, gated = ar.take([NT, D]), ar.take([NT, D])
            s_var, s_sd, s_h, s_sil, s_gt, s_gP, s_v = (sem("s6_" + n) for n in ("var sd h sil gt gP v").split())
            with nc.Block("stage6") as block:
                @block.scalar
                def _(act):
                    norm_on_scalar(act, s_var, s_sd)
                    for t in range(NT):
                        act.wait_ge(s_h, t + 1)
                        nc.scalar.activation(sil[:, t, :], h[:, t, :], ACT.Silu).then_inc(s_sil, 1)

                @block.tensor
                def _(pe):
                    for b in range(B):
                        pe.wait_ge(s_gt, 2 * b + 2)
                        for l in range(2):
                            for k in range(KD):
                                m = nc.tensor.transpose(ps[:, b, l * D + k * P:l * D + (k + 1) * P],
                                                        gated[:, 2 * b + k, l * P:(l + 1) * P], ident[:, :])
                        m.then_inc(s_gP, 1)

                @block.vector
                def _(dve):
                    v = Steps(dve, s_v)
                    norm_on_vector(dve, v, s_var, s_sd, s_h)
                    for b in range(B):
                        for k in range(KD):
                            t = 2 * b + k
                            dve.wait_ge(s_sil, t + 1)
                            nc.vector.tensor_tensor(gated[:, t, :], sil[:, t, :], yssm[:, k, b * S:(b + 1) * S],
                                                    ALU.mult).then_inc(s_gt, 1)
                    for b in range(B):
                        dve.wait_ge(s_gP, b + 1)
                        xb = x[:, 2 * b:2 * b + 2, :]
                        nc.vector.scalar_tensor_tensor(xb, ps[:, b, :].rearrange("p (t m) -> p t m", t=2),
                                                       tg[:, 3:4], xb, ALU.mult, ALU.add)

        s_w3, s_w7 = (ctx.enter_context(nc.semaphore(n)) for n in ("w3_loaded", "w7_loaded"))
        NE3, NE7, F7 = 16, 8, 176
        NC3, NC7 = NE3 + 1, NE7 * F7 // P
        UW = 6 * P
        W3 = regB[:, 0:NC3 * UW].rearrange("p (c n) -> p c n", n=UW)
        W7 = regA[:, 0:NC7 * UW].rearrange("p (c n) -> p c n", n=UW)
        RING = 3
        LOROW = 32

        def load_w3(sp):
            sp.dma_start(W3, a["L1_w"]).then_inc(s_w3, 16)
            sp.dma_start(rt3[:, :, :], a["L1_router"]).then_inc(s_w3, 16)
            sp.dma_start(bias3[:, :], a["L1_bias"].partition_broadcast(P)).then_inc(s_w3, 16)

        def load_w7(sp):
            sp.dma_start(W7, a["L3_w"]).then_inc(s_w7, 16)
            sp.dma_start(rt7[:, :, :], a["L3_router"]).then_inc(s_w7, 16)

        def moe_stage(tag, E, NC, W, router, gate_col, s_weights, loads, ar, parts, sel_name, load=None,
                      shared=False, bias=None):
            hP, wP, iP, cS, selS = parts
            SW = selS.shape[1]
            gel, itm = ar.take([2, HALF]), ar.take([2, HALF])
            sel = ar.take([SW])
            lg, ex, comb, hit = (ar.take([NT, E]) for _ in range(4))
            top, idx, idf, wk = ar.take([NT, 8]), ar.take([NT, 8], U32), ar.take([NT, 2]), ar.take([NT, 2])
            col = ar.take([3, NT])
            KC = LOROW + E
            combp = ar.take([NT, KC])
            (s_var, s_sd, s_h, s_hTp, s_hT, s_v, s_lg, s_ein, s_exp, s_comb, s_cTp, s_cT, s_gu, s_gel, s_itm, s_down,
             s_add, s_hH, s_hL, s_wH, s_wL, s_sl, s_sel, s_zero) = (sem(f"{tag}_" + n) for n in (
                 "var sd h hTp hT v lg ein exp comb cTp cT gu gel itm down add hH hL wH wL sl sel zero").split())
            NU = 2 * NC
            HI, LO = 0, 1
            PRODUCTS = ((HI, HI), (HI, LO), (LO, HI))
            routed = lambda u: not (shared and u % NC == NC - 1)
            over = lambda v: v.unsqueeze(2).broadcast_to([P, NT, E])
            with nc.Block(tag) as block:
                @block.sync
                def _(sp):
                    if load is not None:
                        load(sp)
                    sp.dma_start(sel[0:KC, :], a[sel_name]).then_inc(s_sl, 16)

                @block.scalar
                def _(act):
                    def high_part(u):
                        if u >= RING:
                            act.wait_ge(s_down, u - RING + 1)
                        if u == 0:
                            act.wait_ge(s_weights, 16 * loads)
                        nc.scalar.copy(wP[HI][:, u % RING, :], W[:, u % NC, :]).then_inc(s_wH, 1)

                    norm_on_scalar(act, s_var, s_sd)
                    for i in range(NT // 2):
                        act.wait_ge(s_hTp, i + 1)
                        nc.scalar.copy(hT[:, :, i * 2 * P:(i + 1) * 2 * P], turned(2 + i)).then_inc(s_hT, 1)
                    for u in range(RING):
                        high_part(u)
                    act.wait_ge(s_ein, 1)
                    if shared:
                        nc.scalar.activation(ex, lg, ACT.Exp).then_inc(s_exp, 1)
                    else:
                        nc.scalar.activation(col[:, 1, :], col[:, 0, :], ACT.Exp).then_inc(s_exp, 1)
                    act.wait_ge(s_cTp, 1)
                    nc.scalar.copy(cS[0:KC, :], ps[0:KC, 6:8, :].rearrange("p b n -> p (b n)")).then_inc(s_cT, 1)
                    for u in range(NU):
                        act.wait_ge(s_gu, u + 1)
                        if u >= 2:
                            act.wait_ge(s_itm, u - 1)
                        nc.scalar.activation(gel[:, u % 2, :], ps[:, 2 + 2 * (u % 2), :], ACT.Silu).then_inc(s_gel, 1)
                        if RING <= u + 2 < NU:
                            high_part(u + 2)

                @block.gpsimd
                def _(pool):
                    pool.wait_ge(s_hT, NT // 2)
                    pool.wait_ge(s_hH, NT // 2)
                    for u in range(NU):
                        pool.wait_ge(s_wH, u + 1)
                        if u >= RING:
                            pool.wait_ge(s_down, u - RING + 1)
                        nc.gpsimd.tensor_tensor(wP[LO][:, u % RING, :], W[:, u % NC, :], wP[HI][:, u % RING, :].bitcast(F32),
                                                ALU.subtract).then_inc(s_wL, 1)

                @block.tensor
                def _(pe):
                    turn_on_tensor(pe, h, 2, s_h, lambda t: t + 1, s_hTp)
                    pe.wait_ge(s_hT, NT // 2)
                    pe.wait_ge(s_weights, 16 * loads)
                    for t in range(NT):
                        for k in range(KD):
                            m = nc.tensor.matmul(ps[:, 6, t * E:(t + 1) * E], hT[:, k, t * P:(t + 1) * P],
                                                 router[:, k, :], start=k == 0, stop=k == KD - 1)
                    m.then_inc(s_lg, 1)
                    pe.wait_ge(s_comb, 1)
                    for t in range(NT):
                        m = nc.tensor.transpose(ps[0:KC, 6 + t // 4, (t % 4) * P:(t % 4 + 1) * P], combp[:, t, :], ident[:, :])
                    m.then_inc(s_cTp, 1)
                    pe.wait_ge(s_cT, 1)
                    pe.wait_ge(s_sel, 1)
                    pe.wait_ge(s_hL, 1)

                    def gate_up(u):
                        hf, c = divmod(u, NC)
                        if u >= 2:
                            pe.wait_ge(s_itm, u - 1)
                        pe.wait_ge(s_wL, u + 1)
                        w = u % 2
                        if routed(u):
                            rows = (selS[0:KC, c:c + 1].broadcast_to([KC, P]) if shared
                                    else selS[0:KC, c * P:(c + 1) * P])
                            m = nc.tensor.matmul(ps[:, 6 + w, :], rows, cS[0:KC, hf * HALF:(hf + 1) * HALF],
                                                 start=True, stop=True)
                        for j in range(2):
                            for k in range(KD):
                                for n, (pw, ph) in enumerate(PRODUCTS):
                                    c0 = (2 * j + k) * P
                                    m = nc.tensor.matmul(ps[:, 2 + 2 * w + j, :], wP[pw][:, u % RING, c0:c0 + P],
                                                         hP[ph][:, k, hf * HALF:(hf + 1) * HALF],
                                                         start=k == 0 and n == 0, stop=k == KD - 1 and n == 2)
                        m.then_inc(s_gu, 1)

                    def down(u):
                        hf, c = divmod(u, NC)
                        w = u % 2
                        pe.wait_ge(s_itm, u + 1)
                        if u == NC:
                            pe.wait_ge(s_add, 1)
                        for t in range(TPH):
                            for n, (pi, pw) in enumerate(PRODUCTS):
                                m = nc.tensor.matmul(ps[:, t // 2, (t % 2) * D:(t % 2 + 1) * D],
                                                     iP[pi][:, w, t * P:(t + 1) * P], wP[pw][:, u % RING, 4 * P:6 * P],
                                                     start=(c == 0 and n == 0 and t % 2 == 0),
                                                     stop=c == NC - 1 and n == 2, skip_group_check=True)
                        m.then_inc(s_down, 1)

                    gate_up(0)
                    for u in range(NU):
                        if u + 1 < NU:
                            gate_up(u + 1)
                        down(u)

                @block.vector
                def _(dve):
                    v = Steps(dve, s_v)
                    norm_on_vector(dve, v, s_var, s_sd, s_h)
                    nc.vector.memset(combp, 0.0).then_inc(s_zero, 1)
                    for i in range(NT // 2):
                        dve.wait_ge(s_hT, i + 1)
                        cols = slice(i * 2 * P, (i + 1) * 2 * P)
                        nc.vector.tensor_copy(hP[HI][:, :, cols], hT[:, :, cols]).then_inc(s_hH, 1)
                    dve.wait_ge(s_hH, NT // 2)
                    nc.vector.tensor_tensor(hP[LO][:, :, :], hT[:, :, :], hP[HI][:, :, :].bitcast(F32),
                                            ALU.subtract).then_inc(s_hL, 1)
                    dve.wait_ge(s_sl, 16)
                    nc.vector.tensor_copy(selS[0:KC, :], sel[0:KC, :]).then_inc(s_sel, 1)
                    dve.wait_ge(s_lg, 1)
                    psl = ps[:, 6, 0:NT * E].rearrange("p (t e) -> p t e", e=E)
                    if shared:
                        v.link(nc.vector.tensor_tensor(lg, psl, bias[:, :].unsqueeze(1).broadcast_to([P, NT, E]), ALU.add))
                        v.link(nc.vector.tensor_reduce(col[:, 0, :], lg, AX.X, ALU.max))
                        nc.vector.tensor_tensor(lg, lg, over(col[:, 0, :]), ALU.subtract).then_inc(s_ein, 1)
                        dve.wait_ge(s_exp, 1)
                        v.link(nc.vector.tensor_reduce(col[:, 1, :], ex, AX.X, ALU.add))
                        v.link(nc.vector.reciprocal(col[:, 2, :], col[:, 1, :]))
                        v.link(nc.vector.tensor_tensor(lg, ex, over(col[:, 2, :]), ALU.mult))
                    else:
                        v.link(nc.vector.tensor_copy(lg, psl))
                    for t in range(NT):
                        v.mark(nc.vector.max(top[:, t, :], lg[:, t, :]))
                    v.settle()
                    for t in range(NT):
                        v.mark(nc.vector.max_index(idx[:, t, :], top[:, t, :], lg[:, t, :]))
                    v.settle()
                    v.link(nc.vector.tensor_copy(idf, idx[:, :, 0:2]))
                    if shared:
                        v.link(nc.vector.tensor_reduce(col[:, 0, :], top[:, :, 0:2], AX.X, ALU.add))
                        v.link(nc.vector.tensor_scalar(col[:, 0, :], col[:, 0, :], 1e-9, None, ALU.add))
                        v.link(nc.vector.reciprocal(col[:, 1, :], col[:, 0, :]))
                        v.link(nc.vector.tensor_tensor(wk, top[:, :, 0:2], col[:, 1, :].unsqueeze(2).broadcast_to([P, NT, 2]),
                                                       ALU.mult))
                    else:
                        nc.vector.tensor_tensor(col[:, 0, :], top[:, :, 1], top[:, :, 0], ALU.subtract).then_inc(s_ein, 1)
                        dve.wait_ge(s_exp, 1)
                        v.link(nc.vector.tensor_scalar(col[:, 2, :], col[:, 1, :], 1.0, None, ALU.add))
                        v.link(nc.vector.reciprocal(wk[:, :, 0], col[:, 2, :]))
                        v.link(nc.vector.tensor_tensor(wk[:, :, 1], wk[:, :, 0], col[:, 1, :], ALU.mult))
                    it = iota[:, 0:E].unsqueeze(1).broadcast_to([P, NT, E])
                    for k, dst in ((0, comb), (1, hit)):
                        v.link(nc.vector.tensor_tensor(dst, it, over(idf[:, :, k]), ALU.is_equal))
                        v.link(nc.vector.tensor_tensor(dst, dst, over(wk[:, :, k]), ALU.mult))
                    v.link(nc.vector.tensor_tensor(comb, comb, hit, ALU.add))
                    dve.wait_ge(s_zero, 1)
                    v.link(nc.vector.tensor_copy(combp[:, :, 0:E].bitcast(F32R), comb))
                    nc.vector.tensor_tensor(combp[:, :, LOROW:KC].bitcast(F32R), comb, combp[:, :, 0:E],
                                            ALU.subtract).then_inc(s_comb, 1)

                    def add_half(hf):
                        dve.wait_ge(s_down, NC * (hf + 1))
                        for i in range(2):
                            xv = x[:, hf * TPH + 2 * i:hf * TPH + 2 * i + 2, :]
                            ins = nc.vector.scalar_tensor_tensor(xv, ps[:, i, :].rearrange("p (t n) -> p t n", t=2),
                                                                 tg[:, gate_col:gate_col + 1], xv, ALU.mult, ALU.add)
                        ins.then_inc(s_add, 1)

                    for u in range(NU):
                        dve.wait_ge(s_gel, u + 1)
                        if u >= 2:
                            dve.wait_ge(s_down, u - 1)
                        o = itm[:, u % 2, :]
                        v.link(nc.vector.tensor_tensor(o, gel[:, u % 2, :], ps[:, 3 + 2 * (u % 2), :], ALU.mult))
                        if routed(u):
                            v.link(nc.vector.tensor_tensor(o, o, ps[:, 6 + u % 2, :], ALU.mult))
                        v.link(nc.vector.tensor_copy(iP[HI][:, u % 2, :], o))
                        nc.vector.tensor_tensor(iP[LO][:, u % 2, :], o, iP[HI][:, u % 2, :].bitcast(F32),
                                                ALU.subtract).then_inc(s_itm, 1)
                        if u == NC - 1:
                            add_half(0)
                    add_half(1)

        def stage3(parts):
            moe_stage("stage3", NE3, NC3, W3, rt3, 5, s_w3, 3, Arena(regA), parts, "sel3", shared=True, bias=bias3,
                      load=load_w3 if start == 3 else None)

        NH, HD, NDCA = 16, 16, 16
        HPAD = 2 * HD
        SCALE4, EPS4 = HD ** -0.5, 1e-6
        NMAIN = S - NDCA
        VW = 2 * (HD + 1)
        HC, KS, KA = 64, 3 * HD, 3 * HD + 4
        HPB = P // HC
        NBLK = NH // HPB

        def stage4(k4T, q4T, regD):
            ar = Arena(regA, regD, regC)
            qpad, kpad = ar.take([2, 2, NH, HC]), ar.take([2, 2, NH, HC])
            kv = ar.take([NT, 2 * D])
            q, t1 = ar.take([NT, D]), h
            vaug = ar.take([NT, NH, VW])
            prob = ar.take([4, 2 * S])
            wq, wkv, wdca, wo = ar.take([KD, D]), ar.take([2 * D]), ar.take([2 * D]), ar.take([KD, D])
            ctxm, ctxd = ar.take([B, P]), ar.take([B, P])
            bkv = ar.take([2, 2 * D])
            bq, bo = ar.take([D]), ar.take([D])
            qn, kn = ar.take([2, HD]), ar.take([2, 2, HD])
            mask = ar.take([2, 2])
            st = ar.take([4, NT * NH])
            rz = ar.take([2, 4, 2, 2])
            nm = ar.take([2, 2, NH, 2])
            o = h
            part = ar.take([2, 4, 2, HD])
            (s_var, s_sd, s_h, s_hTp, s_hT, s_w, s_v, s_q, s_qe, s_kv, s_kve, s_qv, s_qs, s_sqi, s_sq, s_kp, s_qp, s_T, s_Te,
             s_s1, s_mx, s_qm, s_s2, s_p, s_pv, s_o, s_oP, s_oT, s_fin, s_ctx, s_va) = (
                sem("s4_" + n) for n in ("var sd h hTp hT w v q qe kv kve qv qs sqi sq kp qp T Te s1 mx qm s2 p pv o oP oT "
                                         "fin ctx va").split())
            groups = lambda w: w.rearrange("p t (g d) -> p (t g) d", d=HD)
            kview = kv.rearrange("p t (g d) -> p (t g) d", d=HPAD)[:, :, 0:HD]
            wide = lambda c: st[:, c, :].unsqueeze(2).broadcast_to([P, NT * NH, HD])
            NHB = B * NH
            NVA = 2 + 8 + 2 * NT + 4

            TK, TQ, MAX0, TM = 0, 2, 4, 13

            def flat(v):
                return v.rearrange("p a b -> p (a b)")

            with nc.Block("stage4") as block:
                @block.sync
                def _(sp):
                    for dst, nm in ((wq, "q4_wq"), (wkv, "q4_wkv"), (wdca, "q4_wdca"), (wo, "q4_wo")):
                        sp.dma_start(dst, a[nm]).then_inc(s_w, 16)
                    row = lambda nm: a[nm].partition_broadcast(P)
                    sp.dma_start(bkv[:, 0, :], row("q4_bkv")).then_inc(s_w, 16)
                    sp.dma_start(bkv[0:NMAIN - P, 1, :], a["q4_bkv"].partition_broadcast(NMAIN - P)).then_inc(s_w, 16)
                    sp.dma_start(bkv[NMAIN - P:P, 1, :], a["q4_bdca"].partition_broadcast(NDCA)).then_inc(s_w, 16)
                    sp.dma_start(bq, row("q4_bq")).then_inc(s_w, 16)
                    sp.dma_start(bo, row("q4_bo")).then_inc(s_w, 16)
                    sp.dma_start(qn, row("q4_qn")).then_inc(s_w, 16)
                    sp.dma_start(kn[:, 0], row("q4_kn")).then_inc(s_w, 16)
                    sp.dma_start(kn[0:NMAIN - P, 1], a["q4_kn"].partition_broadcast(NMAIN - P)).then_inc(s_w, 16)
                    sp.dma_start(kn[NMAIN - P:P, 1], a["q4_kd"].partition_broadcast(NDCA)).then_inc(s_w, 16)
                    sp.dma_start(mask, a["q4_mask"]).then_inc(s_w, 16)

                @block.gpsimd
                def _(pool):
                    pool.wait_ge(s_w, 16 * 14)
                    c = ctxT[:, :].rearrange("p (b two n) -> p b two n", two=2, n=P)[:, :, 1, :]
                    nc.gpsimd.tensor_copy(ctxm[:, :, 0:NMAIN - P], c[:, :, 0:NMAIN - P]).then_inc(s_ctx, 1)
                    nc.gpsimd.memset(ctxm[:, :, NMAIN - P:P], 0.0).then_inc(s_ctx, 1)
                    nc.gpsimd.memset(ctxd[:, :, 0:NMAIN - P], 0.0).then_inc(s_ctx, 1)
                    nc.gpsimd.tensor_copy(ctxd[:, :, NMAIN - P:P], c[:, :, NMAIN - P:P]).then_inc(s_ctx, 1)
                    for v_ in (qpad, kpad):
                        nc.gpsimd.memset(v_.rearrange("p a t g d -> p (a t g) d")[:, :, KS:HC], 0.0).then_inc(s_va, 1)
                    pool.wait_ge(s_va, 2)
                    for t in range(2):
                        for j in range(4):
                            ones = kpad[:, :, t, :, KS + j]
                            nc.gpsimd.tensor_scalar(ones, ones, mask[:, t, j % 2:j % 2 + 1], None, ALU.add).then_inc(s_va, 1)
                    pool.wait_ge(s_kve, NT)
                    for t in range(NT):
                        for j in range(2):
                            mk = mask[:, t % 2, j:j + 1]
                            src = kv[:, t, :].rearrange("p (g d) -> p g d", d=HPAD)[:, :, HD:HPAD]
                            c0 = j * (HD + 1)
                            nc.gpsimd.tensor_scalar(vaug[:, t, :, c0:c0 + HD], src, mk, None, ALU.mult).then_inc(s_va, 1)
                    pool.wait_ge(s_va, 10 + 2 * NT)
                    for par in range(2):
                        for j in range(2):
                            c0 = j * (HD + 1) + HD
                            ones = kpad[:, 0, par, :, KS + j].unsqueeze(1).broadcast_to([P, NT // 2, NH])
                            nc.gpsimd.tensor_copy(vaug[:, par::2, :, c0], ones).then_inc(s_va, 1)

                @block.scalar
                def _(act):
                    norm_on_scalar(act, s_var, s_sd)
                    for i in range(NT // 2):
                        act.wait_ge(s_hTp, i + 1)
                        nc.scalar.copy(hT[:, :, i * 2 * P:(i + 1) * 2 * P], turned(4 + i)).then_inc(s_hT, 1)
                    for i in range(2):
                        act.wait_ge(s_sqi, i + 1)
                        nc.scalar.activation(groups(t1[:, :, :]), (kview, groups(q))[i], ACT.Square).then_inc(s_sq, 1)
                        act.wait_ge(s_qv, i + 1)
                        nc.scalar.activation(st[:, 1, :], st[:, 0, :], ACT.Sqrt).then_inc(s_qs, 1)

                    def evacuate(b, i):
                        act.wait_ge(s_T, 3 * b + i + 1)
                        if i == 0 and b >= 2:
                            act.wait_ge(s_pv, 4 * (b - 1))
                        dst = (k4T, q4T, q4T)[i]
                        nc.scalar.copy(flat(dst[:, b % 2]), flat(ps[:, 0:4, :])).then_inc(s_Te, 1)

                    def exponent(n):
                        act.wait_ge(s_s2, n + 1)
                        if n >= 4:
                            act.wait_ge(s_pv, n // 4)
                        nc.scalar.activation(prob[:, n % 4, :], ps[:, 4 + n % 2, :], ACT.Exp, scale=SCALE4).then_inc(s_p, 1)

                    for b in range(-1, B):
                        for slot in range(NH):
                            n = b * NH + slot + 1
                            if 0 <= n < NHB and b >= 0:
                                exponent(n)
                            if b + 1 < B and slot in (TK, TQ, TM):
                                evacuate(b + 1, (TK, TQ, TM).index(slot))
                        if b == -1:
                            exponent(0)
                    for i in range(4):
                        act.wait_ge(s_oP, i + 1)
                        nc.scalar.copy(hT[:, :, i * 2 * P:(i + 1) * 2 * P], turned(i)).then_inc(s_oT, 1)

                @block.tensor
                def _(pe):
                    turn_on_tensor(pe, h, 4, s_h, lambda t: t + 1, s_hTp)
                    pe.wait_ge(s_w, 16 * 14)
                    pe.wait_ge(s_ctx, 4)
                    for t in range(NT):
                        if t >= 4:
                            pe.wait_ge(s_kve, t - 3)
                        b = t // 2
                        if t % 2 == 0:
                            m = nc.tensor.matmul(ps[:, t % 4, :], ctxT[:, t * P:(t + 1) * P], wkv, start=True, stop=True)
                        else:
                            nc.tensor.matmul(ps[:, t % 4, :], ctxm[:, b, :], wkv, start=True, stop=False)
                            m = nc.tensor.matmul(ps[:, t % 4, :], ctxd[:, b, :], wdca, start=False, stop=True)
                        m.then_inc(s_kv, 1)
                    pe.wait_ge(s_hT, 4)
                    for t in range(NT):
                        for k in range(KD):
                            m = nc.tensor.matmul(ps[:, 4 + t // 2, (t % 2) * D:(t % 2 + 1) * D], hT[:, k, t * P:(t + 1) * P],
                                                 wq[:, k, :], start=k == 0, stop=k == KD - 1)
                        if t % 2:
                            m.then_inc(s_q, 1)

                    def turn_heads(src, b):
                        for blk in range(NBLK):
                            for t in range(2):
                                c0 = (blk % 2) * S + t * P
                                m = nc.tensor.transpose(ps[:, blk // 2, c0:c0 + P],
                                                        flat(src[:, b % 2, t])[:, blk * P:(blk + 1) * P], ident[:, :])
                        m.then_inc(s_T, 1)

                    def maximum_scores(b, g):
                        t, h0 = g // 4, 4 * (g % 4)
                        if g >= 2:
                            pe.wait_ge(s_mx, 2 * (8 * b + g - 1))
                        for i in range(4):
                            hd = h0 + i
                            r = slice(HC * (hd % 2), HC * (hd % 2) + KS)
                            m = nc.tensor.matmul(ps[:, 2 * (g % 2) + i % 2, (i // 2) * S:(i // 2 + 1) * S],
                                                 q4T[r, b % 2, hd // 2, t * P:(t + 1) * P], k4T[r, b % 2, hd // 2, :],
                                                 start=True, stop=True)
                        m.then_inc(s_s1, 1)

                    def prepare(b, slot):
                        if slot == TK:
                            if b >= 1:
                                pe.wait_ge(s_Te, 3 * b)
                            pe.wait_ge(s_kp, b + 1)
                            turn_heads(kpad, b)
                        elif slot == TQ:
                            pe.wait_ge(s_Te, 3 * b + 1)
                            pe.wait_ge(s_qp, b + 1)
                            turn_heads(qpad, b)
                        elif MAX0 <= slot < MAX0 + 8:
                            if slot == MAX0:
                                pe.wait_ge(s_Te, 3 * b + 2)
                            maximum_scores(b, slot - MAX0)
                        elif slot == TM:
                            pe.wait_ge(s_qm, b + 1)
                            turn_heads(qpad, b)

                    def scores(n):
                        b, hd = divmod(n, NH)
                        if hd == 0:
                            pe.wait_ge(s_Te, 3 * b + 3)
                        if n >= 2:
                            pe.wait_ge(s_p, n - 1)
                        r = slice(HC * (hd % 2), HC * (hd % 2) + KA)
                        for kt in range(2):
                            m = nc.tensor.matmul(ps[:, 4 + n % 2, kt * S:(kt + 1) * S],
                                                 k4T[r, b % 2, hd // 2, kt * P:(kt + 1) * P], q4T[r, b % 2, hd // 2, :],
                                                 start=True, stop=True)
                        m.then_inc(s_s2, 1)

                    def values(n):
                        b, hd = divmod(n, NH)
                        g = n // 4
                        pe.wait_ge(s_p, n + 1)
                        if n % 4 == 0 and g >= 2:
                            pe.wait_ge(s_o, g - 1)
                        for qt in range(2):
                            c0 = (2 * (n % 4) + qt) * VW
                            for kt in range(2):
                                m = nc.tensor.matmul(ps[:, 6 + g % 2, c0:c0 + VW],
                                                     prob[:, n % 4, kt * S + qt * P:kt * S + (qt + 1) * P],
                                                     vaug[:, 2 * b + kt, hd, :], start=kt == 0, stop=kt == 1)
                        if n % 4 == 3:
                            m.then_inc(s_pv, 1)

                    pe.wait_ge(s_va, NVA)
                    pe.wait_ge(s_kve, NT)
                    pe.wait_ge(s_qe, 4)
                    for b in range(-1, B):
                        for slot in range(NH):
                            n = b * NH + slot
                            if b >= 0:
                                if n + 1 < NHB and slot + 1 < NH:
                                    scores(n + 1)
                                values(n)
                            if b + 1 < B:
                                prepare(b + 1, slot)
                        if b + 1 < B:
                            scores((b + 1) * NH)
                    pe.wait_ge(s_o, NHB // 4)
                    turn_on_tensor(pe, o, 0, None, None, s_oP)
                    pe.wait_ge(s_oT, 4)
                    for t in range(NT):
                        for k in range(KD):
                            m = nc.tensor.matmul(ps[:, 4 + t // 2, (t % 2) * D:(t % 2 + 1) * D], hT[:, k, t * P:(t + 1) * P],
                                                 wo[:, k, :], start=k == 0, stop=k == KD - 1)
                        if t % 2:
                            m.then_inc(s_fin, 1)

                @block.vector
                def _(dve):
                    v = Steps(dve, s_v)
                    norm_on_vector(dve, v, s_var, s_sd, s_h)
                    dve.wait_ge(s_w, 16 * 14)
                    for t in range(NT):
                        dve.wait_ge(s_kv, t + 1)
                        nc.vector.tensor_tensor(kv[:, t, :], ps[:, t % 4, :], bkv[:, t % 2, :], ALU.add).then_inc(s_kve, 1)
                    for i in range(4):
                        dve.wait_ge(s_q, i + 1)
                        nc.vector.tensor_tensor(q[:, 2 * i:2 * i + 2, :], ps[:, 4 + i, :].rearrange("p (t n) -> p t n", t=2),
                                                bq.unsqueeze(1).broadcast_to([P, 2, D]), ALU.add).then_inc(s_qe, 1)
                    dve.wait_ge(s_kve, NT)
                    dve.wait_ge(s_qe, 4)
                    dve.wait_ge(s_va, 10)

                    def head_norm(i, src, w, bias):
                        v.link(nc.vector.tensor_reduce(st[:, 2, :], src, AX.X, ALU.add))
                        v.link(nc.vector.tensor_scalar(st[:, 3, :], st[:, 2, :], 1.0 / HD, None, ALU.mult))
                        nc.vector.tensor_tensor(src, src, wide(3), ALU.subtract).then_inc(s_sqi, 1)
                        dve.wait_ge(s_sq, i + 1)
                        v.link(nc.vector.tensor_reduce(st[:, 2, :], groups(t1[:, :, :]), AX.X, ALU.add))
                        nc.vector.tensor_scalar(st[:, 0, :], st[:, 2, :], 1.0 / HD, EPS4, ALU.mult, ALU.add).then_inc(s_qv, 1)
                        dve.wait_ge(s_qs, i + 1)
                        v.link(nc.vector.reciprocal(st[:, 2, :], st[:, 1, :]))
                        v.link(nc.vector.tensor_tensor(src, src, wide(2), ALU.mult))
                        for row, op in ((w, ALU.mult), (bias, ALU.add)):
                            for t in range(NT):
                                sv = src[:, t * NH:(t + 1) * NH, :]
                                v.mark(nc.vector.tensor_tensor(sv, sv, row(t % 2).unsqueeze(1).broadcast_to([P, NH, HD]), op))
                            v.settle()

                    head_norm(0, kview, lambda p_: kn[:, p_, 0, :], lambda p_: kn[:, p_, 1, :])
                    head_norm(1, groups(q), lambda p_: qn[:, 0, :], lambda p_: qn[:, 1, :])

                    def pads(b):
                        for src, pad, lo, his, s_done in (
                                (kview, kpad, HD, (0, 2 * HD), s_kp), (groups(q), qpad, 2 * HD, (0, HD), s_qp)):
                            dst = pad[:, b % 2].rearrange("p t g d -> p (t g) d").bitcast(F32R)
                            sv = src[:, 2 * b * NH:2 * (b + 1) * NH, :]
                            for c0 in his:
                                v.mark(nc.vector.tensor_copy(dst[:, :, c0:c0 + HD], sv))
                            v.settle()
                            nc.vector.tensor_tensor(dst[:, :, lo:lo + HD], sv, dst[:, :, 0:HD].bitcast(F32),
                                                    ALU.subtract).then_inc(s_done, 1)

                    def maxima(b, g):
                        t, h0 = g // 4, 4 * (g % 4)
                        dve.wait_ge(s_s1, 8 * b + g + 1)
                        sc = ps[:, 2 * (g % 2):2 * (g % 2) + 2, :].rearrange("p j (c n) -> p j c n", c=2)
                        dst = nm[:, b % 2, t, h0:h0 + 4, :].rearrange("p (c j) d -> p j c d", j=2)
                        for j, (lo, hi) in enumerate(((0, NMAIN), (NMAIN, S))):
                            nc.vector.tensor_reduce(dst[:, :, :, j], sc[:, :, :, lo:hi], AX.X, ALU.max,
                                                    negate=True).then_inc(s_mx, 1)

                    def place_maxima(b):
                        dve.wait_ge(s_mx, 16 * (b + 1))
                        dst = qpad[:, b % 2].rearrange("p t g d -> p (t g) d").bitcast(F32R)
                        src = nm[:, b % 2].rearrange("p t g d -> p (t g) d")
                        v.link(nc.vector.tensor_copy(dst[:, :, KS:KS + 2], src))
                        nc.vector.tensor_tensor(dst[:, :, KS + 2:KS + 4], src, dst[:, :, KS:KS + 2].bitcast(F32),
                                                ALU.subtract).then_inc(s_qm, 1)

                    def normalize(g):
                        b, blk = divmod(g, NH // 4)
                        dve.wait_ge(s_pv, g + 1)
                        pv = ps[:, 6 + g % 2, 0:8 * VW].rearrange("p (j t c d) -> p j t c d", j=4, t=2, c=2)
                        for c in range(2):
                            v.mark(nc.vector.reciprocal(rz[:, g % 2, :, :, c], pv[:, :, :, c, HD]))
                        v.settle()
                        for c in range(2):
                            v.mark(nc.vector.tensor_tensor(part[:, c], pv[:, :, :, c, 0:HD],
                                                           rz[:, g % 2, :, :, c].unsqueeze(3).broadcast_to([P, 4, 2, HD]),
                                                           ALU.mult))
                        v.settle()
                        dst = o[:, 2 * b:2 * b + 2, :].rearrange("p t (g d) -> p g t d", d=HD)[:, 4 * blk:4 * (blk + 1)]
                        nc.vector.tensor_tensor(dst, part[:, 0], part[:, 1], ALU.add).then_inc(s_o, 1)

                    pads(0)
                    pads(1)
                    for b in range(-1, B):
                        for slot in range(NH):
                            if b >= 0 and slot % 4 == 0 and slot >= 4:
                                normalize(4 * b + slot // 4 - 1)
                            if b >= 1 and slot == 0:
                                normalize(4 * b - 1)
                            if b + 1 < B and MAX0 <= slot < MAX0 + 8:
                                maxima(b + 1, slot - MAX0)
                                if slot == MAX0 + 7:
                                    place_maxima(b + 1)
                            if slot == TM + 1 and b >= 0 and b + 2 < B:
                                dve.wait_ge(s_T, 3 * (b + 1))
                                pads(b + 2)
                    normalize(NHB // 4 - 1)
                    for i in range(4):
                        dve.wait_ge(s_fin, i + 1)
                        xb = x[:, 2 * i:2 * i + 2, :]
                        v.link(nc.vector.tensor_tensor(q[:, 2 * i:2 * i + 2, :], ps[:, 4 + i, :].rearrange("p (t n) -> p t n", t=2),
                                                       bo.unsqueeze(1).broadcast_to([P, 2, D]), ALU.add))
                        nc.vector.scalar_tensor_tensor(xb, q[:, 2 * i:2 * i + 2, :], tg[:, 2:3], xb, ALU.mult, ALU.add)

        BLK, FF = 32, 4 * D
        s_w5 = ctx.enter_context(nc.semaphore("w5_loaded"))
        W5raw = regC[:, 8960:13056].rearrange("p (j n) -> p j n", j=2)

        def load_w5(sp):
            sp.dma_start(W5raw[:, 0, :], a["L2_W1"]).then_inc(s_w5, 16)
            sp.dma_start(W5raw[:, 1, :], a["L2_W2"]).then_inc(s_w5, 16)

        def mx_quantize(v, src, dst, tmp, am, s_done=None):
            n = src.shape[1]
            wide = lambda c: am[:, c, 0:n].unsqueeze(2).broadcast_to([P, n, BLK])
            v.link(nc.vector.tensor_reduce(am[:, 0, 0:n], src, AX.X, ALU.max, apply_absolute_value=True))
            e = am[:, 0, 0:n].bitcast(I32)
            v.link(nc.vector.tensor_scalar(e, e, 0x7F800000, None, ALU.bitwise_and))
            v.mark(nc.vector.tensor_scalar(am[:, 1, 0:n], am[:, 0, 0:n], 2.0 ** -100, ROUND / 64, ALU.max, ALU.mult))
            v.link(nc.vector.tensor_scalar(am[:, 2, 0:n], am[:, 0, 0:n], 2.0 ** -100, 127 / 64, ALU.max, ALU.mult))
            v.link(nc.vector.tensor_tensor(tmp, src, wide(1), ALU.add))
            v.link(nc.vector.tensor_tensor(tmp, tmp, wide(1), ALU.subtract))
            ins = nc.vector.tensor_tensor(dst, tmp, wide(2), ALU.min)
            if s_done is None:
                v.link(ins)
            else:
                ins.then_inc(s_done, 1)

        def stage5():
            ar = Arena(regB, regC[:, 0:8960])
            blocks = lambda w: w.rearrange("p (n k) -> p n k", k=BLK)
            wq = ar.take([2, 2048], BF16)
            tmp = ar.take([2048])
            am = ar.take([3, 64])
            rb = ar.take([NT, D], BF16)
            y1, g1 = ar.take([2, FF], BF16), ar.take([2, FF], BF16)
            q1, q2 = ar.take([NT * D], BF16), ar.take([2, FF], BF16)
            q1T, q2T = ar.take([KD, T], BF16), ar.take([2, FF // P, P], BF16)
            tmp2 = ar.take([2, FF])
            am2 = ar.take([3, 64])
            lnw, lnb, b2 = ar.take([D]), ar.take([D]), ar.take([D])
            b1 = ar.take([FF])
            hb = ar.take([NT * D], BF16)
            y2, z = ar.take([D], BF16), ar.take([D], BF16)
            (s_var, s_sd, s_h, s_var2, s_sd2, s_h2, s_b, s_v, s_wq, s_wqT, s_wqe, s_q1, s_q1P, s_q1T, s_y1, s_y1b,
             s_g1, s_q2, s_q2P, s_q2T, s_y2, s_x) = (
                sem("s5_" + n) for n in ("var sd h var2 sd2 h2 b v wq wqT wqe q1 q1P q1T y1 y1b g1 q2 q2P q2T y2 x").split())
            with nc.Block("stage5") as block:
                @block.sync
                def _(sp):
                    load_w5(sp)
                    load_w7(sp)
                    for dst, nm in ((lnw, "L2_lnw"), (lnb, "L2_lnb"), (b1, "L2_b1"), (b2, "L2_b2")):
                        sp.dma_start(dst, a[nm].partition_broadcast(P)).then_inc(s_b, 16)

                @block.scalar
                def _(act):
                    norm_on_scalar(act, s_var, s_sd)
                    act.wait_ge(s_var2, 1)
                    nc.scalar.activation(lnsd[:, 1, :], lnsd[:, 0, :], ACT.Sqrt).then_inc(s_sd2, 1)
                    act.wait_ge(s_wqT, 1)
                    nc.scalar.copy(W1q[:, :, :], psb[:, 0:2, 0:FF]).then_inc(s_wqe, 1)
                    act.wait_ge(s_wqT, 2)
                    nc.scalar.copy(W2q[:, :, :].rearrange("p (b k) n -> p b (k n)", b=2), psb[:, 2:4, 0:FF]).then_inc(s_wqe, 1)
                    for i in range(4):
                        act.wait_ge(s_q1P, i + 1)
                        nc.scalar.copy(q1T[:, :, i * 2 * P:(i + 1) * 2 * P], turned(4 + i, psb)).then_inc(s_q1T, 1)
                    for t in range(NT + 1):
                        if t < NT:
                            act.wait_ge(s_y1b, t + 1)
                            if t >= 2:
                                act.wait_ge(s_q2, t - 1)
                            nc.scalar.activation(g1[:, t % 2, :], y1[:, t % 2, :], ACT.Gelu_apprx_tanh).then_inc(s_g1, 1)
                        if t >= 1:
                            act.wait_ge(s_q2P, t)
                            if t >= 3:
                                act.wait_ge(s_y2, t - 2)
                            nc.scalar.copy(q2T[:, (t - 1) % 2].rearrange("p k n -> p (k n)"),
                                           psb[:, 4 + (t - 1) % 2, 0:FF]).then_inc(s_q2T, 1)

                @block.tensor
                def _(pe):
                    pe.wait_ge(s_wq, 1)
                    for o in range(FF // P):
                        for k in range(KD):
                            m = nc.tensor.transpose(psb[:, k, o * P:(o + 1) * P], wq[:, 0, o * D + k * P:o * D + (k + 1) * P],
                                                    identb[:, :])
                    m.then_inc(s_wqT, 1)
                    pe.wait_ge(s_wq, 2)
                    for k in range(FF // P):
                        for o in range(KD):
                            m = nc.tensor.transpose(psb[:, 2 + k // 4, (k % 4) * D + o * P:(k % 4) * D + (o + 1) * P],
                                                    wq[:, 1, o * FF + k * P:o * FF + (k + 1) * P], identb[:, :])
                    m.then_inc(s_wqT, 1)
                    turn_on_tensor(pe, q1.rearrange("p (t n) -> p t n", n=D), 4, s_q1, lambda t: 1, s_q1P,
                                   dst_psum=psb, idn=identb)
                    pe.wait_ge(s_wqe, 2)
                    pe.wait_ge(s_q1T, 4)

                    def up(t):
                        if t >= 2:
                            pe.wait_ge(s_y1b, t - 1)
                        for n in range(2):
                            for k in range(KD):
                                m = nc.tensor.matmul(ps[:, 2 * (t % 2) + n, :], q1T[:, k, t * P:(t + 1) * P],
                                                     W1q[:, k, n * HALF:(n + 1) * HALF], start=k == 0, stop=k == KD - 1)
                        m.then_inc(s_y1, 1)

                    up(0)
                    for t in range(NT):
                        if t + 1 < NT:
                            up(t + 1)
                        pe.wait_ge(s_q2, t + 1)
                        if t >= 2:
                            pe.wait_ge(s_q2T, t - 1)
                        for k in range(FF // P):
                            m = nc.tensor.transpose(psb[:, 4 + t % 2, k * P:(k + 1) * P], q2[:, t % 2, k * P:(k + 1) * P],
                                                    identb[:, :])
                        m.then_inc(s_q2P, 1)
                        pe.wait_ge(s_q2T, t + 1)
                        if t >= 2:
                            pe.wait_ge(s_x, t - 1)
                        for k in range(FF // P):
                            m = nc.tensor.matmul(ps[:, 6 + t % 2, 0:D], q2T[:, t % 2, k, :], W2q[:, k, :],
                                                 start=k == 0, stop=k == FF // P - 1)
                        m.then_inc(s_y2, 1)

                @block.vector
                def _(dve):
                    v = Steps(dve, s_v)
                    dve.wait_ge(s_w5, 32)
                    for j in range(2):
                        mx_quantize(v, blocks(W5raw[:, j, :]), blocks(wq[:, j, :]), blocks(tmp), am, s_wq)
                    norm_on_vector(dve, v, s_var, s_sd, s_h, dst=rb)
                    dve.wait_ge(s_h, NT)
                    norm_on_vector(dve, v, s_var2, s_sd2, s_h2, src=rb, dst=h)
                    dve.wait_ge(s_h2, NT)
                    dve.wait_ge(s_b, 64)
                    rows = lambda w: w.unsqueeze(1).broadcast_to([P, NT, D])
                    v.link(nc.vector.tensor_tensor(h[:, :, :], h[:, :, :], rows(lnw), ALU.mult))
                    v.link(nc.vector.tensor_tensor(hb.rearrange("p (t n) -> p t n", n=D), h[:, :, :], rows(lnb), ALU.add))
                    mx_quantize(v, blocks(hb), blocks(q1), blocks(tmp), am, s_q1)

                    def hidden(t):
                        dve.wait_ge(s_y1, t + 1)
                        if t >= 2:
                            dve.wait_ge(s_g1, t - 1)
                        nc.vector.tensor_tensor(y1[:, t % 2, :], ps[:, 2 * (t % 2):2 * (t % 2) + 2, :].rearrange("p b n -> p (b n)"),
                                                b1, ALU.add).then_inc(s_y1b, 1)

                    def result(t):
                        dve.wait_ge(s_y2, t + 1)
                        v.link(nc.vector.tensor_tensor(y2, ps[:, 6 + t % 2, 0:D], b2, ALU.add))
                        v.link(nc.vector.tensor_tensor(z, y2, rb[:, t, :], ALU.add))
                        nc.vector.scalar_tensor_tensor(x[:, t, :], z, tg[:, 6:7], x[:, t, :], ALU.mult,
                                                       ALU.add).then_inc(s_x, 1)

                    hidden(0)
                    for t in range(NT):
                        if t + 1 < NT:
                            hidden(t + 1)
                        dve.wait_ge(s_g1, t + 1)
                        if t >= 2:
                            dve.wait_ge(s_q2P, t - 1)
                        mx_quantize(v, blocks(g1[:, t % 2, :]), blocks(q2[:, t % 2, :]), blocks(tmp2[:, t % 2, :]), am2, s_q2)
                        if t >= 1:
                            result(t - 1)
                    result(NT - 1)

        def stage7(parts):
            moe_stage("stage7", NE7, NC7, W7, rt7, 7, s_w7, 2, Arena(regB), parts, "sel7",
                      load=load_w7 if start == 7 else None)

        stages = [stage0, stage1, stage2, stage3, stage4, stage5, stage6, stage7]
        setup()
        for i, f in enumerate(stages):
            if start <= i <= stop:
                if i == 1:
                    ssm_prepare()
                if i == 4:
                    low.close()
                    with (nc.sbuf_tensor("k4T", [P, 2, NBLK, S], F32R) as k4T,
                          nc.sbuf_tensor("q4T", [P, 2, NBLK, S], F32R) as q4T,
                          nc.sbuf_tensor("regD", [P, WORDS_B - 4 * NBLK * S], F32) as regD):
                        f(k4T, q4T, regD)
                    regB = ctx.enter_context(nc.sbuf_tensor("regB2", [P, WORDS_B], F32))
                    continue
                if i in (3, 7):
                    high.close()
                    with ExitStack() as st:
                        def part(name, shape):
                            return st.enter_context(nc.sbuf_tensor(f"{name}_{i}", shape, F32R, side="right"))
                        pairs = [[part(name + p_, shape) for p_ in ("hi", "lo")]
                                 for name, shape in (("h_", [P, KD, T]), ("w_", [P, RING, UW]), ("i_", [P, 2, HALF]))]
                        f(pairs + [part("comb", [P, T]), part("sel", [P, NE3 if i == 3 else NC7 * P])])
                    if i == 3:
                        give_back()
                        regC = high.enter_context(nc.sbuf_tensor("regC2", [P, WORDS_C], F32, side="right"))
                        W5raw = regC[:, 8960:13056].rearrange("p (j n) -> p j n", j=2)
                    continue
                f()

        with nc.Block("store") as block:
            @block.sync
            def _(sp):
                sp.dma_start(out.rearrange("b (h p) d -> p (b h) d", p=P), x[:, :, :]).then_inc(s_out, 16)
                sp.wait_ge(s_out, 16)
        high.close()
        low.close()


def kernel(**inputs):
    import numpy as np
    import concourse.bacc as _bacc
    from concourse import mybir as _mybir
    from concourse.bass_utils import run_bass_kernel_spmd as _run

    f = {k: np.asarray(v) for k, v in inputs.items()}
    C2 = np.ascontiguousarray
    f["xx"] = f["x"]

    def pair_order(w):
        return C2(w.reshape(w.shape[0], -1, P, 2).transpose(0, 1, 3, 2)).reshape(w.shape[0], -1)

    def moe_units(gate, up, down):
        def rows(w):
            return w.reshape(-1, KD, P, P).transpose(2, 0, 1, 3).reshape(P, -1, D)
        return C2(np.concatenate([rows(gate), rows(up), down.transpose(1, 0, 2)], 2))

    def two_rows(sel):
        return np.concatenate([sel, np.zeros((32 - len(sel), sel.shape[1]), np.float32), sel], 0)

    def packed_rows(w):
        return pair_order(C2(w.T))

    arrays = {
        "x": f["xx"],
        "g_xattn": f["g_xattn"], "g_ffn": f["g_ffn"],
        "ctxT": C2(f["ctx_1024"].reshape(T, C).T),
        "L0_qkT": C2(np.stack([f["L0_xattn_Wq"].T, f["L0_xattn_Wk"].T], 1)),
        "L0_bqk": C2(np.stack([f["L0_xattn_bq"], f["L0_xattn_bk"]], 1)),
        "fsT": C2(f["fside_BxS2xS2_0"].transpose(2, 0, 1).reshape(KD, P, T).transpose(1, 0, 2)),
        **{f"L0_{n}_pk": packed_rows(f[f"L0_ffn_{n}_W_packed"]) for n in ("gate", "up")},
        **{f"L0_{n}_sc": pair_order(C2(f[f"L0_ffn_{n}_scales"].T)) for n in ("gate", "up")},
        "L0_down_pk": C2(f["L0_ffn_down_W_packed"].T.reshape(8, P, D).transpose(1, 0, 2)).reshape(P, -1),
        "L0_down_sc": C2(f["L0_ffn_down_scales"].T.reshape(8, 8, D).transpose(1, 0, 2)).reshape(8, -1),
        "L1_w": moe_units(*(np.concatenate([f[f"L1_ffn_{n}"], f[f"L1_ffn_s{n}"][None]], 0) for n in ("Wg", "Wu", "Wd"))),
        "L1_router": C2(f["L1_ffn_Wr"].T.reshape(KD, P, 16).transpose(1, 0, 2)),
        "L2_W1": C2(f["L2_ffn_W1"].reshape(8, P, D).transpose(1, 0, 2)).reshape(P, -1),
        "L2_W2": C2(f["L2_ffn_W2"].reshape(2, P, 4 * D).transpose(1, 0, 2)).reshape(P, -1),
        "L2_lnw": f["L2_ffn_ln_w"], "L2_lnb": f["L2_ffn_ln_b"], "L2_b1": f["L2_ffn_b1"], "L2_b2": f["L2_ffn_b2"],
        "m_in": C2(f["L3_xattn_in_proj_w"].T),
        "m_cw": C2(np.concatenate([f["L3_xattn_conv_w"].reshape(D, 4), f["L3_xattn_conv_b"][:, None],
                                   f["L3_xattn_dt_proj_b"][:, None], f["L3_xattn_D"][:, None]], 1)
                   .reshape(KD, P, 7).transpose(1, 0, 2)),
        "m_alog": C2(f["L3_xattn_A_log"].reshape(KD, P, 16).transpose(1, 0, 2)),
        "m_xp": C2(np.concatenate([f["L3_xattn_x_proj_w"][8:]] * 3 + [f["L3_xattn_x_proj_w"][:8]], 0).T
                   .reshape(KD, P, 104).transpose(1, 0, 2)),
        "m_dtw": C2(f["L3_xattn_dt_proj_w"].T),
        "m_sel": np.tile(np.eye(32, dtype=np.float32), (3, 1)),
        "q4_wq": C2(f["L2_xattn_Wq"].reshape(KD, P, D).transpose(1, 0, 2)),
        "q4_wo": C2(f["L2_xattn_Wo"].reshape(KD, P, D).transpose(1, 0, 2)),
        "q4_wkv": C2(np.concatenate([f["L2_xattn_Wk"], f["L2_xattn_Wv"]], 1)),
        "q4_wdca": C2(f["L2_xattn_Wkv_dca"].reshape(P, 2, 16, 16).transpose(0, 2, 1, 3)).reshape(P, -1),
        "q4_bkv": np.concatenate([f["L2_xattn_bk"], f["L2_xattn_bv"]]),
        "q4_bdca": C2(f["L2_xattn_bkv_dca"].reshape(2, 16, 16).transpose(1, 0, 2)).reshape(-1),
        "q4_bq": f["L2_xattn_bq"], "q4_bo": f["L2_xattn_bo"],
        "q4_qn": np.stack([f["L2_xattn_qn_w"], f["L2_xattn_qn_b"]]),
        "q4_kn": np.stack([f["L2_xattn_kn_w"], f["L2_xattn_kn_b"]]),
        "q4_kd": np.stack([f["L2_xattn_kn_dca_w"], f["L2_xattn_kn_dca_b"]]),
        "q4_mask": np.stack([np.stack([np.ones(P), np.arange(P) < P - 16], 1),
                             np.stack([np.zeros(P), np.arange(P) >= P - 16], 1)], 2).astype(np.float32),
        "L1_bias": f["L1_ffn_bias"],
        "L3_w": moe_units(*(f[f"L3_ffn_{n}_proj"].reshape(-1, P, D).transpose(0, 2, 1) for n in ("gate", "up")),
                          f["L3_ffn_down_proj"].transpose(0, 2, 1).reshape(-1, P, D)),
        "L3_router": C2(f["L3_ffn_gate_w"].T.reshape(KD, P, 8).transpose(1, 0, 2)),
        "iota": np.arange(16, dtype=np.float32),
        "sel3": two_rows(np.eye(16, dtype=np.float32)),
        "sel7": two_rows(np.repeat(np.eye(8, dtype=np.float32), 176, 1)),
        "ident": np.eye(P, dtype=np.float32),
    }
    nc = _bacc.Bacc("TRN2", target_bir_lowering=False, num_devices=1)
    args = {k: nc.dram_tensor("in_" + k, v.shape, _mybir.dt.from_np(v.dtype), kind="ExternalInput").ap()
            for k, v in arrays.items()}
    out = nc.dram_tensor("out_x", (B, S, D), F32, kind="ExternalOutput").ap()
    build(nc, args, out)
    r = _run(nc, [{"in_" + k: v for k, v in arrays.items()}], core_ids=[0])
    return r.results[0]["out_x"]
```

```python
from contextlib import ExitStack

import concourse.bass as bass
from concourse import mybir

P = 128
B, S, D, C = 4, 256, 256, 128
T = B * S
NT = T // P
KD = D // P
HALF = T // 2
TPH = HALF // P
LN_EPS = 1e-5
ROUND = 12582912.0

ALU = mybir.AluOpType
ACT = mybir.ActivationFunctionType
AX = mybir.AxisListType
F32 = mybir.dt.float32
BF16 = mybir.dt.bfloat16
U16 = mybir.dt.uint16
U32 = mybir.dt.uint32
I32 = mybir.dt.int32
F32R = mybir.dt.float32r


class Steps:

    def __init__(self, eng, sem):
        self.eng, self.sem, self.n = eng, sem, 0

    def mark(self, ins):
        ins.then_inc(self.sem, 1)
        self.n += 1

    def settle(self):
        self.eng.wait_ge(self.sem, self.n)

    def link(self, ins):
        self.mark(ins)
        self.settle()


def build(nc, a, out):
    with ExitStack() as ctx:
        def sb(name, shape, dt=F32):
            return ctx.enter_context(nc.sbuf_tensor(name, shape, dt))

        s_out = ctx.enter_context(nc.semaphore("out_stored"))
        held = []

        def sem(name):
            held.append(nc.alloc_semaphore(name=name))
            return held[-1]

        def give_back():
            with nc.Block(f"give_back_{len(held)}") as block:
                @block.gpsimd
                def _(pool):
                    nc.clear_and_free_semaphores(held)
            held.clear()

        ps = ctx.enter_context(nc.psum_tensor("ps", [P, 8, 512], F32))
        psb = ps[:, :, :].rearrange("p b n -> p (b n)").bitcast(BF16).rearrange("p (b n) -> p b n", b=8)

        x = sb("x", [P, NT, D])
        h = sb("h", [P, NT, D])
        hT = sb("hT", [P, KD, T])
        ctxT = sb("ctxT", [P, T])
        yssm = sb("yssm", [P, KD, T])
        ident = sb("ident", [P, P])
        identb = sb("identb", [P, P], BF16)
        iota = sb("iota", [P, 16])
        tg = sb("tg", [P, 8])
        lnst = sb("lnst", [P, NT, 6])
        lnmv = sb("lnmv", [P, NT, 2])
        lnsd = sb("lnsd", [P, 2, NT])
        W1q = sb("W1q", [P, KD, 4 * D], BF16)
        W2q = sb("W2q", [P, 4 * D // P, D], BF16)
        regA = sb("regA", [P, 12288])
        g8 = sb("g8", [P, 8])
        rt3, rt7 = sb("rt3", [P, KD, 16]), sb("rt7", [P, KD, 8])
        bias3 = sb("bias3", [P, 16])
        WORDS_B = WORDS_C = 13056
        low = ExitStack()
        regB = low.enter_context(nc.sbuf_tensor("regB", [P, WORDS_B], F32))
        high = ExitStack()
        regC = high.enter_context(nc.sbuf_tensor("regC", [P, WORDS_C], F32, side="right"))

        class Arena:

            def __init__(self, *regs):
                self.regs = [[r, 0, r.shape[1]] for r in regs]

            def take(self, shape, dt=F32):
                n = 1
                for s in shape:
                    n *= s
                words = n if dt in (F32, I32, U32) else (n + 1) // 2
                words = (words + 7) // 8 * 8
                for r in self.regs:
                    if r[1] + words <= r[2]:
                        v = r[0][:, r[1]:r[1] + (n if dt in (F32, I32, U32) else n // 2)]
                        r[1] += words
                        break
                else:
                    raise ValueError(f"arena full for {shape}: {[(q[1], q[2]) for q in self.regs]}")
                if dt != F32:
                    v = v.bitcast(dt)
                if len(shape) > 1:
                    names = "abcde"[:len(shape)]
                    v = v.rearrange(f"p ({' '.join(names)}) -> p {' '.join(names)}",
                                    **{k: s for k, s in zip(names[1:], shape[1:])})
                return v

        def norm_on_vector(dve, v, s_var, s_sd, s_h, interleave=False, src=x, dst=h):
            for t in range(NT):
                v.mark(nc.vector.bn_stats(lnst[:, t, :], src[:, t, :]))
            v.settle()
            for t in range(NT):
                v.mark(nc.vector.bn_aggr(lnmv[:, t, :], lnst[:, t, :]))
            v.settle()
            nc.vector.tensor_scalar(lnsd[:, 0, :], lnmv[:, :, 1], LN_EPS, None, ALU.add).then_inc(s_var, 1)
            dve.wait_ge(s_sd, 1)
            v.link(nc.vector.reciprocal(lnsd[:, 0, :], lnsd[:, 1, :]))
            for t in range(NT):
                o, i = dst[:, t, :], src[:, t, :]
                if interleave:
                    o = o.rearrange("p (a j) -> p j a", a=2)
                    i = i.rearrange("p (j a) -> p j a", a=2)
                nc.vector.tensor_scalar(o, i, lnmv[:, t, 0:1], lnsd[:, 0, t:t + 1],
                                        ALU.subtract, ALU.mult).then_inc(s_h, 1)

        def norm_on_scalar(act, s_var, s_sd):
            act.wait_ge(s_var, 1)
            nc.scalar.activation(lnsd[:, 1, :], lnsd[:, 0, :], ACT.Sqrt).then_inc(s_sd, 1)

        def turn_on_tensor(pe, src, bank0, s_src, src_at, s_turned, dst_psum=None, idn=None, after=None):
            pt = ps if dst_psum is None else dst_psum
            for i in range(NT // 2):
                for t in (2 * i, 2 * i + 1):
                    if s_src is not None:
                        pe.wait_ge(s_src, src_at(t))
                    for k in range(KD):
                        o = pt[:, bank0 + i, k * 2 * P + (t % 2) * P:k * 2 * P + (t % 2) * P + P]
                        last = nc.tensor.transpose(o, src[:, t, k * P:(k + 1) * P], (idn or ident)[:, :])
                last.then_inc(s_turned, 1)
                if after is not None:
                    after(i)

        def turned(bank, pt=None):
            return (ps if pt is None else pt)[:, bank, 0:KD * 2 * P].rearrange("p (k n) -> p k n", k=KD)

        NHC = 2048 // P
        WG, WU, WD = (regA[:, i * 4096:(i + 1) * 4096] for i in range(3))
        raw = [regB[:, i * 2048:(i + 1) * 2048].bitcast(I32) for i in range(3)]
        scl = [regB[:, (3 + i) * 2048:(4 + i) * 2048] for i in range(3)]
        WDv = WD.rearrange("p (c a n) -> p c a n", c=NHC // 2, a=2)

        def load_packed(sp, s_pk):
            for i, nm in enumerate(("gate", "up", "down")):
                sp.dma_start(raw[i], a[f"L0_{nm}_pk"]).then_inc(s_pk[i], 16)
                for g in range(8):
                    sp.dma_start(scl[i][16 * g:16 * g + 16, :],
                                 a[f"L0_{nm}_sc"][g, :].partition_broadcast(16)).then_inc(s_pk[i], 16)

        def dequant_on_vector(dve, v, dq, s_pk, s_nib, s_dq, pieces):
            val, mag, tmp = dq
            for n in pieces:
                i, par = divmod(n, 2)
                dve.wait_ge(s_pk[i], 16 * 9)
                lo16 = raw[i].bitcast(U16).rearrange("p (n two) -> p n two", two=2)[:, :, 0]
                if n >= 1:
                    dve.wait_ge(s_nib, n)
                if n >= 2:
                    dve.wait_ge(s_dq, n - 1)
                o = val[:, par, :]
                v.mark(nc.vector.tensor_scalar(mag, lo16, 4 * par, 7, ALU.logical_shift_right, ALU.bitwise_and))
                v.link(nc.vector.tensor_scalar(o, lo16, 8 << (4 * par), 12 - 4 * par,
                                               ALU.bitwise_and, ALU.logical_shift_left))
                v.link(nc.vector.tensor_scalar(tmp, mag, 64.0, float(0x3F00), ALU.mult, ALU.add))
                v.link(nc.vector.tensor_scalar(mag, mag, float(0x3F00), float(0x7F00), ALU.mult, ALU.min))
                v.link(nc.vector.tensor_tensor(tmp, tmp, mag, ALU.min))
                nc.vector.tensor_tensor(o, o, tmp, ALU.bitwise_or).then_inc(s_nib, 1)

        def dequant_on_gpsimd(pool, dq, s_nib, s_dq):
            for i, w in enumerate((WG, WU, WD)):
                for par in range(2):
                    pool.wait_ge(s_nib, 2 * i + par + 1)
                    code = dq[0][:, par, :].bitcast(BF16)
                    if i < 2:
                        o, q, sc = w[:, par * 2048:(par + 1) * 2048], code, scl[i]
                    else:
                        o = WDv[:, :, par, :]
                        q = code.rearrange("p (c n) -> p c n", n=D)
                        sc = scl[i].rearrange("p (c n) -> p c n", n=D)
                    nc.gpsimd.tensor_tensor(o, q, sc, ALU.mult).then_inc(s_dq, 1)

        def stage0():
            ar = Arena(regC)
            qT, kT = ar.take([T]), ar.take([T])
            att, attT = ar.take([NT, D]), ar.take([KD, T])
            w = ar.take([2, C])
            bqk = ar.take([2])
            nmx, den = ar.take([NT]), ar.take([NT])
            dq = [ar.take([2, 4 * HALF], U16), ar.take([4 * HALF], U16), ar.take([4 * HALF], U16)]
            s_c, s_x, s_in = sem("s0_context"), sem("s0_x"), sem("s0_constants")
            s_var, s_sd, s_h = sem("s0_var"), sem("s0_sd"), sem("s0_h")
            s_proj, s_qk, s_en, s_mx = sem("s0_proj"), sem("s0_qk"), sem("s0_en"), sem("s0_mx")
            s_exp, s_att, s_hTp, s_hT = sem("s0_exp"), sem("s0_att"), sem("s0_hTp"), sem("s0_hT")
            s_pk, s_nib, s_dq = [sem(f"s0_pk{i}") for i in range(3)], sem("s0_nib"), sem("s0_dq")
            s_aTp, s_aT, s_mix, s_v = sem("s0_aTp"), sem("s0_aT"), sem("s0_mix"), sem("s0_v")
            s_tg = sem("s0_gates")
            with nc.Block("stage0") as block:
                @block.sync
                def _(sp):
                    sp.dma_start(x[:, :, :], a["x"].rearrange("b (h p) d -> p (b h) d", p=P)).then_inc(s_x, 16)
                    sp.dma_start(w, a["L0_qkT"]).then_inc(s_c, 16)
                    sp.dma_start(bqk, a["L0_bqk"]).then_inc(s_c, 16)
                    sp.dma_start(ctxT[:, :], a["ctxT"]).then_inc(s_c, 16)
                    sp.dma_start(ident[:, :], a["ident"]).then_inc(s_in, 16)
                    sp.dma_start(g8[:, 0:4], a["g_xattn"].partition_broadcast(P)).then_inc(s_in, 16)
                    sp.dma_start(g8[:, 4:8], a["g_ffn"].partition_broadcast(P)).then_inc(s_in, 16)
                    sp.dma_start(iota[:, :], a["iota"].partition_broadcast(P)).then_inc(s_in, 16)
                    load_packed(sp, s_pk)

                @block.scalar
                def _(act):
                    norm_on_scalar(act, s_var, s_sd)
                    act.wait_ge(s_in, 64)
                    nc.scalar.activation(tg[:, :], g8[:, :], ACT.Tanh).then_inc(s_tg, 1)
                    act.wait_ge(s_c, 48)
                    for i, dst in enumerate((qT, kT)):
                        for hf in range(2):
                            act.wait_ge(s_proj, 2 * i + hf + 1)
                            nc.scalar.activation(dst[:, hf * HALF:(hf + 1) * HALF], ps[:, 2 * i + hf, :],
                                                 ACT.Identity, bias=bqk[:, i:i + 1]).then_inc(s_qk, 1)
                    for t in range(NT):
                        act.wait_ge(s_mx, t // 2 + 1)
                        nc.scalar.activation(att[:, t, :], ps[:, 4 + t // 2, (t % 2) * S:(t % 2 + 1) * S], ACT.Exp,
                                             bias=nmx[:, t:t + 1], accum_out=den[:, t:t + 1]).then_inc(s_exp, 1)
                    for i in range(NT // 2):
                        act.wait_ge(s_hTp, i + 1)
                        nc.scalar.copy(hT[:, :, i * 2 * P:(i + 1) * 2 * P], turned(i)).then_inc(s_hT, 1)

                @block.tensor
                def _(pe):
                    pe.wait_ge(s_c, 48)
                    for i in range(2):
                        for hf in range(2):
                            nc.tensor.matmul(ps[:, 2 * i + hf, :], w[:, i, :], ctxT[:, hf * HALF:(hf + 1) * HALF],
                                             start=True, stop=True).then_inc(s_proj, 1)
                    pe.wait_ge(s_qk, 4)
                    for t in range(NT):
                        b = t // 2
                        e = nc.tensor.matmul(ps[:, 4 + b, (t % 2) * S:(t % 2 + 1) * S], qT[:, t * P:(t + 1) * P],
                                             kT[:, b * S:(b + 1) * S], start=True, stop=True)
                        if t % 2:
                            e.then_inc(s_en, 1)
                    pe.wait_ge(s_in, 64)
                    turn_on_tensor(pe, h, 0, s_h, lambda t: t + 1, s_hTp)
                    pe.wait_ge(s_exp, NT)
                    turn_on_tensor(pe, att, 4, s_att, lambda t: t + 1, s_aTp)
                    pe.wait_ge(s_hT, NT // 2)
                    for t in range(NT):
                        b = t // 2
                        pe.wait_ge(s_aT, b + 1)
                        for k in range(KD):
                            m = nc.tensor.matmul(ps[:, b, (t % 2) * S:(t % 2 + 1) * S], hT[:, k, t * P:(t + 1) * P],
                                                 attT[:, k, b * S:(b + 1) * S], start=k == 0, stop=k == KD - 1)
                        if t % 2:
                            m.then_inc(s_mix, 1)

                @block.vector
                def _(dve):
                    v = Steps(dve, s_v)
                    dve.wait_ge(s_x, 16)
                    norm_on_vector(dve, v, s_var, s_sd, s_h)
                    for b in range(B):
                        dve.wait_ge(s_en, b + 1)
                        nc.vector.tensor_reduce(nmx[:, 2 * b:2 * b + 2], ps[:, 4 + b, :].rearrange("p (t m) -> p t m", t=2),
                                                AX.X, ALU.max, negate=True).then_inc(s_mx, 1)
                    dequant_on_vector(dve, v, dq, s_pk, s_nib, s_dq, range(0, 1))
                    for t in range(NT):
                        dve.wait_ge(s_exp, t + 1)
                        v.link(nc.vector.reciprocal(den[:, t:t + 1], den[:, t:t + 1]))
                        nc.vector.tensor_scalar(att[:, t, :], att[:, t, :], den[:, t:t + 1], None,
                                                ALU.mult).then_inc(s_att, 1)
                    for i in range(NT // 2):
                        dve.wait_ge(s_aTp, i + 1)
                        nc.vector.tensor_copy(attT[:, :, i * 2 * P:(i + 1) * 2 * P], turned(4 + i)).then_inc(s_aT, 1)
                    dequant_on_vector(dve, v, dq, s_pk, s_nib, s_dq, range(1, 2))
                    dve.wait_ge(s_in, 64)
                    nc.vector.tensor_copy(identb[:, :], ident[:, :])
                    dve.wait_ge(s_tg, 1)
                    for b in range(B):
                        dve.wait_ge(s_mix, b + 1)
                        xb = x[:, 2 * b:2 * b + 2, :]
                        nc.vector.scalar_tensor_tensor(xb, ps[:, b, :].rearrange("p (t m) -> p t m", t=2),
                                                       tg[:, 0:1], xb, ALU.mult, ALU.add)
                    dequant_on_vector(dve, v, dq, s_pk, s_nib, s_dq, range(2, 6))

                @block.gpsimd
                def _(pool):
                    dequant_on_gpsimd(pool, dq, s_nib, s_dq)

        NST, DTR, TAPS = 16, 8, 4
        NBC = 2 * NST

        arS = Arena(regC)
        u_ssm, dt, du = arS.take([KD, T]), arS.take([KD, T]), arS.take([KD, T])
        cw = arS.take([KD, TAPS + 3])
        alog = arS.take([KD, NST])
        bcs = arS.take([T], BF16)
        selb = arS.take([NBC], BF16)

        L = (0.810930216216, -0.288527111915, 0.132609761683, -0.0676876229793, 0.0366112232653, -0.0205713852149,
             0.0118477560374, -0.0067441046525, 0.00401169096238, -0.00325434358357, 0.00198669635839)
        LDEG = len(L) - 1

        def stage1():
            ar = Arena(regC[:, arS.regs[0][1]:])
            gel = ar.take([2, HALF])
            itm = ar.take([2, HALF])
            HB = B // 2
            RD = 6
            arB, arP = Arena(regB, ar.regs[0][0][:, ar.regs[0][1]:]), Arena(regB)
            dA = arB.take([RD, KD, HB, S])
            dBu, hs = arB.take([KD, HALF]), arB.take([KD, HALF])
            hc = arB.take([2, KD, HALF])
            LP = S + TAPS - 1
            xpad = arP.take([KD, B, LP])
            sA, sB = arP.take([T]), arP.take([T])
            zpos = arP.take([KD, T])
            bcf = arP.take([T])
            in_w = arB.take([KD * P])
            xp_w = arB.take([KD, 3 * NBC + DTR])
            dt_w = arB.take([D])
            dtl = arB.take([T])
            bc1, bc2 = arB.take([T], BF16), arB.take([T], BF16)
            self_ = arB.take([NBC])
            s_var, s_sd, s_h, s_hTp, s_hT = (sem("s1_" + n) for n in ("var", "sd", "h", "hTp", "hT"))
            s_gu, s_gel, s_itm, s_down, s_add, s_v = (sem("s1_" + n) for n in ("gu", "gel", "itm", "down", "add", "v"))
            s_b, s_c, s_bu, s_dA, s_ready, s_scan, s_hc, s_y = (
                sem("s1_" + n) for n in ("brow", "crow", "bu", "dA", "ready", "scan", "hc", "y"))
            s_w, s_xi, s_xc, s_u, s_z, s_xp, s_bcs, s_pre, s_e, s_dt, s_max, s_A, s_skip = (
                sem("m_" + n) for n in "w xi xc u z xp bcs pre e dt max A skip".split())
            NU = 2 * NHC
            NGR = 2 * NST
            SP = 3
            SCAN0 = SP + 3 * KD
            LAST = NU - 2
            unit_of = [SCAN0 + g * (LAST - SCAN0) // NGR for g in range(NGR)]

            def groups_at(u):
                return [g for g in range(NGR) if unit_of[g] == u]

            def half(v, k, hf):
                return v[:, k, hf * HALF:(hf + 1) * HALF]

            pair = ps[:, 6:8, :].rearrange("p b n -> p (b n)")

            with nc.Block("stage1") as block:
                @block.sync
                def _(sp):
                    for dst, nm in ((in_w, "m_in"), (cw, "m_cw"), (alog, "m_alog"), (xp_w, "m_xp"),
                                    (dt_w[3 * NBC:3 * NBC + DTR, :], "m_dtw"), (self_[0:3 * NBC, :], "m_sel")):
                        sp.dma_start(dst, a[nm]).then_inc(s_w, 16)

                @block.scalar
                def _(act):
                    def decays(g):
                        hf, n = divmod(g, NST)
                        if g == 0:
                            act.wait_ge(s_ready, 1)
                        if g >= RD:
                            act.wait_ge(s_scan, g - RD + 1)
                        for k in range(KD):
                            src = half(dt, k, hf).rearrange("p (b l) -> p b l", b=HB)[:, :, 1:S]
                            nc.scalar.activation(dA[:, g % RD, k, :, 1:S], src, ACT.Exp,
                                                 scale=alog[:, k, n:n + 1]).then_inc(s_dA, 1)

                    def step_exponent(k):
                        act.wait_ge(s_pre, k + 1)
                        w = (sA, sB)[k]
                        nc.scalar.activation(w, pair, ACT.Abs, bias=cw[:, k, TAPS + 1:TAPS + 2]).then_inc(s_e, 1)
                        act.wait_ge(s_e, k + 1)
                        nc.scalar.activation(dt[:, k, :], w, ACT.Exp, scale=-1.0).then_inc(s_dt, 1)

                    norm_on_scalar(act, s_var, s_sd)
                    for k in range(KD):
                        act.wait_ge(s_xi, k + 1)
                        nc.scalar.copy(xpad[:, k, :, TAPS - 1:LP], pair.rearrange("p (b l) -> p b l", b=B)).then_inc(s_xc, 1)
                    for i in range(NT // 2):
                        act.wait_ge(s_hTp, i + 1)
                        nc.scalar.copy(hT[:, :, i * 2 * P:(i + 1) * 2 * P], turned(2 + i)).then_inc(s_hT, 1)
                    for k in range(KD):
                        act.wait_ge(s_u, k + 1)
                        nc.scalar.activation(u_ssm[:, k, :], u_ssm[:, k, :], ACT.Silu).then_inc(s_z, 1)
                    issued = 0
                    for u in range(0, NU, 2):
                        for w in (u, u + 1):
                            act.wait_ge(s_gu, w + 1)
                            if w >= 2:
                                act.wait_ge(s_itm, w - 1)
                            nc.scalar.activation(gel[:, w % 2, :], ps[:, 2 + 2 * (w % 2), :],
                                                 ACT.Gelu_apprx_tanh).then_inc(s_gel, 1)
                        if u == 0:
                            nc.scalar.activation(alog, alog, ACT.Exp).then_inc(s_A, 1)
                        if u in (2, 4):
                            step_exponent(u // 2 - 1)
                        if u >= SCAN0 - 2:
                            due = [g for g in range(NGR) if unit_of[g] <= u + 3]
                            for g in due[issued:]:
                                decays(g)
                            issued = len(due)

                @block.tensor
                def _(pe):
                    def row(g, j):
                        hf, n = divmod(g, NST)
                        if g == 0:
                            pe.wait_ge(s_max, KD)
                        else:
                            pe.wait_ge((s_bu, s_hc)[j], g)
                        r = j * NST + n
                        nc.tensor.matmul(ps[:, 6 + j, :], selb[0:3 * NBC, r:r + 1].broadcast_to([3 * NBC, P]),
                                         bcs[0:3 * NBC, hf * HALF:(hf + 1) * HALF],
                                         start=True, stop=True).then_inc((s_b, s_c)[j], 1)

                    def project_context(k):
                        if k >= 1:
                            pe.wait_ge(s_xc, k)
                        for hf in range(2):
                            m = nc.tensor.matmul(ps[:, 6 + hf, :], in_w[:, k * P:(k + 1) * P],
                                                 ctxT[:, hf * HALF:(hf + 1) * HALF], start=True, stop=True)
                        m.then_inc(s_xi, 1)

                    def project_bc():
                        pe.wait_ge(s_z, KD)
                        for hf in range(2):
                            for k in range(KD):
                                m = nc.tensor.matmul(ps[0:3 * NBC + DTR, 6 + hf, :], xp_w[:, k, :],
                                                     half(u_ssm, k, hf), start=k == 0, stop=k == KD - 1)
                        m.then_inc(s_xp, 1)

                    def project_steps(k):
                        pe.wait_ge(s_bcs, 1)
                        if k >= 1:
                            pe.wait_ge(s_max, k)
                        dtr = slice(3 * NBC, 3 * NBC + DTR)
                        for hf in range(2):
                            m = nc.tensor.matmul(ps[:, 6 + hf, :], dt_w[dtr, k * P:(k + 1) * P],
                                                 dtl[dtr, hf * HALF:(hf + 1) * HALF], start=True, stop=True)
                        m.then_inc(s_pre, 1)

                    pe.wait_ge(s_w, 96)
                    project_context(0)
                    project_context(1)
                    turn_on_tensor(pe, h, 2, s_h, lambda t: t + 1, s_hTp)

                    def gate_up(u):
                        hf, c = divmod(u, NHC)
                        if u < 2:
                            pe.wait_ge(s_hT, NT // 2)
                        else:
                            pe.wait_ge(s_itm, u - 1)
                        for j, w in enumerate((WG, WU)):
                            for k in range(2):
                                m = nc.tensor.matmul(ps[:, 2 + 2 * (u % 2) + j, :],
                                                     w[:, k * 2048 + c * P:k * 2048 + (c + 1) * P],
                                                     hT[:, k, hf * HALF:(hf + 1) * HALF], start=k == 0, stop=k == 1)
                        m.then_inc(s_gu, 1)

                    def down(u):
                        c = u % NHC
                        pe.wait_ge(s_itm, u + 1)
                        if u == NHC:
                            pe.wait_ge(s_add, 1)
                        for t in range(TPH):
                            m = nc.tensor.matmul(ps[:, t // 2, (t % 2) * D:(t % 2 + 1) * D],
                                                 itm[:, u % 2, t * P:(t + 1) * P], WDv[:, c // 2, c % 2, :],
                                                 start=(c == 0 and t % 2 == 0), stop=c == NHC - 1,
                                                 skip_group_check=True)
                        m.then_inc(s_down, 1)

                    gate_up(0)
                    project_bc()
                    for u in range(NU):
                        if u + 1 < NU:
                            gate_up(u + 1)
                        for g in groups_at(u - 1)[1:]:
                            row(g, 1)
                        for g in groups_at(u)[:1]:
                            row(g, 0)
                        if u == SP - 1:
                            project_steps(0)
                        down(u)
                        for g in groups_at(u)[:1]:
                            row(g, 1)
                        for g in groups_at(u)[1:]:
                            row(g, 0)
                        if u == SP:
                            project_steps(1)

                @block.vector
                def _(dve):
                    v = Steps(dve, s_v)
                    norm_on_vector(dve, v, s_var, s_sd, s_h, interleave=True)

                    def convolve(k):
                        dve.wait_ge(s_xc, k + 1)
                        o = u_ssm[:, k, :].rearrange("p (b l) -> p b l", b=B)
                        v.link(nc.vector.tensor_scalar(o, xpad[:, k, :, TAPS - 1:LP], cw[:, k, TAPS - 1:TAPS],
                                                       cw[:, k, TAPS:TAPS + 1], ALU.mult, ALU.add))
                        for q in range(TAPS - 1):
                            ins = nc.vector.scalar_tensor_tensor(o, xpad[:, k, :, q:q + S], cw[:, k, q:q + 1], o,
                                                                 ALU.mult, ALU.add)
                            if q < TAPS - 2:
                                v.link(ins)
                        ins.then_inc(s_u, 1)

                    R = 3 * NBC

                    def split_rows_1():
                        dve.wait_ge(s_xp, 1)
                        v.mark(nc.vector.tensor_copy(dtl[R:R + DTR, :], pair[R:R + DTR, :]))
                        v.link(nc.vector.tensor_copy(bc1[0:R, :], pair[0:R, :]))
                        v.link(nc.vector.tensor_tensor(bcf[0:R, :], pair[0:R, :], bc1[0:R, :], ALU.subtract))
                        v.link(nc.vector.tensor_copy(bc2[0:R, :], bcf[0:R, :]))

                    def split_rows_2():
                        v.link(nc.vector.tensor_tensor(bcf[0:R, :], bcf[0:R, :], bc2[0:R, :], ALU.subtract))
                        v.mark(nc.vector.tensor_copy(bcs[0:NBC, :], bc1[0:NBC, :]))
                        v.mark(nc.vector.tensor_copy(bcs[NBC:2 * NBC, :], bc2[NBC:2 * NBC, :]))
                        v.mark(nc.vector.tensor_copy(bcs[2 * NBC:R, :], bcf[2 * NBC:R, :]))
                        v.settle()
                        dve.sem_inc(s_bcs, 1)

                    def softplus(k, part):
                        t, q, w = dt[:, k, :], du[:, k, :], (sA, sB)[k]
                        if part == 0:
                            dve.wait_ge(s_e, k + 1)
                            nc.vector.tensor_scalar(zpos[:, k, :], pair, cw[:, k, TAPS + 1:TAPS + 2], 0.0,
                                                    ALU.add, ALU.max).then_inc(s_max, 1)
                            dve.wait_ge(s_dt, k + 1)
                            v.link(nc.vector.tensor_scalar(q, t, -0.5, None, ALU.add))
                            v.link(nc.vector.tensor_scalar(w, q, L[LDEG], L[LDEG - 1], ALU.mult, ALU.add))
                            v.link(nc.vector.tensor_tensor(w, w, q, ALU.mult))
                        for c in {0: (8, ), 1: (7, 6, 5, 4), 2: (3, 2, 1)}[part]:
                            v.link(nc.vector.scalar_tensor_tensor(w, w, L[c], q, ALU.add, ALU.mult))
                        if part == 2:
                            v.link(nc.vector.scalar_tensor_tensor(w, w, L[0], t, ALU.add, ALU.mult))
                            dve.wait_ge(s_max, k + 1)
                            v.link(nc.vector.tensor_tensor(t, w, zpos[:, k, :], ALU.add))
                            v.link(nc.vector.tensor_tensor(q, t, u_ssm[:, k, :], ALU.mult))

                    v.mark(nc.vector.memset(xpad[:, :, :, 0:TAPS - 1], 0.0))
                    dve.wait_ge(s_w, 96)
                    v.link(nc.vector.tensor_copy(selb[0:3 * NBC, :], self_[0:3 * NBC, :]))
                    convolve(0)
                    convolve(1)

                    def add_half(hf):
                        dve.wait_ge(s_down, NHC * (hf + 1))
                        for i in range(2):
                            xv = x[:, hf * TPH + 2 * i:hf * TPH + 2 * i + 2, :]
                            ins = nc.vector.scalar_tensor_tensor(xv, ps[:, i, :].rearrange("p (t n) -> p t n", t=2),
                                                                 tg[:, 4:5], xv, ALU.mult, ALU.add)
                        ins.then_inc(s_add, 1)

                    def scan_group(g):
                        hf, n = divmod(g, NST)
                        dve.wait_ge(s_b, g + 1)
                        for k in range(KD):
                            v.mark(nc.vector.tensor_tensor(dBu[:, k, :], half(du, k, hf), ps[:, 6, :], ALU.mult))
                        v.settle()
                        dve.sem_inc(s_bu, 1)
                        dve.wait_ge(s_dA, KD * (g + 1))
                        for k in range(KD):
                            v.mark(nc.vector.tensor_tensor_scan(hs[:, k, :], dA[:, g % RD, k].rearrange("p b l -> p (b l)"),
                                                                dBu[:, k, :], 0.0, ALU.mult, ALU.add))
                        v.settle()
                        dve.sem_inc(s_scan, 1)
                        dve.wait_ge(s_c, g + 1)
                        if g >= 2:
                            dve.wait_ge(s_y, g - 1)
                        for k in range(KD):
                            ins = nc.vector.tensor_tensor(hc[:, g % 2, k, :], hs[:, k, :], ps[:, 7, :], ALU.mult)
                        ins.then_inc(s_hc, 1)

                    def gated(u):
                        dve.wait_ge(s_gel, u + 1)
                        if u >= 2:
                            dve.wait_ge(s_down, u - 1)
                        nc.vector.tensor_tensor(itm[:, u % 2, :], gel[:, u % 2, :], ps[:, 3 + 2 * (u % 2), :],
                                                ALU.mult).then_inc(s_itm, 1)

                    gated(0)
                    for u in range(NU):
                        if u == 0:
                            split_rows_1()
                        elif u == 1:
                            split_rows_2()
                        elif u == 2:
                            dve.wait_ge(s_A, 1)
                            v.link(nc.vector.tensor_scalar(alog, alog, -1.0, None, ALU.mult))
                            for k in range(KD):
                                nc.vector.tensor_scalar(yssm[:, k, :], u_ssm[:, k, :], cw[:, k, TAPS + 2:TAPS + 3], None,
                                                        ALU.mult).then_inc(s_skip, 1)
                        elif u < SCAN0:
                            softplus(*divmod(u - SP, 3))
                            if u == SCAN0 - 1:
                                v.link(nc.vector.memset(dA[:, :, :, :, 0:1].rearrange("p a b c d -> p (a b c) d"), 0.0))
                                dve.sem_inc(s_ready, 1)
                        if u == NHC:
                            add_half(0)
                        due = groups_at(u)
                        for g in due[:1]:
                            scan_group(g)
                        if u + 1 < NU:
                            gated(u + 1)
                        for g in due[1:]:
                            scan_group(g)
                    add_half(1)

                @block.gpsimd
                def _(pool):
                    for g in range(NGR):
                        hf, n = divmod(g, NST)
                        pool.wait_ge(s_hc, g + 1)
                        y = yssm[:, :, hf * HALF:(hf + 1) * HALF]
                        if g == 0:
                            pool.wait_ge(s_skip, KD)
                        else:
                            pool.wait_ge(s_y, g)
                        nc.gpsimd.tensor_tensor(y, y, hc[:, g % 2], ALU.add).then_inc(s_y, 1)

        QEPS, QMAX = 1e-6, 127.0

        def stage2():
            ar = Arena(regA, regC)
            fsT = ar.take([KD, T])
            xs, ws = ar.take([KD, T]), ar.take([KD, T])
            q1f, qbf = ar.take([2 * T * KD]), ar.take([2 * T * KD], BF16)
            four = lambda v, n: v.rearrange("p (j t n) -> p j t n", j=2, n=n)
            q1, qb = four(q1f, D), four(qbf, D)
            xqT, wqT = ar.take([KD, T], BF16), ar.take([KD, T], BF16)
            rows = ar.take([2, T])
            am = ar.take([4, NT])
            tok = ar.take([2, 3, NT])
            am2 = ar.take([4, B])
            tok2 = ar.take([2, 3, NT])
            gu = ar.take([B, 2, S])
            sil = ar.take([B, S])
            res = gu.rearrange("p b g s -> p (b g s)")
            aT = ar.take([T])
            as2, wd2 = ar.take([T]), ar.take([T])
            q2, q2b = four(q1f[:, 0:2 * T], P), four(qbf[:, 0:2 * T], P)
            aqT, dqT = ar.take([T], BF16), ar.take([T], BF16)
            (s_var, s_sd, s_h, s_hTp, s_hT, s_fs, s_v, s_am, s_s, s_xs, s_xsP, s_q, s_qP, s_qT, s_mm, s_rowP, s_row,
             s_gus, s_sil, s_am2, s_s2, s_as, s_asP, s_q2, s_q2P, s_q2T, s_mm2, s_row2P, s_row2, s_tokx, s_tokw, s_rec, s_sc) = (
                sem("s2_" + n) for n in ("var sd h hTp hT fs v am s xs xsP q qP qT mm rowP row gus sil am2 s2 as asP q2 "
                                         "q2P q2T mm2 row2P row2 tokx tokw rec sc").split())

            def tiles(v, n):
                return v.rearrange("p (t n) -> p t n", n=n)

            def feature_rows(j):
                return ps[:, 4 * j:4 * j + 4, :].rearrange("p b (t n) -> p (b t) n", t=2)

            def inner_rows(j):
                return ps[:, 2 * j:2 * j + 2, :].rearrange("p b (t n) -> p (b t) n", t=4)

            with nc.Block("stage2") as block:
                @block.sync
                def _(sp):
                    sp.dma_start(fsT, a["fsT"]).then_inc(s_fs, 16)
                    load_w3(sp)

                @block.scalar
                def _(act):
                    norm_on_scalar(act, s_var, s_sd)
                    for i in range(4):
                        act.wait_ge(s_hTp, i + 1)
                        nc.scalar.copy(hT[:, :, i * 2 * P:(i + 1) * 2 * P], turned(i)).then_inc(s_hT, 1)
                    act.wait_ge(s_am, 1)
                    nc.scalar.activation(am[:, 3, :], am[:, 2, :], ACT.Sqrt).then_inc(s_s, 1)

                    def scale_rows(r, src, tk, q):
                        act.wait_ge(s_rec, r + 1)
                        for t in range(NT // 2, NT):
                            nc.scalar.activation(q[:, t, :], src[:, t, :], ACT.Copy,
                                                 scale=tk[:, 2, t:t + 1]).then_inc(s_sc, 1)

                    for j in range(2):
                        scale_rows(j, feature_rows(j), tok[:, j], q1[:, j])
                    for j, dst in enumerate((xqT, wqT)):
                        for i in range(4):
                            act.wait_ge(s_qP, 4 * j + i + 1)
                            nc.scalar.copy(dst[:, :, i * 2 * P:(i + 1) * 2 * P], turned(4 * j + i, psb)).then_inc(s_qT, 1)
                        if j == 0:
                            act.wait_ge(s_rowP, 1)
                            nc.scalar.copy(rows[:, 0, :], ps[:, 0:2, :].rearrange("p b n -> p (b n)")).then_inc(s_row, 1)
                    act.wait_ge(s_gus, 1)
                    nc.scalar.activation(sil, gu[:, :, 0, :], ACT.Silu).then_inc(s_sil, 1)
                    act.wait_ge(s_am2, 1)
                    nc.scalar.activation(am2[:, 3, :], am2[:, 2, :], ACT.Sqrt).then_inc(s_s2, 1)
                    for j in range(2):
                        scale_rows(2 + j, inner_rows(j), tok2[:, j], q2[:, j])
                    for j, dst in enumerate((aqT, dqT)):
                        act.wait_ge(s_q2P, j + 1)
                        nc.scalar.copy(dst, psb[:, 4 + j, 0:T]).then_inc(s_q2T, 1)
                        if j == 0:
                            act.wait_ge(s_row2P, 1)
                            nc.scalar.copy(rows[:, 1, :], ps[:, 6:8, :].rearrange("p b n -> p (b n)")).then_inc(s_row2, 1)

                @block.tensor
                def _(pe):
                    turn_on_tensor(pe, h, 0, s_h, lambda t: t + 1, s_hTp)

                    def turn_back(src, bank0, sem_src, at):
                        pe.wait_ge(sem_src, at)
                        for t in range(NT):
                            for k in range(KD):
                                m = nc.tensor.transpose(ps[:, bank0 + t // 2, (t % 2) * D + k * P:(t % 2) * D + (k + 1) * P],
                                                        src[:, k, t * P:(t + 1) * P], ident[:, :])
                        m.then_inc(s_xsP, 1)

                    pe.wait_ge(s_hT, 4)
                    turn_back(xs, 0, s_xs, 1)
                    turn_back(ws, 4, s_xs, 2)
                    for j in range(2):
                        pe.wait_ge(s_q, j + 1)
                        turn_on_tensor(pe, qb[:, j], 4 * j, None, None, s_qP, dst_psum=psb, idn=identb)
                        if j == 0:
                            pe.wait_ge(s_tokx, 1)
                            pe.wait_ge(s_qT, 4)
                            for t in range(NT):
                                m = nc.tensor.matmul(ps[:, t // 4, (t % 4) * P:(t % 4 + 1) * P],
                                                     tok[:, 0, 1, t:t + 1].broadcast_to([P, P]), ident[:, :],
                                                     start=True, stop=True)
                            m.then_inc(s_rowP, 1)
                    pe.wait_ge(s_qT, 8)
                    pe.wait_ge(s_row, 1)
                    for b in range(B):
                        for o in range(2):
                            for k in range(KD):
                                m = nc.tensor.matmul(ps[:, b, o * S:(o + 1) * S],
                                                     wqT[:, k, (2 * b + o) * P:(2 * b + o + 1) * P],
                                                     xqT[:, k, b * S:(b + 1) * S], start=k == 0, stop=k == KD - 1)
                        m.then_inc(s_mm, 1)
                    pe.wait_ge(s_gus, 1)
                    for j, src in enumerate((as2, wd2)):
                        pe.wait_ge(s_as, j + 1)
                        for t in range(NT):
                            m = nc.tensor.transpose(ps[:, 2 * j + t // 4, (t % 4) * P:(t % 4 + 1) * P],
                                                    src[:, t * P:(t + 1) * P], ident[:, :])
                        m.then_inc(s_asP, 1)
                    for j in range(2):
                        if j == 1:
                            pe.wait_ge(s_tokw, 1)
                            for t in range(NT):
                                m = nc.tensor.matmul(ps[:, 6 + t // 4, (t % 4) * P:(t % 4 + 1) * P],
                                                     tok2[:, 1, 1, t:t + 1].broadcast_to([P, P]), ident[:, :],
                                                     start=True, stop=True)
                            m.then_inc(s_row2P, 1)
                        pe.wait_ge(s_q2, j + 1)
                        for t in range(NT):
                            m = nc.tensor.transpose(psb[:, 4 + j, t * P:(t + 1) * P], q2b[:, j, t, :], identb[:, :])
                        m.then_inc(s_q2P, 1)
                    pe.wait_ge(s_q2T, 2)
                    for t in range(NT):
                        b = t // 2
                        m = nc.tensor.matmul(ps[:, b, (t % 2) * D:(t % 2 + 1) * D], aqT[:, t * P:(t + 1) * P],
                                             dqT[:, b * S:(b + 1) * S], start=True, stop=True)
                        if t % 2:
                            m.then_inc(s_mm2, 1)

                @block.vector
                def _(dve):
                    v = Steps(dve, s_v)
                    norm_on_vector(dve, v, s_var, s_sd, s_h)

                    def channel_scales(m, s_ready, s_root):
                        v.link(nc.vector.tensor_scalar(m[:, 0:2, :], m[:, 0:2, :], QEPS, None, ALU.max))
                        v.link(nc.vector.reciprocal(m[:, 1, :], m[:, 1, :]))
                        nc.vector.tensor_tensor(m[:, 2, :], m[:, 0, :], m[:, 1, :], ALU.mult).then_inc(s_ready, 1)
                        dve.wait_ge(s_root, 1)
                        v.link(nc.vector.tensor_scalar(m[:, 2, :], m[:, 3, :], QEPS, None, ALU.max))
                        v.link(nc.vector.reciprocal(m[:, 0, :], m[:, 2, :]))

                    def row_scales(tk, amax_src, s_ready=None):
                        v.link(nc.vector.tensor_reduce(tk[:, 0, :], amax_src, AX.X, ALU.max, apply_absolute_value=True))
                        v.link(nc.vector.tensor_scalar(tk[:, 1, :], tk[:, 0, :], QEPS, 1.0 / QMAX, ALU.max, ALU.mult))
                        nc.vector.reciprocal(tk[:, 2, :], tk[:, 1, :]).then_inc(s_rec, 1)
                        if s_ready is not None:
                            nc.vector.tensor_copy(tk[:, 0, :], tk[:, 1, :]).then_inc(s_ready, 1)

                    def round_rows(r, src, tk, q, qb_, s_done):
                        dve.wait_ge(s_rec, r + 1)
                        for t in range(NT // 2):
                            v.mark(nc.vector.tensor_scalar(q[:, t, :], src[:, t, :], tk[:, 2, t:t + 1], None, ALU.mult))
                        v.settle()
                        dve.wait_ge(s_sc, NT // 2 * (r + 1))
                        v.link(nc.vector.tensor_scalar(q, q, -QMAX, ROUND, ALU.max, ALU.add))
                        nc.vector.tensor_scalar(qb_, q, -ROUND, QMAX, ALU.add, ALU.min).then_inc(s_done, 1)

                    segs = lambda w: w.rearrange("p k (b n) -> p (k b) n", b=B)
                    dve.wait_ge(s_fs, 16)
                    v.mark(nc.vector.tensor_reduce(am[:, 1, :], segs(fsT), AX.X, ALU.max, apply_absolute_value=True))
                    dve.wait_ge(s_hT, 4)
                    v.link(nc.vector.tensor_reduce(am[:, 0, :], segs(hT[:, :, :]), AX.X, ALU.max,
                                                   apply_absolute_value=True))
                    channel_scales(am, s_am, s_s)
                    nc.vector.tensor_tensor(segs(xs), segs(hT[:, :, :]), am[:, 0, :].unsqueeze(2).broadcast_to([P, NT, S]),
                                            ALU.mult).then_inc(s_xs, 1)
                    nc.vector.tensor_tensor(segs(ws), segs(fsT), am[:, 2, :].unsqueeze(2).broadcast_to([P, NT, S]),
                                            ALU.mult).then_inc(s_xs, 1)
                    for j in range(2):
                        dve.wait_ge(s_xsP, j + 1)
                        src = feature_rows(j)
                        row_scales(tok[:, j], src, s_tokx if j == 0 else None)
                        round_rows(j, src, tok[:, j], q1[:, j], qb[:, j], s_q)
                    dve.wait_ge(s_row, 1)
                    for b in range(B):
                        dve.wait_ge(s_mm, b + 1)
                        for o in range(2):
                            v.mark(nc.vector.scalar_tensor_tensor(
                                gu[:, b, o, :], ps[:, b, o * S:(o + 1) * S], tok[:, 1, 1, 2 * b + o:2 * b + o + 1],
                                rows[:, 0, b * S:(b + 1) * S], ALU.mult, ALU.mult))
                    v.settle()
                    v.link(nc.vector.tensor_reduce(am2[:, 1, :], tiles(ctxT[:, :], S), AX.X, ALU.max,
                                                   apply_absolute_value=True))
                    v.settle()
                    dve.sem_inc(s_gus, 1)
                    dve.wait_ge(s_sil, 1)
                    v.link(nc.vector.tensor_tensor(tiles(aT, S), sil, gu[:, :, 1, :], ALU.mult))
                    v.link(nc.vector.tensor_reduce(am2[:, 0, :], tiles(aT, S), AX.X, ALU.max, apply_absolute_value=True))
                    channel_scales(am2, s_am2, s_s2)
                    nc.vector.tensor_tensor(tiles(as2, S), tiles(aT, S), am2[:, 0, :].unsqueeze(2).broadcast_to([P, B, S]),
                                            ALU.mult).then_inc(s_as, 1)
                    nc.vector.tensor_tensor(tiles(wd2, S), tiles(ctxT[:, :], S),
                                            am2[:, 2, :].unsqueeze(2).broadcast_to([P, B, S]), ALU.mult).then_inc(s_as, 1)
                    for j in range(2):
                        dve.wait_ge(s_asP, j + 1)
                        src = inner_rows(j)
                        row_scales(tok2[:, j], src, s_tokw if j == 1 else None)
                        round_rows(2 + j, src, tok2[:, j], q2[:, j], q2b[:, j], s_q2)
                    dve.wait_ge(s_row2, 1)
                    for b in range(B):
                        dve.wait_ge(s_mm2, b + 1)
                        for o in range(2):
                            t = 2 * b + o
                            v.mark(nc.vector.scalar_tensor_tensor(
                                res[:, t * D:(t + 1) * D], ps[:, b, o * D:(o + 1) * D], tok2[:, 0, 1, t:t + 1],
                                rows[:, 1, b * S:(b + 1) * S], ALU.mult, ALU.mult))
                        v.settle()
                        xb = x[:, 2 * b:2 * b + 2, :]
                        nc.vector.scalar_tensor_tensor(xb, tiles(res[:, 2 * b * D:2 * (b + 1) * D], D), tg[:, 1:2], xb,
                                                       ALU.mult, ALU.add)

        def stage6():
            ar = Arena(regC)
            sil, gated = ar.take([NT, D]), ar.take([NT, D])
            s_var, s_sd, s_h, s_sil, s_gt, s_gP, s_v = (sem("s6_" + n) for n in ("var sd h sil gt gP v").split())
            with nc.Block("stage6") as block:
                @block.scalar
                def _(act):
                    norm_on_scalar(act, s_var, s_sd)
                    for t in range(NT):
                        act.wait_ge(s_h, t + 1)
                        nc.scalar.activation(sil[:, t, :], h[:, t, :], ACT.Silu).then_inc(s_sil, 1)

                @block.tensor
                def _(pe):
                    for b in range(B):
                        pe.wait_ge(s_gt, 2 * b + 2)
                        for l in range(2):
                            for k in range(KD):
                                m = nc.tensor.transpose(ps[:, b, l * D + k * P:l * D + (k + 1) * P],
                                                        gated[:, 2 * b + k, l * P:(l + 1) * P], ident[:, :])
                        m.then_inc(s_gP, 1)

                @block.vector
                def _(dve):
                    v = Steps(dve, s_v)
                    norm_on_vector(dve, v, s_var, s_sd, s_h)
                    for b in range(B):
                        for k in range(KD):
                            t = 2 * b + k
                            dve.wait_ge(s_sil, t + 1)
                            nc.vector.tensor_tensor(gated[:, t, :], sil[:, t, :], yssm[:, k, b * S:(b + 1) * S],
                                                    ALU.mult).then_inc(s_gt, 1)
                    for b in range(B):
                        dve.wait_ge(s_gP, b + 1)
                        xb = x[:, 2 * b:2 * b + 2, :]
                        nc.vector.scalar_tensor_tensor(xb, ps[:, b, :].rearrange("p (t m) -> p t m", t=2),
                                                       tg[:, 3:4], xb, ALU.mult, ALU.add)

        s_w3, s_w7 = (ctx.enter_context(nc.semaphore(n)) for n in ("w3_loaded", "w7_loaded"))
        NE3, NE7, F7 = 16, 8, 176
        NC3, NC7 = NE3 + 1, NE7 * F7 // P
        UW = 6 * P
        W3 = regB[:, 0:NC3 * UW].rearrange("p (c n) -> p c n", n=UW)
        W7 = regA[:, 0:NC7 * UW].rearrange("p (c n) -> p c n", n=UW)
        RING = 3
        LOROW = 32

        def load_w3(sp):
            sp.dma_start(W3, a["L1_w"]).then_inc(s_w3, 16)
            sp.dma_start(rt3[:, :, :], a["L1_router"]).then_inc(s_w3, 16)
            sp.dma_start(bias3[:, :], a["L1_bias"].partition_broadcast(P)).then_inc(s_w3, 16)

        def load_w7(sp):
            sp.dma_start(W7, a["L3_w"]).then_inc(s_w7, 16)
            sp.dma_start(rt7[:, :, :], a["L3_router"]).then_inc(s_w7, 16)

        BLK, FF = 32, 4 * D

        def blocks(w):
            return w.rearrange("p (n k) -> p n k", k=BLK)

        def mx_scales(v, src, am):
            n = src.shape[1]
            v.link(nc.vector.tensor_reduce(am[:, 0, 0:n], src, AX.X, ALU.max, apply_absolute_value=True))
            e = am[:, 0, 0:n].bitcast(I32)
            v.link(nc.vector.tensor_scalar(e, e, 0x7F800000, None, ALU.bitwise_and))
            v.mark(nc.vector.tensor_scalar(am[:, 1, 0:n], am[:, 0, 0:n], 2.0 ** -100, ROUND / 64, ALU.max, ALU.mult))
            v.link(nc.vector.tensor_scalar(am[:, 2, 0:n], am[:, 0, 0:n], 2.0 ** -100, 127 / 64, ALU.max, ALU.mult))

        def mx_wide(am, c, n):
            return am[:, c, 0:n].unsqueeze(2).broadcast_to([P, n, BLK])

        def mx_wide(am, c, n):
            return am[:, c, 0:n].unsqueeze(2).broadcast_to([P, n, BLK])

        def mx_limit(dst, tmp, am, s_done):
            nc.vector.tensor_tensor(dst, tmp, mx_wide(am, 2, tmp.shape[1]), ALU.min).then_inc(s_done, 1)

        def mx_round(v, src, dst, tmp, am, s_done):
            n = src.shape[1]
            v.link(nc.vector.tensor_tensor(tmp, src, mx_wide(am, 1, n), ALU.add))
            v.link(nc.vector.tensor_tensor(tmp, tmp, mx_wide(am, 1, n), ALU.subtract))
            mx_limit(dst, tmp, am, s_done)

        s_w5 = ctx.enter_context(nc.semaphore("w5_loaded"))
        NQ5 = 8
        QW = 2 * FF * KD // NQ5

        def load_w5(sp, raw5):
            sp.dma_start(raw5[:, 0, :], a["L2_W1"]).then_inc(s_w5, 16)
            sp.dma_start(raw5[:, 1, :], a["L2_W2"]).then_inc(s_w5, 16)

        def quantize_w5(dve, v, u, raw5, wq5, tmp5, am5, s_wq):
            piece, step = divmod(u - 2, 2)
            if not 0 <= piece < NQ5:
                return
            part = lambda w: blocks(w.rearrange("p j n -> p (j n)")[:, piece * QW:(piece + 1) * QW])
            if step == 0:
                dve.wait_ge(s_w5, 32)
                if piece >= 1:
                    dve.wait_ge(s_wq, piece)
                mx_scales(v, part(raw5), am5)
            else:
                mx_round(v, part(raw5), part(wq5), blocks(tmp5), am5, s_wq)

        def turn_w5(pe, wq5, s_wq, s_wqT):
            pe.wait_ge(s_wq, NQ5)
            for o in range(FF // P):
                for k in range(KD):
                    m = nc.tensor.transpose(psb[:, 2 + k, o * P:(o + 1) * P], wq5[:, 0, o * D + k * P:o * D + (k + 1) * P],
                                            identb[:, :])
            m.then_inc(s_wqT, 1)
            for k in range(FF // P):
                for o in range(KD):
                    c0 = (k % 4) * D + o * P
                    m = nc.tensor.transpose(psb[:, 4 + k // 4, c0:c0 + P], wq5[:, 1, o * FF + k * P:o * FF + (k + 1) * P],
                                            identb[:, :])
            m.then_inc(s_wqT, 1)

        def keep_w5(act, s_wqT):
            act.wait_ge(s_wqT, 1)
            nc.scalar.copy(W1q[:, :, :], psb[:, 2:4, 0:FF])
            act.wait_ge(s_wqT, 2)
            nc.scalar.copy(W2q[:, :, :].rearrange("p (b k) n -> p b (k n)", b=2), psb[:, 4:6, 0:FF])

        def moe_stage(tag, E, NC, W, router, gate_col, s_weights, loads, ar, parts, sel_name,
                      shared=False, bias=None, with_w5=False, store=False):
            hP, wP, iP, cS, selS = parts
            SW = selS.shape[1]
            gel, itm = ar.take([2, HALF]), ar.take([2, HALF])
            sel = ar.take([SW])
            lg, ex, comb, hit = (ar.take([NT, E]) for _ in range(4))
            top, idx, idf, wk = ar.take([NT, 8]), ar.take([NT, 8], U32), ar.take([NT, 2]), ar.take([NT, 2])
            col = ar.take([3, NT])
            KC = LOROW + E
            combp = ar.take([NT, KC])
            if with_w5:
                raw5, wq5, tmp5, am5 = ar.take([2, KD * FF]), ar.take([2, KD * FF], BF16), ar.take([QW]), ar.take([3, QW // BLK])
                s_wq, s_wqT = sem(f"{tag}_wq"), sem(f"{tag}_wqT")
            (s_var, s_sd, s_h, s_hTp, s_hT, s_v, s_lg, s_ein, s_exp, s_comb, s_cTp, s_cT, s_gu, s_gel, s_itm, s_down,
             s_add, s_tw, s_hL, s_wH, s_wL, s_sl, s_sel, s_zero) = (sem(f"{tag}_" + n) for n in (
                 "var sd h hTp hT v lg ein exp comb cTp cT gu gel itm down add tw hL wH wL sl sel zero").split())
            NU = 2 * NC
            HI, LO = 0, 1
            PRODUCTS = ((HI, HI), (HI, LO), (LO, HI))
            routed = lambda u: not (shared and u % NC == NC - 1)
            over = lambda v: v.unsqueeze(2).broadcast_to([P, NT, E])
            with nc.Block(tag) as block:
                @block.sync
                def _(sp):
                    sp.dma_start(sel[0:KC, :], a[sel_name]).then_inc(s_sl, 16)
                    if with_w5:
                        load_w5(sp, raw5)
                    if store:
                        for hf in range(2):
                            sp.wait_ge(s_add, hf + 1)
                            sp.dma_start(out.rearrange("b (h p) d -> p (b h) d", p=P)[:, hf * TPH:(hf + 1) * TPH, :],
                                         x[:, hf * TPH:(hf + 1) * TPH, :]).then_inc(s_out, 16)
                        sp.wait_ge(s_out, 32)

                @block.scalar
                def _(act):
                    def high_part(u):
                        if u >= RING:
                            act.wait_ge(s_down, u - RING + 1)
                        if u == 0:
                            act.wait_ge(s_weights, 16 * loads)
                        nc.scalar.copy(wP[HI][:, u % RING, :], W[:, u % NC, :]).then_inc(s_wH, 1)

                    for u in range(RING):
                        high_part(u)
                    norm_on_scalar(act, s_var, s_sd)
                    for i in range(NT // 2):
                        act.wait_ge(s_hTp, i + 1)
                        nc.scalar.copy(hT[:, :, i * 2 * P:(i + 1) * 2 * P], turned(2 + i)).then_inc(s_hT, 1)
                    act.wait_ge(s_ein, 1)
                    if shared:
                        nc.scalar.activation(ex, lg, ACT.Exp).then_inc(s_exp, 1)
                    else:
                        nc.scalar.activation(col[:, 1, :], col[:, 0, :], ACT.Exp).then_inc(s_exp, 1)

                    def silu(u):
                        act.wait_ge(s_gu, u + 1)
                        if u >= 2:
                            act.wait_ge(s_itm, u - 1)
                        nc.scalar.activation(gel[:, u % 2, :], ps[:, 2 + 2 * (u % 2), :], ACT.Silu).then_inc(s_gel, 1)

                    silu(0)
                    silu(1)
                    act.wait_ge(s_cTp, 1)
                    nc.scalar.copy(cS[0:KC, :], ps[0:KC, 6:8, :].rearrange("p b n -> p (b n)")).then_inc(s_cT, 1)
                    high_part(RING)
                    for u in range(2, NU):
                        silu(u)
                        if u + 2 < NU:
                            high_part(u + 2)
                    if with_w5:
                        keep_w5(act, s_wqT)

                @block.gpsimd
                def _(pool):
                    for u in range(NU):
                        pool.wait_ge(s_wH, u + 1)
                        if u >= RING:
                            pool.wait_ge(s_down, u - RING + 1)
                        nc.gpsimd.tensor_tensor(wP[LO][:, u % RING, :], W[:, u % NC, :], wP[HI][:, u % RING, :].bitcast(F32),
                                                ALU.subtract).then_inc(s_wL, 1)

                @block.tensor
                def _(pe):
                    turn_on_tensor(pe, h, 2, s_h, lambda t: t + 1, s_hTp)
                    pe.wait_ge(s_hT, NT // 2)
                    pe.wait_ge(s_weights, 16 * loads)
                    for t in range(NT):
                        for k in range(KD):
                            m = nc.tensor.matmul(ps[:, 6, t * E:(t + 1) * E], hT[:, k, t * P:(t + 1) * P],
                                                 router[:, k, :], start=k == 0, stop=k == KD - 1)
                    m.then_inc(s_lg, 1)

                    def products(u):
                        hf, c = divmod(u, NC)
                        if u in (0, NC):
                            pe.wait_ge(s_hL, (hf + 1) * NT // 4)
                        if u >= 2:
                            pe.wait_ge(s_itm, u - 1)
                        pe.wait_ge(s_wL, u + 1)
                        for j in range(2):
                            for k in range(KD):
                                for n, (pw, ph) in enumerate(PRODUCTS):
                                    c0 = (2 * j + k) * P
                                    m = nc.tensor.matmul(ps[:, 2 + 2 * (u % 2) + j, :], wP[pw][:, u % RING, c0:c0 + P],
                                                         hP[ph][:, k, hf * HALF:(hf + 1) * HALF],
                                                         start=k == 0 and n == 0, stop=k == KD - 1 and n == 2)
                        m.then_inc(s_gu, 1)

                    def token_weights(u):
                        hf, c = divmod(u, NC)
                        if routed(u):
                            rows = (selS[0:KC, c:c + 1].broadcast_to([KC, P]) if shared
                                    else selS[0:KC, c * P:(c + 1) * P])
                            nc.tensor.matmul(ps[:, 6 + u % 2, :], rows, cS[0:KC, hf * HALF:(hf + 1) * HALF],
                                             start=True, stop=True).then_inc(s_tw, 1)

                    def down(u):
                        c, w = u % NC, u % 2
                        pe.wait_ge(s_itm, u + 1)
                        if u == NC:
                            pe.wait_ge(s_add, 1)
                        for t in range(TPH):
                            for n, (pi, pw) in enumerate(PRODUCTS):
                                m = nc.tensor.matmul(ps[:, t // 2, (t % 2) * D:(t % 2 + 1) * D],
                                                     iP[pi][:, w, t * P:(t + 1) * P], wP[pw][:, u % RING, 4 * P:6 * P],
                                                     start=(c == 0 and n == 0 and t % 2 == 0),
                                                     stop=c == NC - 1 and n == 2, skip_group_check=True)
                        m.then_inc(s_down, 1)

                    products(0)
                    products(1)
                    pe.wait_ge(s_comb, 1)
                    for t in range(NT):
                        m = nc.tensor.transpose(ps[0:KC, 6 + t // 4, (t % 4) * P:(t % 4 + 1) * P], combp[:, t, :], ident[:, :])
                    m.then_inc(s_cTp, 1)
                    pe.wait_ge(s_cT, 1)
                    pe.wait_ge(s_sel, 1)
                    token_weights(0)
                    token_weights(1)
                    for u in range(NU):
                        if 2 <= u + 1 < NU:
                            products(u + 1)
                            token_weights(u + 1)
                        down(u)
                    if with_w5:
                        turn_w5(pe, wq5, s_wq, s_wqT)

                @block.vector
                def _(dve):
                    v = Steps(dve, s_v)
                    norm_on_vector(dve, v, s_var, s_sd, s_h)
                    nc.vector.memset(combp, 0.0).then_inc(s_zero, 1)
                    for i in range(NT // 2):
                        dve.wait_ge(s_hT, i + 1)
                        cols = slice(i * 2 * P, (i + 1) * 2 * P)
                        v.link(nc.vector.tensor_copy(hP[HI][:, :, cols], hT[:, :, cols]))
                        nc.vector.tensor_tensor(hP[LO][:, :, cols], hT[:, :, cols], hP[HI][:, :, cols].bitcast(F32),
                                                ALU.subtract).then_inc(s_hL, 1)
                    dve.wait_ge(s_sl, 16)
                    nc.vector.tensor_copy(selS[0:KC, :], sel[0:KC, :]).then_inc(s_sel, 1)
                    dve.wait_ge(s_lg, 1)
                    psl = ps[:, 6, 0:NT * E].rearrange("p (t e) -> p t e", e=E)
                    if shared:
                        v.link(nc.vector.tensor_tensor(lg, psl, bias[:, :].unsqueeze(1).broadcast_to([P, NT, E]), ALU.add))
                        v.link(nc.vector.tensor_reduce(col[:, 0, :], lg, AX.X, ALU.max))
                        nc.vector.tensor_tensor(lg, lg, over(col[:, 0, :]), ALU.subtract).then_inc(s_ein, 1)
                        dve.wait_ge(s_exp, 1)
                        v.link(nc.vector.tensor_reduce(col[:, 1, :], ex, AX.X, ALU.add))
                        v.link(nc.vector.reciprocal(col[:, 2, :], col[:, 1, :]))
                        v.link(nc.vector.tensor_tensor(lg, ex, over(col[:, 2, :]), ALU.mult))
                    else:
                        v.link(nc.vector.tensor_copy(lg, psl))
                    for t in range(NT):
                        v.mark(nc.vector.max(top[:, t, :], lg[:, t, :]))
                    v.settle()
                    for t in range(NT):
                        v.mark(nc.vector.max_index(idx[:, t, :], top[:, t, :], lg[:, t, :]))
                    v.settle()
                    v.link(nc.vector.tensor_copy(idf, idx[:, :, 0:2]))
                    if shared:
                        v.link(nc.vector.tensor_reduce(col[:, 0, :], top[:, :, 0:2], AX.X, ALU.add))
                        v.link(nc.vector.tensor_scalar(col[:, 0, :], col[:, 0, :], 1e-9, None, ALU.add))
                        v.link(nc.vector.reciprocal(col[:, 1, :], col[:, 0, :]))
                        v.link(nc.vector.tensor_tensor(wk, top[:, :, 0:2], col[:, 1, :].unsqueeze(2).broadcast_to([P, NT, 2]),
                                                       ALU.mult))
                    else:
                        nc.vector.tensor_tensor(col[:, 0, :], top[:, :, 1], top[:, :, 0], ALU.subtract).then_inc(s_ein, 1)
                        dve.wait_ge(s_exp, 1)
                        v.link(nc.vector.tensor_scalar(col[:, 2, :], col[:, 1, :], 1.0, None, ALU.add))
                        v.link(nc.vector.reciprocal(wk[:, :, 0], col[:, 2, :]))
                        v.link(nc.vector.tensor_tensor(wk[:, :, 1], wk[:, :, 0], col[:, 1, :], ALU.mult))
                    it = iota[:, 0:E].unsqueeze(1).broadcast_to([P, NT, E])
                    for k, dst in ((0, comb), (1, hit)):
                        v.link(nc.vector.tensor_tensor(dst, it, over(idf[:, :, k]), ALU.is_equal))
                        v.link(nc.vector.tensor_tensor(dst, dst, over(wk[:, :, k]), ALU.mult))
                    v.link(nc.vector.tensor_tensor(comb, comb, hit, ALU.add))
                    dve.wait_ge(s_zero, 1)
                    v.link(nc.vector.tensor_copy(combp[:, :, 0:E].bitcast(F32R), comb))
                    nc.vector.tensor_tensor(combp[:, :, LOROW:KC].bitcast(F32R), comb, combp[:, :, 0:E],
                                            ALU.subtract).then_inc(s_comb, 1)

                    def add_half(hf):
                        dve.wait_ge(s_down, NC * (hf + 1))
                        for i in range(2):
                            xv = x[:, hf * TPH + 2 * i:hf * TPH + 2 * i + 2, :]
                            ins = nc.vector.scalar_tensor_tensor(xv, ps[:, i, :].rearrange("p (t n) -> p t n", t=2),
                                                                 tg[:, gate_col:gate_col + 1], xv, ALU.mult, ALU.add)
                        ins.then_inc(s_add, 1)

                    for u in range(NU):
                        dve.wait_ge(s_gel, u + 1)
                        if u >= 2:
                            dve.wait_ge(s_down, u - 1)
                        o = itm[:, u % 2, :]
                        v.link(nc.vector.tensor_tensor(o, gel[:, u % 2, :], ps[:, 3 + 2 * (u % 2), :], ALU.mult))
                        if routed(u):
                            dve.wait_ge(s_tw, sum(routed(w) for w in range(u + 1)))
                            v.link(nc.vector.tensor_tensor(o, o, ps[:, 6 + u % 2, :], ALU.mult))
                        v.link(nc.vector.tensor_copy(iP[HI][:, u % 2, :], o))
                        nc.vector.tensor_tensor(iP[LO][:, u % 2, :], o, iP[HI][:, u % 2, :].bitcast(F32),
                                                ALU.subtract).then_inc(s_itm, 1)
                        if u == NC:
                            add_half(0)
                        if with_w5:
                            quantize_w5(dve, v, u, raw5, wq5, tmp5, am5, s_wq)
                    add_half(1)

        def stage3(parts):
            moe_stage("stage3", NE3, NC3, W3, rt3, 5, s_w3, 3, Arena(regA), parts, "sel3", shared=True, bias=bias3,
                      with_w5=True)

        NH, HD, NDCA = 16, 16, 16
        HPAD = 2 * HD
        SCALE4, EPS4 = HD ** -0.5, 1e-6
        NMAIN = S - NDCA
        VW = 2 * (HD + 1)
        HC, KS, KA = 64, 3 * HD, 3 * HD + 4
        HPB = P // HC
        NBLK = NH // HPB

        def stage4(k4T, q4T, regD):
            ar = Arena(regA, regD, regC)
            qpad, kpad = ar.take([2, 2, NH, HC]), ar.take([2, 2, NH, HC])
            kv = ar.take([NT, 2 * D])
            q = ar.take([NT, D])
            NG = 2 * NH
            sq = ar.take([2, NG * HD])
            vaug = ar.take([NT, NH, VW])
            prob = ar.take([4, 2 * S])
            wq, wkv, wdca, wo = ar.take([KD, D]), ar.take([2 * D]), ar.take([2 * D]), ar.take([KD, D])
            ctxm, ctxd = ar.take([B, P]), ar.take([B, P])
            bkv = ar.take([2, 2 * D])
            bq, bo = ar.take([D]), ar.take([D])
            qn, kn = ar.take([2, HD]), ar.take([2, 2, HD])
            mask = ar.take([2, 2])
            st = ar.take([3, 2, NG])
            dev = ar.take([B, 2, NG])
            rz = ar.take([8])
            pvT = ar.take([2, 2 * S])
            nm = ar.take([2, 2, NH, 2])
            o = h
            part = ar.take([8, HD])
            (s_var, s_sd, s_h, s_hTp, s_hT, s_wk, s_w, s_v, s_q, s_qe, s_kv, s_kve, s_kb, s_qv, s_qs, s_sqi, s_sq, s_kp, s_qp, s_T, s_Te,
             s_s1, s_mx, s_qm, s_s2, s_p, s_pv, s_pe, s_pt, s_o, s_oP, s_oT, s_fin, s_ctx, s_va) = (
                sem("s4_" + n) for n in ("var sd h hTp hT wk w v q qe kv kve kb qv qs sqi sq kp qp T Te s1 mx qm s2 p pv pe pt o oP oT "
                                         "fin ctx va").split())
            groups = lambda w: w.rearrange("p t (g d) -> p (t g) d", d=HD)
            kview = kv.rearrange("p t (g d) -> p (t g) d", d=HPAD)[:, :, 0:HD]
            wide = lambda c: c.unsqueeze(2).broadcast_to([P, NG, HD])
            NHB = B * NH
            NSET, NVB = 2 + 8 + 4, 4

            TK, TQ, MAX0, TM = 0, 2, 4, 13

            def flat(v):
                return v.rearrange("p a b -> p (a b)")

            with nc.Block("stage4") as block:
                @block.sync
                def _(sp):
                    sp.dma_start(wkv, a["q4_wkv"]).then_inc(s_wk, 16)
                    sp.dma_start(wdca, a["q4_wdca"]).then_inc(s_wk, 16)
                    sp.dma_start(mask, a["q4_mask"]).then_inc(s_w, 16)
                    sp.dma_start(wq, a["q4_wq"]).then_inc(s_w, 16)
                    row = lambda nm: a[nm].partition_broadcast(P)
                    sp.dma_start(bkv[:, 0, :], row("q4_bkv")).then_inc(s_w, 16)
                    sp.dma_start(bkv[0:NMAIN - P, 1, :], a["q4_bkv"].partition_broadcast(NMAIN - P)).then_inc(s_w, 16)
                    sp.dma_start(bkv[NMAIN - P:P, 1, :], a["q4_bdca"].partition_broadcast(NDCA)).then_inc(s_w, 16)
                    sp.dma_start(bq, row("q4_bq")).then_inc(s_w, 16)
                    sp.dma_start(bo, row("q4_bo")).then_inc(s_w, 16)
                    sp.dma_start(qn, row("q4_qn")).then_inc(s_w, 16)
                    sp.dma_start(kn[:, 0], row("q4_kn")).then_inc(s_w, 16)
                    sp.dma_start(kn[0:NMAIN - P, 1], a["q4_kn"].partition_broadcast(NMAIN - P)).then_inc(s_w, 16)
                    sp.dma_start(kn[NMAIN - P:P, 1], a["q4_kd"].partition_broadcast(NDCA)).then_inc(s_w, 16)
                    sp.dma_start(wo, a["q4_wo"]).then_inc(s_w, 16)

                @block.gpsimd
                def _(pool):
                    c = ctxT[:, :].rearrange("p (b two n) -> p b two n", two=2, n=P)[:, :, 1, :]
                    nc.gpsimd.tensor_copy(ctxm[:, :, 0:NMAIN - P], c[:, :, 0:NMAIN - P]).then_inc(s_ctx, 1)
                    nc.gpsimd.memset(ctxm[:, :, NMAIN - P:P], 0.0).then_inc(s_ctx, 1)
                    nc.gpsimd.memset(ctxd[:, :, 0:NMAIN - P], 0.0).then_inc(s_ctx, 1)
                    nc.gpsimd.tensor_copy(ctxd[:, :, NMAIN - P:P], c[:, :, NMAIN - P:P]).then_inc(s_ctx, 1)
                    for v_ in (qpad, kpad):
                        nc.gpsimd.memset(v_.rearrange("p a t g d -> p (a t g) d")[:, :, KS:HC], 0.0).then_inc(s_va, 1)
                    pool.wait_ge(s_va, 2)
                    pool.wait_ge(s_w, 16 * 12)
                    for t in range(2):
                        for j in range(4):
                            ones = kpad[:, :, t, :, KS + j]
                            nc.gpsimd.tensor_scalar(ones, ones, mask[:, t, j % 2:j % 2 + 1], None, ALU.add).then_inc(s_va, 1)
                    pool.wait_ge(s_va, 10)
                    for par in range(2):
                        for j in range(2):
                            c0 = j * (HD + 1) + HD
                            ones = kpad[:, 0, par, :, KS + j].unsqueeze(1).broadcast_to([P, NT // 2, NH])
                            nc.gpsimd.tensor_copy(vaug[:, par::2, :, c0], ones).then_inc(s_va, 1)

                    def add_biases(b):
                        for t in (2 * b, 2 * b + 1):
                            pool.wait_ge(s_kve, t + 1)
                            nc.gpsimd.tensor_tensor(kv[:, t, :], kv[:, t, :], bkv[:, t % 2, :], ALU.add).then_inc(s_kb, 1)
                        pool.wait_ge(s_qe, b + 1)
                        nc.gpsimd.tensor_tensor(q[:, 2 * b:2 * b + 2, :], q[:, 2 * b:2 * b + 2, :],
                                                bq.unsqueeze(1).broadcast_to([P, 2, D]), ALU.add).then_inc(s_kb, 1)

                    def place_values(b):
                        pool.wait_ge(s_kb, 3 * (b + 1))
                        for t in (2 * b, 2 * b + 1):
                            for j in range(2):
                                mk = mask[:, t % 2, j:j + 1]
                                src = kv[:, t, :].rearrange("p (g d) -> p g d", d=HPAD)[:, :, HD:HPAD]
                                c0 = j * (HD + 1)
                                nc.gpsimd.tensor_scalar(vaug[:, t, :, c0:c0 + HD], src, mk, None,
                                                        ALU.mult).then_inc(s_va, 1)

                    add_biases(0)
                    add_biases(1)
                    place_values(0)
                    add_biases(2)
                    add_biases(3)
                    for b in range(1, B):
                        place_values(b)

                @block.scalar
                def _(act):
                    norm_on_scalar(act, s_var, s_sd)

                    def keep_kv(t):
                        act.wait_ge(s_kv, t + 1)
                        nc.scalar.copy(kv[:, t, :], ps[:, t % 4, :]).then_inc(s_kve, 1)

                    def keep_q(b):
                        act.wait_ge(s_q, b + 1)
                        nc.scalar.copy(flat(q[:, 2 * b:2 * b + 2, :]), ps[:, 4 + b, :]).then_inc(s_qe, 1)

                    def squares(b):
                        act.wait_ge(s_sqi, 2 * b + 2)
                        for i, src in enumerate((kview, groups(q))):
                            nc.scalar.activation(sq[:, i, :].rearrange("p (g d) -> p g d", d=HD),
                                                 src[:, NG * b:NG * (b + 1), :], ACT.Square).then_inc(s_sq, 1)

                    def roots(b):
                        act.wait_ge(s_qv, b + 1)
                        nc.scalar.activation(dev[:, b], st[:, 0], ACT.Sqrt).then_inc(s_qs, 1)

                    keep_kv(0)
                    keep_kv(1)
                    for i in range(NT // 2):
                        act.wait_ge(s_hTp, i + 1)
                        nc.scalar.copy(hT[:, :, i * 2 * P:(i + 1) * 2 * P], turned(4 + i)).then_inc(s_hT, 1)
                        if i == 0:
                            keep_q(0)
                    for b in range(1, B):
                        keep_kv(2 * b)
                        keep_kv(2 * b + 1)
                        keep_q(b)
                        if b == 1:
                            squares(0)
                            roots(0)

                    def evacuate(b, i, hf):
                        act.wait_ge(s_T, 3 * b + i + 1)
                        if i == 0 and b >= 2:
                            act.wait_ge(s_pv, NH // 2 * (b - 1))
                        dst = (k4T, q4T, q4T)[i]
                        blks = slice(hf * NBLK // 2, (hf + 1) * NBLK // 2)
                        nc.scalar.copy(flat(dst[:, b % 2, blks]), flat(ps[:, 2 * hf:2 * hf + 2, :])).then_inc(s_Te, 1)

                    def exponent(n):
                        act.wait_ge(s_s2, n + 1)
                        if n >= 4:
                            act.wait_ge(s_pv, n // 2 - 1)
                        nc.scalar.activation(prob[:, n % 4, :], ps[:, 4 + n % 2, :], ACT.Exp, scale=SCALE4).then_inc(s_p, 1)

                    def evacuate_values(j):
                        act.wait_ge(s_pv, j + 1)
                        if j >= 2:
                            act.wait_ge(s_pt, j - 1)
                        nc.scalar.copy(pvT[0:VW, j % 2, :], ps[0:VW, 6 + j % 2, :]).then_inc(s_pe, 1)

                    for b in range(-1, B):
                        for slot in range(NH):
                            n = b * NH + slot + 1
                            if 0 <= n < NHB and b >= 0:
                                exponent(n)
                            if n >= 2 and n % 2 == 0:
                                evacuate_values(n // 2 - 1)
                            for i, first in enumerate((TK, TQ, TM)):
                                if b + 1 < B and slot in (first, first + 1):
                                    evacuate(b + 1, i, slot - first)
                            if b == -1 and slot in (1, 14, 15):
                                squares(1 + max(0, slot - 13))
                                roots(1 + max(0, slot - 13))
                        if b == -1:
                            exponent(0)
                    for i in range(4):
                        act.wait_ge(s_oP, i + 1)
                        nc.scalar.copy(hT[:, :, i * 2 * P:(i + 1) * 2 * P], turned(i)).then_inc(s_oT, 1)

                @block.tensor
                def _(pe):
                    def project_kv(t):
                        if t >= 4:
                            pe.wait_ge(s_kve, t - 3)
                        if t % 2 == 0:
                            m = nc.tensor.matmul(ps[:, t % 4, :], ctxT[:, t * P:(t + 1) * P], wkv, start=True, stop=True)
                        else:
                            nc.tensor.matmul(ps[:, t % 4, :], ctxm[:, t // 2, :], wkv, start=True, stop=False)
                            m = nc.tensor.matmul(ps[:, t % 4, :], ctxd[:, t // 2, :], wdca, start=False, stop=True)
                        m.then_inc(s_kv, 1)

                    def project_q(b):
                        pe.wait_ge(s_hT, b + 1)
                        for t in (2 * b, 2 * b + 1):
                            for k in range(KD):
                                m = nc.tensor.matmul(ps[:, 4 + b, (t % 2) * D:(t % 2 + 1) * D],
                                                     hT[:, k, t * P:(t + 1) * P], wq[:, k, :], start=k == 0, stop=k == KD - 1)
                        m.then_inc(s_q, 1)

                    pe.wait_ge(s_wk, 32)
                    project_kv(0)
                    pe.wait_ge(s_ctx, 4)
                    project_kv(1)
                    turn_on_tensor(pe, h, 4, s_h, lambda t: t + 1, s_hTp)
                    pe.wait_ge(s_w, 16 * 12)
                    project_q(0)
                    for b in range(1, B):
                        project_kv(2 * b)
                        project_kv(2 * b + 1)
                        project_q(b)

                    def turn_heads(src, b):
                        for blk in range(NBLK):
                            for t in range(2):
                                c0 = (blk % 2) * S + t * P
                                m = nc.tensor.transpose(ps[:, blk // 2, c0:c0 + P],
                                                        flat(src[:, b % 2, t])[:, blk * P:(blk + 1) * P], ident[:, :])
                        m.then_inc(s_T, 1)

                    def maximum_scores(b, g):
                        t, h0 = g // 4, 4 * (g % 4)
                        if g >= 2:
                            pe.wait_ge(s_mx, 2 * (8 * b + g - 1))
                        for i in range(4):
                            hd = h0 + i
                            r = slice(HC * (hd % 2), HC * (hd % 2) + KS)
                            m = nc.tensor.matmul(ps[:, 2 * (g % 2) + i % 2, (i // 2) * S:(i // 2 + 1) * S],
                                                 q4T[r, b % 2, hd // 2, t * P:(t + 1) * P], k4T[r, b % 2, hd // 2, :],
                                                 start=True, stop=True)
                        m.then_inc(s_s1, 1)

                    def prepare(b, slot):
                        if slot == TK:
                            if b >= 1:
                                pe.wait_ge(s_Te, 6 * b)
                            pe.wait_ge(s_kp, b + 1)
                            turn_heads(kpad, b)
                        elif slot == TQ:
                            pe.wait_ge(s_Te, 6 * b + 2)
                            pe.wait_ge(s_qp, b + 1)
                            turn_heads(qpad, b)
                        elif MAX0 <= slot < MAX0 + 8:
                            if slot == MAX0:
                                pe.wait_ge(s_Te, 6 * b + 4)
                            maximum_scores(b, slot - MAX0)
                        elif slot == TM:
                            pe.wait_ge(s_qm, b + 1)
                            turn_heads(qpad, b)

                    def scores(n):
                        b, hd = divmod(n, NH)
                        if hd == 0:
                            pe.wait_ge(s_Te, 6 * b + 6)
                        if n >= 2:
                            pe.wait_ge(s_p, n - 1)
                        r = slice(HC * (hd % 2), HC * (hd % 2) + KA)
                        for kt in range(2):
                            m = nc.tensor.matmul(ps[:, 4 + n % 2, kt * S:(kt + 1) * S],
                                                 k4T[r, b % 2, hd // 2, kt * P:(kt + 1) * P], q4T[r, b % 2, hd // 2, :],
                                                 start=True, stop=True)
                        m.then_inc(s_s2, 1)

                    def values(n):
                        b, hd = divmod(n, NH)
                        j = n // 2
                        pe.wait_ge(s_p, n + 1)
                        if hd == 0:
                            pe.wait_ge(s_va, NSET + NVB * (b + 1))
                        if n % 2 == 0 and j >= 2:
                            pe.wait_ge(s_o, j - 1)
                        for kt in range(2):
                            m = nc.tensor.matmul(ps[0:VW, 6 + j % 2, (n % 2) * S:(n % 2 + 1) * S], vaug[:, 2 * b + kt, hd, :],
                                                 prob[:, n % 4, kt * S:(kt + 1) * S], start=kt == 0, stop=kt == 1)
                        if n % 2:
                            m.then_inc(s_pv, 1)

                    def turn_values(j):
                        pe.wait_ge(s_pe, j + 1)
                        for i in range(4):
                            m = nc.tensor.transpose(ps[:, 6 + j % 2, i * VW:(i + 1) * VW],
                                                    pvT[0:VW, j % 2, i * P:(i + 1) * P], ident[0:VW, 0:VW])
                        m.then_inc(s_pt, 1)

                    pe.wait_ge(s_kve, NT)
                    pe.wait_ge(s_qe, 4)
                    for b in range(-1, B):
                        for slot in range(NH):
                            n = b * NH + slot
                            if b >= 0:
                                if n + 1 < NHB and slot + 1 < NH:
                                    scores(n + 1)
                                values(n)
                                if n >= 2 and n % 2 == 0:
                                    turn_values(n // 2 - 1)
                            if b + 1 < B:
                                prepare(b + 1, slot)
                        if b + 1 < B:
                            scores((b + 1) * NH)
                    turn_values(NHB // 2 - 1)
                    pe.wait_ge(s_o, NHB // 2)
                    turn_on_tensor(pe, o, 0, None, None, s_oP)
                    pe.wait_ge(s_oT, 4)
                    for t in range(NT):
                        for k in range(KD):
                            m = nc.tensor.matmul(ps[:, 4 + t // 2, (t % 2) * D:(t % 2 + 1) * D], hT[:, k, t * P:(t + 1) * P],
                                                 wo[:, k, :], start=k == 0, stop=k == KD - 1)
                        if t % 2:
                            m.then_inc(s_fin, 1)

                @block.vector
                def _(dve):
                    v = Steps(dve, s_v)
                    norm_on_vector(dve, v, s_var, s_sd, s_h)
                    dve.wait_ge(s_w, 16 * 12)
                    dve.wait_ge(s_va, NSET)

                    def both(b):
                        return [(i, src[:, NG * b:NG * (b + 1), :]) for i, src in enumerate((kview, groups(q)))]

                    def center_heads(b):
                        dve.wait_ge(s_kb, 3 * (b + 1))
                        if b >= 1:
                            dve.wait_ge(s_qv, b)
                        for i, src in both(b):
                            v.mark(nc.vector.tensor_reduce(st[:, 1, i, :], src, AX.X, ALU.add))
                        v.settle()
                        v.link(nc.vector.tensor_scalar(st[:, 2], st[:, 1], 1.0 / HD, None, ALU.mult))
                        for i, src in both(b):
                            nc.vector.tensor_tensor(src, src, wide(st[:, 2, i, :]), ALU.subtract).then_inc(s_sqi, 1)

                    def variances(b):
                        dve.wait_ge(s_sq, 2 * b + 2)
                        v.link(nc.vector.tensor_reduce(st[:, 1].rearrange("p a g -> p (a g)"),
                                                       sq.rearrange("p a (g d) -> p (a g) d", d=HD), AX.X, ALU.add))
                        if b >= 1:
                            dve.wait_ge(s_qs, b)
                        nc.vector.tensor_scalar(st[:, 0], st[:, 1], 1.0 / HD, EPS4, ALU.mult, ALU.add).then_inc(s_qv, 1)

                    def scale_heads(b):
                        dve.wait_ge(s_qs, b + 1)
                        dve.wait_ge(s_sqi, 2 * b + 2)
                        v.link(nc.vector.reciprocal(dev[:, b], dev[:, b]))
                        for i, src in both(b):
                            v.mark(nc.vector.tensor_tensor(src, src, wide(dev[:, b, i, :]), ALU.mult))
                        v.settle()

                    def affine_heads(b):
                        keys = kv[:, 2 * b:2 * b + 2, :].rearrange("p t (g d) -> p t g d", d=HPAD)[:, :, :, 0:HD]
                        queries = both(b)[1][1]
                        for row, op in ((0, ALU.mult), (1, ALU.add)):
                            v.mark(nc.vector.tensor_tensor(keys, keys, kn[:, :, row, :].unsqueeze(2)
                                                           .broadcast_to([P, 2, NH, HD]), op))
                            v.mark(nc.vector.tensor_tensor(queries, queries, qn[:, row, :].unsqueeze(1)
                                                           .broadcast_to([P, NG, HD]), op))
                            v.settle()

                    def pads(b, which):
                        for src, pad, lo, his, s_done in (
                                (kview, kpad, HD, (0, 2 * HD), s_kp), (groups(q), qpad, 2 * HD, (0, HD), s_qp))[which:which + 1]:
                            dst = pad[:, b % 2].rearrange("p t g d -> p (t g) d").bitcast(F32R)
                            sv = src[:, 2 * b * NH:2 * (b + 1) * NH, :]
                            for c0 in his:
                                v.mark(nc.vector.tensor_copy(dst[:, :, c0:c0 + HD], sv))
                            v.settle()
                            nc.vector.tensor_tensor(dst[:, :, lo:lo + HD], sv, dst[:, :, 0:HD].bitcast(F32),
                                                    ALU.subtract).then_inc(s_done, 1)

                    def maxima(b, g):
                        t, h0 = g // 4, 4 * (g % 4)
                        dve.wait_ge(s_s1, 8 * b + g + 1)
                        sc = ps[:, 2 * (g % 2):2 * (g % 2) + 2, :].rearrange("p j (c n) -> p j c n", c=2)
                        dst = nm[:, b % 2, t, h0:h0 + 4, :].rearrange("p (c j) d -> p j c d", j=2)
                        for j, (lo, hi) in enumerate(((0, NMAIN), (NMAIN, S))):
                            nc.vector.tensor_reduce(dst[:, :, :, j], sc[:, :, :, lo:hi], AX.X, ALU.max,
                                                    negate=True).then_inc(s_mx, 1)

                    def place_maxima(b):
                        dve.wait_ge(s_mx, 16 * (b + 1))
                        dst = qpad[:, b % 2].rearrange("p t g d -> p (t g) d").bitcast(F32R)
                        src = nm[:, b % 2].rearrange("p t g d -> p (t g) d")
                        v.link(nc.vector.tensor_copy(dst[:, :, KS:KS + 2], src))
                        nc.vector.tensor_tensor(dst[:, :, KS + 2:KS + 4], src, dst[:, :, KS:KS + 2].bitcast(F32),
                                                ALU.subtract).then_inc(s_qm, 1)

                    def normalize(j):
                        b, pair = divmod(j, NH // 2)
                        dve.wait_ge(s_pt, j + 1)
                        pv = ps[:, 6 + j % 2, 0:4 * VW].rearrange("p (c d) -> p c d", d=HD + 1)
                        v.link(nc.vector.reciprocal(rz, pv[:, :, HD]))
                        v.link(nc.vector.tensor_tensor(part, pv[:, :, 0:HD], rz.unsqueeze(2).broadcast_to([P, 8, HD]),
                                                       ALU.mult))
                        both = part.rearrange("p (h t c) d -> p h t c d", h=2, t=2)
                        dst = o[:, 2 * b:2 * b + 2, :].rearrange("p t (g d) -> p g t d", d=HD)[:, 2 * pair:2 * pair + 2]
                        nc.vector.tensor_tensor(dst, both[:, :, :, 0, :], both[:, :, :, 1, :], ALU.add).then_inc(s_o, 1)

                    center_heads(0)
                    variances(0)
                    scale_heads(0)
                    affine_heads(0)
                    pads(0, 0)
                    pads(0, 1)
                    for b in range(-1, B):
                        for slot in range(NH):
                            n = b * NH + slot
                            if n >= 2 and n % 2 == 0:
                                normalize(n // 2 - 1)
                            if b + 1 < B and MAX0 <= slot < MAX0 + 8:
                                maxima(b + 1, slot - MAX0)
                                if slot == MAX0 + 7:
                                    place_maxima(b + 1)
                            if b == -1 and slot in (0, 1, 12, 13, 14, 15):
                                c = 1 + max(0, slot - 10) // 2
                                (center_heads, variances)[slot % 2](c)
                            step = slot - (12 if b >= 0 else 2)
                            if b + 2 < B and step == 0:
                                scale_heads(b + 2)
                            if b + 2 < B and step == 1:
                                affine_heads(b + 2)
                            if b + 2 < B and step == 2 and b >= 0:
                                dve.wait_ge(s_T, 3 * (b + 1))
                            if b + 2 < B and step in ((2, 3) if b >= 0 else (1,)):
                                for which in ((step - 2,) if b >= 0 else (0, 1)):
                                    pads(b + 2, which)
                    normalize(NHB // 2 - 1)
                    for i in range(4):
                        dve.wait_ge(s_fin, i + 1)
                        xb = x[:, 2 * i:2 * i + 2, :]
                        v.link(nc.vector.tensor_tensor(q[:, 2 * i:2 * i + 2, :], ps[:, 4 + i, :].rearrange("p (t n) -> p t n", t=2),
                                                       bo.unsqueeze(1).broadcast_to([P, 2, D]), ALU.add))
                        nc.vector.scalar_tensor_tensor(xb, q[:, 2 * i:2 * i + 2, :], tg[:, 2:3], xb, ALU.mult, ALU.add)

        def stage5():
            ar = Arena(regB, regC)
            tmp = ar.take([NT * D])
            am = ar.take([NT // 2, 3, 2 * D // BLK])
            rb = ar.take([NT, D], BF16)
            y1, g1 = ar.take([2, FF], BF16), ar.take([2, FF], BF16)
            q1, q2 = ar.take([NT * D], BF16), ar.take([2, FF], BF16)
            q1T, q2T = ar.take([KD, T], BF16), ar.take([2, FF // P, P], BF16)
            tmp2 = ar.take([2, FF])
            am2 = ar.take([2, 3, FF // BLK])
            lnw, lnb, b2 = ar.take([D]), ar.take([D]), ar.take([D])
            b1 = ar.take([FF])
            hb = ar.take([NT * D], BF16)
            y2, z = ar.take([D], BF16), ar.take([D], BF16)
            (s_var, s_sd, s_h, s_var2, s_sd2, s_h2, s_b, s_v, s_hw, s_hb, s_ra, s_rs, s_q1, s_q1P, s_q1T, s_y1, s_y1b,
             s_g1, s_q2, s_q2P, s_q2T, s_y2, s_x) = (
                sem("s5_" + n) for n in ("var sd h var2 sd2 h2 b v hw hb ra rs q1 q1P q1T y1 y1b g1 q2 q2P q2T y2 x").split())
            with nc.Block("stage5") as block:
                @block.sync
                def _(sp):
                    for dst, nm in ((lnw, "L2_lnw"), (lnb, "L2_lnb"), (b1, "L2_b1"), (b2, "L2_b2")):
                        sp.dma_start(dst, a[nm].partition_broadcast(P)).then_inc(s_b, 16)
                    load_w7(sp)

                @block.gpsimd
                def _(pool):
                    hbv = hb.rearrange("p (i n) -> p i n", n=2 * D)
                    row = lambda w: w.unsqueeze(1).broadcast_to([P, 2, D])

                    def affine(i):
                        pool.wait_ge(s_h2, 2 * i + 2)
                        hp = h[:, 2 * i:2 * i + 2, :]
                        nc.gpsimd.tensor_tensor(hp, hp, row(lnw), ALU.mult).then_inc(s_hw, 1)
                        pool.wait_ge(s_hw, i + 1)
                        nc.gpsimd.tensor_tensor(hbv[:, i].rearrange("p (t n) -> p t n", n=D), hp, row(lnb),
                                                ALU.add).then_inc(s_hb, 1)

                    pool.wait_ge(s_b, 64)
                    for i in range(NT // 2):
                        affine(i)
                    for t in range(NT):
                        pool.wait_ge(s_ra, t + 1)
                        w = blocks(tmp2[:, t % 2, :])
                        nc.gpsimd.tensor_tensor(w, w, mx_wide(am2[:, t % 2], 1, FF // BLK), ALU.subtract).then_inc(s_rs, 1)

                @block.scalar
                def _(act):
                    norm_on_scalar(act, s_var, s_sd)
                    act.wait_ge(s_var2, 1)
                    nc.scalar.activation(lnsd[:, 1, :], lnsd[:, 0, :], ACT.Sqrt).then_inc(s_sd2, 1)
                    for i in range(4):
                        act.wait_ge(s_q1P, i + 1)
                        nc.scalar.copy(q1T[:, :, i * 2 * P:(i + 1) * 2 * P], turned(4 + i, psb)).then_inc(s_q1T, 1)
                    for t in range(NT + 1):
                        if t < NT:
                            act.wait_ge(s_y1b, t + 1)
                            if t >= 2:
                                act.wait_ge(s_ra, t - 1)
                            nc.scalar.activation(g1[:, t % 2, :], y1[:, t % 2, :], ACT.Gelu_apprx_tanh).then_inc(s_g1, 1)
                        if t >= 1:
                            act.wait_ge(s_q2P, t)
                            if t >= 3:
                                act.wait_ge(s_y2, t - 2)
                            nc.scalar.copy(q2T[:, (t - 1) % 2].rearrange("p k n -> p (k n)"),
                                           psb[:, 4 + (t - 1) % 2, 0:FF]).then_inc(s_q2T, 1)

                @block.tensor
                def _(pe):
                    def up(t):
                        pe.wait_ge(s_q1T, t // 2 + 1)
                        if t >= 2:
                            pe.wait_ge(s_y1b, t - 1)
                        for n in range(2):
                            for k in range(KD):
                                m = nc.tensor.matmul(ps[:, 2 * (t % 2) + n, :], q1T[:, k, t * P:(t + 1) * P],
                                                     W1q[:, k, n * HALF:(n + 1) * HALF], start=k == 0, stop=k == KD - 1)
                        m.then_inc(s_y1, 1)

                    def first_two(i):
                        if i == 0:
                            up(0)
                            up(1)

                    turn_on_tensor(pe, q1.rearrange("p (t n) -> p t n", n=D), 4, s_q1, lambda t: t // 2 + 1, s_q1P,
                                   dst_psum=psb, idn=identb, after=first_two)
                    pe.wait_ge(s_q1T, 4)
                    up(2)
                    for t in range(NT):
                        pe.wait_ge(s_q2, t + 1)
                        if t >= 2:
                            pe.wait_ge(s_q2T, t - 1)
                        for k in range(FF // P):
                            m = nc.tensor.transpose(psb[:, 4 + t % 2, k * P:(k + 1) * P], q2[:, t % 2, k * P:(k + 1) * P],
                                                    identb[:, :])
                        m.then_inc(s_q2P, 1)
                        if t + 3 < NT:
                            up(t + 3)
                        pe.wait_ge(s_q2T, t + 1)
                        if t >= 2:
                            pe.wait_ge(s_x, t - 1)
                        for k in range(FF // P):
                            m = nc.tensor.matmul(ps[:, 6 + t % 2, 0:D], q2T[:, t % 2, k, :], W2q[:, k, :],
                                                 start=k == 0, stop=k == FF // P - 1)
                        m.then_inc(s_y2, 1)

                @block.vector
                def _(dve):
                    v = Steps(dve, s_v)
                    norm_on_vector(dve, v, s_var, s_sd, s_h, dst=rb)
                    dve.wait_ge(s_h, NT)
                    norm_on_vector(dve, v, s_var2, s_sd2, s_h2, src=rb, dst=h)
                    hbv, q1v, tmpv = (w.rearrange("p (i n) -> p i n", n=2 * D) for w in (hb, q1, tmp))
                    for i in range(NT // 2):
                        dve.wait_ge(s_hb, i + 1)
                        mx_scales(v, blocks(hbv[:, i]), am[:, i])
                        mx_round(v, blocks(hbv[:, i]), blocks(q1v[:, i]), blocks(tmpv[:, i]), am[:, i], s_q1)
                    dve.wait_ge(s_b, 64)

                    def hidden(t):
                        dve.wait_ge(s_y1, t + 1)
                        if t >= 2:
                            dve.wait_ge(s_g1, t - 1)
                        nc.vector.tensor_tensor(y1[:, t % 2, :], ps[:, 2 * (t % 2):2 * (t % 2) + 2, :].rearrange("p b n -> p (b n)"),
                                                b1, ALU.add).then_inc(s_y1b, 1)

                    def result(t):
                        dve.wait_ge(s_y2, t + 1)
                        v.link(nc.vector.tensor_tensor(y2, ps[:, 6 + t % 2, 0:D], b2, ALU.add))
                        v.link(nc.vector.tensor_tensor(z, y2, rb[:, t, :], ALU.add))
                        nc.vector.scalar_tensor_tensor(x[:, t, :], z, tg[:, 6:7], x[:, t, :], ALU.mult,
                                                       ALU.add).then_inc(s_x, 1)

                    hidden(0)
                    hidden(1)
                    for t in range(NT):
                        dve.wait_ge(s_g1, t + 1)
                        g, w = blocks(g1[:, t % 2, :]), blocks(tmp2[:, t % 2, :])
                        if t >= 2:
                            dve.wait_ge(s_q2, t - 1)
                        mx_scales(v, g, am2[:, t % 2])
                        nc.vector.tensor_tensor(w, g, mx_wide(am2[:, t % 2], 1, FF // BLK), ALU.add).then_inc(s_ra, 1)
                        if t + 2 < NT:
                            hidden(t + 2)
                        dve.wait_ge(s_rs, t + 1)
                        if t >= 2:
                            dve.wait_ge(s_q2P, t - 1)
                        mx_limit(blocks(q2[:, t % 2, :]), w, am2[:, t % 2], s_q2)
                        if t >= 1:
                            result(t - 1)
                    result(NT - 1)

        def stage7(parts):
            moe_stage("stage7", NE7, NC7, W7, rt7, 7, s_w7, 2, Arena(regB), parts, "sel7", store=True)

        def float32r_parts(tag, sel_columns):
            held_parts = ExitStack()

            def part(name, shape):
                return held_parts.enter_context(nc.sbuf_tensor(f"{name}_{tag}", shape, F32R, side="right"))

            pairs = [[part(name + p_, shape) for p_ in ("hi", "lo")]
                     for name, shape in (("h_", [P, KD, T]), ("w_", [P, RING, UW]), ("i_", [P, 2, HALF]))]
            return held_parts, pairs + [part("comb", [P, T]), part("sel", [P, sel_columns])]

        stage0()
        stage1()
        stage2()
        high.close()
        held_parts, parts = float32r_parts("3", NE3)
        with held_parts:
            stage3(parts)
        give_back()
        regC = high.enter_context(nc.sbuf_tensor("regC2", [P, WORDS_C], F32, side="right"))
        low.close()
        with (nc.sbuf_tensor("k4T", [P, 2, NBLK, S], F32R) as k4T,
              nc.sbuf_tensor("q4T", [P, 2, NBLK, S], F32R) as q4T,
              nc.sbuf_tensor("regD", [P, WORDS_B - 4 * NBLK * S], F32) as regD):
            stage4(k4T, q4T, regD)
        regB = low.enter_context(nc.sbuf_tensor("regB2", [P, WORDS_B], F32))
        stage5()
        stage6()
        high.close()
        held_parts, parts = float32r_parts("7", NC7 * P)
        with held_parts:
            stage7(parts)
        low.close()


def kernel(**inputs):
    import numpy as np
    import concourse.bacc as _bacc
    from concourse import mybir as _mybir
    from concourse.bass_utils import run_bass_kernel_spmd as _run

    f = {k: np.asarray(v) for k, v in inputs.items()}
    C2 = np.ascontiguousarray

    def pair_order(w):
        return C2(w.reshape(w.shape[0], -1, P, 2).transpose(0, 1, 3, 2)).reshape(w.shape[0], -1)

    def moe_units(gate, up, down):
        def rows(w):
            return w.reshape(-1, KD, P, P).transpose(2, 0, 1, 3).reshape(P, -1, D)
        return C2(np.concatenate([rows(gate), rows(up), down.transpose(1, 0, 2)], 2))

    def two_rows(sel):
        return np.concatenate([sel, np.zeros((32 - len(sel), sel.shape[1]), np.float32), sel], 0)

    def packed_rows(w):
        return pair_order(C2(w.T))

    arrays = {
        "x": f["x"],
        "g_xattn": f["g_xattn"], "g_ffn": f["g_ffn"],
        "ctxT": C2(f["ctx_1024"].reshape(T, C).T),
        "L0_qkT": C2(np.stack([f["L0_xattn_Wq"].T, f["L0_xattn_Wk"].T], 1)),
        "L0_bqk": C2(np.stack([f["L0_xattn_bq"], f["L0_xattn_bk"]], 1)),
        "fsT": C2(f["fside_BxS2xS2_0"].transpose(2, 0, 1).reshape(KD, P, T).transpose(1, 0, 2)),
        **{f"L0_{n}_pk": packed_rows(f[f"L0_ffn_{n}_W_packed"]) for n in ("gate", "up")},
        **{f"L0_{n}_sc": pair_order(C2(f[f"L0_ffn_{n}_scales"].T)) for n in ("gate", "up")},
        "L0_down_pk": C2(f["L0_ffn_down_W_packed"].T.reshape(8, P, D).transpose(1, 0, 2)).reshape(P, -1),
        "L0_down_sc": C2(f["L0_ffn_down_scales"].T.reshape(8, 8, D).transpose(1, 0, 2)).reshape(8, -1),
        "L1_w": moe_units(*(np.concatenate([f[f"L1_ffn_{n}"], f[f"L1_ffn_s{n}"][None]], 0) for n in ("Wg", "Wu", "Wd"))),
        "L1_router": C2(f["L1_ffn_Wr"].T.reshape(KD, P, 16).transpose(1, 0, 2)),
        "L2_W1": C2(f["L2_ffn_W1"].reshape(8, P, D).transpose(1, 0, 2)).reshape(P, -1),
        "L2_W2": C2(f["L2_ffn_W2"].reshape(2, P, 4 * D).transpose(1, 0, 2)).reshape(P, -1),
        "L2_lnw": f["L2_ffn_ln_w"], "L2_lnb": f["L2_ffn_ln_b"], "L2_b1": f["L2_ffn_b1"], "L2_b2": f["L2_ffn_b2"],
        "m_in": C2(f["L3_xattn_in_proj_w"].T),
        "m_cw": C2(np.concatenate([f["L3_xattn_conv_w"].reshape(D, 4), f["L3_xattn_conv_b"][:, None],
                                   f["L3_xattn_dt_proj_b"][:, None], f["L3_xattn_D"][:, None]], 1)
                   .reshape(KD, P, 7).transpose(1, 0, 2)),
        "m_alog": C2(f["L3_xattn_A_log"].reshape(KD, P, 16).transpose(1, 0, 2)),
        "m_xp": C2(np.concatenate([f["L3_xattn_x_proj_w"][8:]] * 3 + [f["L3_xattn_x_proj_w"][:8]], 0).T
                   .reshape(KD, P, 104).transpose(1, 0, 2)),
        "m_dtw": C2(f["L3_xattn_dt_proj_w"].T),
        "m_sel": np.tile(np.eye(32, dtype=np.float32), (3, 1)),
        "q4_wq": C2(f["L2_xattn_Wq"].reshape(KD, P, D).transpose(1, 0, 2)),
        "q4_wo": C2(f["L2_xattn_Wo"].reshape(KD, P, D).transpose(1, 0, 2)),
        "q4_wkv": C2(np.concatenate([f["L2_xattn_Wk"], f["L2_xattn_Wv"]], 1)),
        "q4_wdca": C2(f["L2_xattn_Wkv_dca"].reshape(P, 2, 16, 16).transpose(0, 2, 1, 3)).reshape(P, -1),
        "q4_bkv": np.concatenate([f["L2_xattn_bk"], f["L2_xattn_bv"]]),
        "q4_bdca": C2(f["L2_xattn_bkv_dca"].reshape(2, 16, 16).transpose(1, 0, 2)).reshape(-1),
        "q4_bq": f["L2_xattn_bq"], "q4_bo": f["L2_xattn_bo"],
        "q4_qn": np.stack([f["L2_xattn_qn_w"], f["L2_xattn_qn_b"]]),
        "q4_kn": np.stack([f["L2_xattn_kn_w"], f["L2_xattn_kn_b"]]),
        "q4_kd": np.stack([f["L2_xattn_kn_dca_w"], f["L2_xattn_kn_dca_b"]]),
        "q4_mask": np.stack([np.stack([np.ones(P), np.arange(P) < P - 16], 1),
                             np.stack([np.zeros(P), np.arange(P) >= P - 16], 1)], 2).astype(np.float32),
        "L1_bias": f["L1_ffn_bias"],
        "L3_w": moe_units(*(f[f"L3_ffn_{n}_proj"].reshape(-1, P, D).transpose(0, 2, 1) for n in ("gate", "up")),
                          f["L3_ffn_down_proj"].transpose(0, 2, 1).reshape(-1, P, D)),
        "L3_router": C2(f["L3_ffn_gate_w"].T.reshape(KD, P, 8).transpose(1, 0, 2)),
        "iota": np.arange(16, dtype=np.float32),
        "sel3": two_rows(np.eye(16, dtype=np.float32)),
        "sel7": two_rows(np.repeat(np.eye(8, dtype=np.float32), 176, 1)),
        "ident": np.eye(P, dtype=np.float32),
    }
    nc = _bacc.Bacc("TRN2", target_bir_lowering=False, num_devices=1)
    args = {k: nc.dram_tensor("in_" + k, v.shape, _mybir.dt.from_np(v.dtype), kind="ExternalInput").ap()
            for k, v in arrays.items()}
    out = nc.dram_tensor("out_x", (B, S, D), F32, kind="ExternalOutput").ap()
    build(nc, args, out)
    r = _run(nc, [{"in_" + k: v for k, v in arrays.items()}], core_ids=[0])
    return r.results[0]["out_x"]
```
